# Optimizing a Trainium2 kernel written in Bass

```python
import numpy as np
import jax
import jax.numpy as jnp

def _softmax(x, axis=-1):
    return jax.nn.softmax(x, axis=axis)

def _gelu(x):
    return jax.nn.gelu(x, approximate=True)

def _silu(x):
    return jax.nn.silu(x)

def _sigmoid(x):
    return jax.nn.sigmoid(x)

def _layernorm(x, axis=-1, eps=1e-05):
    m = jnp.mean(x, axis=axis, keepdims=True)
    v = jnp.var(x, axis=axis, keepdims=True)
    return (x - m) / jnp.sqrt(v + eps)

def _scatter_add(tgt, idx, src, axis=0):
    return tgt.at[idx].add(src)

def _segment_sum(src, seg, n):
    return jax.ops.segment_sum(src, seg, n)
kernel_name = 'mk_gnn_ffn_d1_gnn_r8_e8e657'

def setup_inputs(seed: int=0):
    np.random.seed(seed)
    _w = jnp.asarray

    def _rec_inputs():
        import jax
        import jax.numpy as jnp
        _gk = jax.random.key(seed)
        x = -0.000364 + 1 * jax.random.normal(jax.random.fold_in(_gk, 1), (1250, 768), jnp.float32)
        src = jax.random.randint(jax.random.fold_in(_gk, 2), (40000,), 0, 1250, jnp.int32)
        dst = jnp.minimum((1250 * jax.random.uniform(jax.random.fold_in(_gk, 3), (40000,)) ** 2.0).astype(jnp.int32), 9999)
        _o = jnp.argsort(dst, stable=True)
        src = src[_o]
        dst = dst[_o]
        return (x, src, dst)
    x, src, dst = _rec_inputs()

    def _L0_gnn_setup():
        import jax, jax.numpy as jnp
        import numpy as np
        N_NODES = 2500
        N_EDGES = 20000
        IN_DIM = 768
        HID = 256
        HEADS = 4
        OUT_DIM = 768
        LN_EPS = 1e-05

        def _add_self_loops(edge_index, n):
            loop = jnp.arange(n, dtype=edge_index.dtype)
            return jnp.concatenate([edge_index, jnp.stack([loop, loop])], axis=1)

        def gat_conv(x, edge_index, W, a_src, a_dst, bias, heads, out_ch, concat):
            n = x.shape[0]
            ei = _add_self_loops(edge_index, n)
            src, dst = (ei[0], ei[1])
            xl = (x @ W).reshape(n, heads, out_ch)
            alpha_src = jnp.einsum('nhc,hc->nh', xl, a_src)
            alpha_dst = jnp.einsum('nhc,hc->nh', xl, a_dst)
            e = jax.nn.leaky_relu(alpha_src[src] + alpha_dst[dst], 0.2)
            m = jax.ops.segment_max(e, dst, num_segments=n)
            e = jnp.exp(e - m[dst])
            s = jax.ops.segment_sum(e, dst, num_segments=n)
            alpha = e / (s[dst] + 1e-16)
            msg = xl[src] * alpha[:, :, None]
            out = jax.ops.segment_sum(msg, dst, num_segments=n)
            out = out.reshape(n, heads * out_ch) if concat else out.mean(axis=1)
            return out + bias

        def layer_norm(x, g, b):
            mu = jnp.mean(x, axis=-1, keepdims=True)
            var = jnp.var(x, axis=-1, keepdims=True)
            return (x - mu) * jax.lax.rsqrt(var + LN_EPS) * g + b
        key = jax.random.key(seed)
        ks = jax.random.split(key, 16)
        s = 0.02
        HC = HID * HEADS
        return {'x': jax.random.normal(ks[0], (N_NODES, IN_DIM), jnp.float32), 'edge_index': jax.random.randint(ks[1], (2, N_EDGES), 0, N_NODES, jnp.int64 if jax.config.jax_enable_x64 else jnp.int32), 'W1': jax.random.normal(ks[2], (IN_DIM, HC), jnp.float32) * s, 'a_src1': jax.random.normal(ks[3], (HEADS, HID), jnp.float32) * s, 'a_dst1': jax.random.normal(ks[4], (HEADS, HID), jnp.float32) * s, 'b1': jnp.zeros((HC,), jnp.float32), 'g1': jnp.ones((HC,), jnp.float32), 'be1': jnp.zeros((HC,), jnp.float32), 'Wr1': jax.random.normal(ks[5], (IN_DIM, HC), jnp.float32) * s, 'br1': jnp.zeros((HC,), jnp.float32), 'W2': jax.random.normal(ks[6], (HC, OUT_DIM), jnp.float32) * s, 'a_src2': jax.random.normal(ks[7], (1, OUT_DIM), jnp.float32) * s, 'a_dst2': jax.random.normal(ks[8], (1, OUT_DIM), jnp.float32) * s, 'b2': jnp.zeros((OUT_DIM,), jnp.float32), 'g2': jnp.ones((OUT_DIM,), jnp.float32), 'be2': jnp.zeros((OUT_DIM,), jnp.float32), 'Wr2': jax.random.normal(ks[9], (HC, OUT_DIM), jnp.float32) * s, 'br2': jnp.zeros((OUT_DIM,), jnp.float32)}
    _L0_gnn_all = _L0_gnn_setup()
    _L0_gnn_in = {k: v for k, v in _L0_gnn_all.items() if k in ('W1', 'a_src1', 'a_dst1', 'b1', 'g1', 'be1', 'Wr1', 'br1', 'W2', 'a_src2', 'a_dst2', 'b2', 'g2', 'be2', 'Wr2', 'br2')}
    del _L0_gnn_all

    def _L0_ffn_setup():
        import jax, jax.numpy as jnp
        import numpy as np
        import math
        B, T, C = (8, 256, 768)
        E = 3
        HD = C // E
        TOPK = 2
        NGLOB = 4

        def _masked_softmax(att, mask):
            att = jnp.where(mask, -jnp.inf, att)
            return jax.nn.softmax(att, axis=-1)
        key = jax.random.key(seed)
        ks = jax.random.split(key, 16)
        s = 0.02
        return {'x': jax.random.normal(ks[0], (B, T, C), jnp.float32), 'Wqk': jax.random.normal(ks[1], (C, 2 * C), jnp.float32) * s, 'bqk': jnp.zeros((2 * C,), jnp.float32), 'Wv': jax.random.normal(ks[2], (E, C, HD), jnp.float32) * s, 'bv': jnp.zeros((E, HD), jnp.float32), 'conv_w': jax.random.normal(ks[3], (HD, 1, 3), jnp.float32) * s, 'conv_b': jnp.zeros((HD,), jnp.float32), 'glob': jax.random.normal(ks[4], (NGLOB, HD), jnp.float32) * 0.02, 'pos_bias': jnp.zeros((64, 64), jnp.float32), 'Wg1': jax.random.normal(ks[5], (C, 32), jnp.float32) * s, 'bg1': jnp.zeros((32,), jnp.float32), 'Wg2': jax.random.normal(ks[6], (32, E), jnp.float32) * s, 'bg2': jnp.zeros((E,), jnp.float32), 'Wp': jax.random.normal(ks[7], (C, C), jnp.float32) * s, 'bp': jnp.zeros((C,), jnp.float32)}
    _L0_ffn_all = _L0_ffn_setup()
    _L0_ffn_in = {k: v for k, v in _L0_ffn_all.items() if k in ('Wqk', 'bqk', 'Wv', 'bv', 'conv_w', 'conv_b', 'glob', 'pos_bias', 'Wg1', 'bg1', 'Wg2', 'bg2', 'Wp', 'bp')}
    del _L0_ffn_all
    return {'x': x, 'src': src, 'dst': dst, 'L0_gnn_W1': _L0_gnn_in['W1'], 'L0_gnn_a_src1': _L0_gnn_in['a_src1'], 'L0_gnn_a_dst1': _L0_gnn_in['a_dst1'], 'L0_gnn_b1': _L0_gnn_in['b1'], 'L0_gnn_g1': _L0_gnn_in['g1'], 'L0_gnn_be1': _L0_gnn_in['be1'], 'L0_gnn_Wr1': _L0_gnn_in['Wr1'], 'L0_gnn_br1': _L0_gnn_in['br1'], 'L0_gnn_W2': _L0_gnn_in['W2'], 'L0_gnn_a_src2': _L0_gnn_in['a_src2'], 'L0_gnn_a_dst2': _L0_gnn_in['a_dst2'], 'L0_gnn_b2': _L0_gnn_in['b2'], 'L0_gnn_g2': _L0_gnn_in['g2'], 'L0_gnn_be2': _L0_gnn_in['be2'], 'L0_gnn_Wr2': _L0_gnn_in['Wr2'], 'L0_gnn_br2': _L0_gnn_in['br2'], 'L0_ffn_Wqk': _L0_ffn_in['Wqk'], 'L0_ffn_bqk': _L0_ffn_in['bqk'], 'L0_ffn_Wv': _L0_ffn_in['Wv'], 'L0_ffn_bv': _L0_ffn_in['bv'], 'L0_ffn_conv_w': _L0_ffn_in['conv_w'], 'L0_ffn_conv_b': _L0_ffn_in['conv_b'], 'L0_ffn_glob': _L0_ffn_in['glob'], 'L0_ffn_pos_bias': _L0_ffn_in['pos_bias'], 'L0_ffn_Wg1': _L0_ffn_in['Wg1'], 'L0_ffn_bg1': _L0_ffn_in['bg1'], 'L0_ffn_Wg2': _L0_ffn_in['Wg2'], 'L0_ffn_bg2': _L0_ffn_in['bg2'], 'L0_ffn_Wp': _L0_ffn_in['Wp'], 'L0_ffn_bp': _L0_ffn_in['bp']}

def reference(x, src, dst, L0_gnn_W1, L0_gnn_a_src1, L0_gnn_a_dst1, L0_gnn_b1, L0_gnn_g1, L0_gnn_be1, L0_gnn_Wr1, L0_gnn_br1, L0_gnn_W2, L0_gnn_a_src2, L0_gnn_a_dst2, L0_gnn_b2, L0_gnn_g2, L0_gnn_be2, L0_gnn_Wr2, L0_gnn_br2, L0_ffn_Wqk, L0_ffn_bqk, L0_ffn_Wv, L0_ffn_bv, L0_ffn_conv_w, L0_ffn_conv_b, L0_ffn_glob, L0_ffn_pos_bias, L0_ffn_Wg1, L0_ffn_bg1, L0_ffn_Wg2, L0_ffn_bg2, L0_ffn_Wp, L0_ffn_bp):
    import jax
    import jax.numpy as jnp

    def _L0_gnn_ref(x, edge_index, W1, a_src1, a_dst1, b1, g1, be1, Wr1, br1, W2, a_src2, a_dst2, b2, g2, be2, Wr2, br2):
        import jax, jax.numpy as jnp
        import numpy as np
        N_NODES = 2500
        N_EDGES = 20000
        IN_DIM = 768
        HID = 256
        HEADS = 4
        OUT_DIM = 768
        LN_EPS = 1e-05

        def _add_self_loops(edge_index, n):
            loop = jnp.arange(n, dtype=edge_index.dtype)
            return jnp.concatenate([edge_index, jnp.stack([loop, loop])], axis=1)

        def gat_conv(x, edge_index, W, a_src, a_dst, bias, heads, out_ch, concat):
            n = x.shape[0]
            ei = _add_self_loops(edge_index, n)
            src, dst = (ei[0], ei[1])
            xl = (x @ W).reshape(n, heads, out_ch)
            alpha_src = jnp.einsum('nhc,hc->nh', xl, a_src)
            alpha_dst = jnp.einsum('nhc,hc->nh', xl, a_dst)
            e = jax.nn.leaky_relu(alpha_src[src] + alpha_dst[dst], 0.2)
            m = jax.ops.segment_max(e, dst, num_segments=n)
            e = jnp.exp(e - m[dst])
            s = jax.ops.segment_sum(e, dst, num_segments=n)
            alpha = e / (s[dst] + 1e-16)
            msg = xl[src] * alpha[:, :, None]
            out = jax.ops.segment_sum(msg, dst, num_segments=n)
            out = out.reshape(n, heads * out_ch) if concat else out.mean(axis=1)
            return out + bias

        def layer_norm(x, g, b):
            mu = jnp.mean(x, axis=-1, keepdims=True)
            var = jnp.var(x, axis=-1, keepdims=True)
            return (x - mu) * jax.lax.rsqrt(var + LN_EPS) * g + b
        h0 = x
        h = gat_conv(x, edge_index, W1, a_src1, a_dst1, b1, HEADS, HID, True)
        h = layer_norm(h, g1, be1)
        h = jax.nn.relu(h)
        h = h + (h0 @ Wr1 + br1)
        h1 = h
        h = gat_conv(h, edge_index, W2, a_src2, a_dst2, b2, 1, OUT_DIM, False)
        h = layer_norm(h, g2, be2)
        h = h + (h1 @ Wr2 + br2)
        return h

    def _L0_ffn_ref(x, Wqk, bqk, Wv, bv, conv_w, conv_b, glob, pos_bias, Wg1, bg1, Wg2, bg2, Wp, bp):
        import jax, jax.numpy as jnp
        import numpy as np
        import math
        B, T, C = (8, 256, 768)
        E = 3
        HD = C // E
        TOPK = 2
        NGLOB = 4

        def _masked_softmax(att, mask):
            att = jnp.where(mask, -jnp.inf, att)
            return jax.nn.softmax(att, axis=-1)
        Bx, Tx, Cx = x.shape
        scale = 1.0 / math.sqrt(HD)
        gate = jax.nn.softmax(jax.nn.relu(x @ Wg1 + bg1) @ Wg2 + bg2, axis=-1)
        top_w, top_i = jax.lax.top_k(gate, TOPK)
        top_w = jax.nn.softmax(top_w, axis=-1)
        qk = x @ Wqk + bqk
        q, k = (qk[..., :Cx], qk[..., Cx:])
        q = q.reshape(Bx, Tx, E, HD)
        k = k.reshape(Bx, Tx, E, HD)
        rows = jnp.arange(Tx)[:, None]
        ys = []
        for e in range(E):
            qe = q[:, :, e]
            ke = k[:, :, e]
            ve = x @ Wv[e] + bv[e]
            if e == 0:
                qc = jnp.transpose(qe, (0, 2, 1))
                qc = jax.lax.conv_general_dilated(qc, conv_w, window_strides=(1,), padding=((1, 1),), feature_group_count=HD, dimension_numbers=('NCH', 'OIH', 'NCH'))
                qe = jnp.transpose(qc + conv_b[None, :, None], (0, 2, 1))
            elif e == 1:
                gb = jnp.broadcast_to(glob[None], (Bx, NGLOB, HD))
                ke = jnp.concatenate([ke, gb], axis=1)
                ve = jnp.concatenate([ve, gb], axis=1)
            att = jnp.einsum('btd,bsd->bts', qe, ke) * scale
            if e == 2 and Tx <= 64:
                att = att + pos_bias[:Tx, :Tx][None]
            S = att.shape[-1]
            mask = jnp.arange(S)[None, :] > rows
            att = _masked_softmax(att, mask[None])
            ys.append(jnp.einsum('bts,bsd->btd', att, ve))
        ys = jnp.stack(ys, axis=2)
        w_e = jnp.sum(jax.nn.one_hot(top_i, E, dtype=x.dtype) * top_w[..., None], axis=-2)
        combined = (ys * w_e[..., None]).reshape(Bx, Tx, Cx)
        return combined @ Wp + bp
    edge_index = jnp.stack([src, dst])
    x = x + _L0_gnn_ref(_layernorm(x, axis=-1), edge_index, L0_gnn_W1, L0_gnn_a_src1, L0_gnn_a_dst1, L0_gnn_b1, L0_gnn_g1, L0_gnn_be1, L0_gnn_Wr1, L0_gnn_br1, L0_gnn_W2, L0_gnn_a_src2, L0_gnn_a_dst2, L0_gnn_b2, L0_gnn_g2, L0_gnn_be2, L0_gnn_Wr2, L0_gnn_br2)
    x = x + _L0_ffn_ref(_layernorm(x, axis=-1)[None], L0_ffn_Wqk, L0_ffn_bqk, L0_ffn_Wv, L0_ffn_bv, L0_ffn_conv_w, L0_ffn_conv_b, L0_ffn_glob, L0_ffn_pos_bias, L0_ffn_Wg1, L0_ffn_bg1, L0_ffn_Wg2, L0_ffn_bg2, L0_ffn_Wp, L0_ffn_bp)[0]
    return x

_drawn_inputs = setup_inputs


def setup_inputs(seed=0):
    import zlib

    import numpy as np

    out = dict(_drawn_inputs(seed))
    spreads = {'L0_gnn_b1': (0.0, 0.1),
     'L0_gnn_g1': (1.0, 0.2),
     'L0_gnn_be1': (0.0, 0.1),
     'L0_gnn_br1': (0.0, 0.1),
     'L0_gnn_b2': (0.0, 0.1),
     'L0_gnn_g2': (1.0, 0.2),
     'L0_gnn_be2': (0.0, 0.1),
     'L0_gnn_br2': (0.0, 0.1),
     'L0_ffn_bqk': (0.0, 2.0),
     'L0_ffn_bv': (0.0, 0.556),
     'L0_ffn_conv_b': (0.0, 2.0),
     'L0_ffn_pos_bias': (0.0, 0.1),
     'L0_ffn_bg1': (0.0, 2.0),
     'L0_ffn_bg2': (0.0, 2.0),
     'L0_ffn_bp': (0.0, 0.1)}
    factors = {'L0_gnn_a_dst1': 50.067,
     'L0_gnn_a_dst2': 56.013,
     'L0_ffn_Wqk': 8.0,
     'L0_ffn_conv_w': 200.0,
     'L0_ffn_Wg1': 6.451,
     'L0_ffn_Wg2': 8.0}
    for name, (base, spread) in spreads.items():
        noise = np.random.default_rng([zlib.crc32(name.encode()), seed]).standard_normal(out[name].shape)
        drawn = base * np.exp(spread * noise) if base else spread * noise
        out[name] = jnp.asarray(drawn.astype(out[name].dtype))
    for name, factor in factors.items():
        out[name] = (out[name] * factor).astype(out[name].dtype)
    return out
```

```python
import concourse.bass as bass
from concourse import mybir
from contextlib import ExitStack

FP32 = mybir.dt.float32
FP16 = mybir.dt.float16
BF16 = mybir.dt.bfloat16
I32 = mybir.dt.int32
U16 = mybir.dt.uint16
ALU = mybir.AluOpType
ACT = mybir.ActivationFunctionType
AX = mybir.AxisListType

NODES, C_IN = 1250, 768
P = 128
NB = 10
NPAD = NB * P
KT = C_IN // P
HEADS, HID = 4, 256
HC = HEADS * HID
HKT = HC // P
EDGES, EDGE_P = 40000, 125
CHUNKS = EDGES // EDGE_P
GROUP = 4
GROUPS = CHUNKS // GROUP
EXPERTS, HD = 3, 256
GATE = 32
LN_EPS = 1e-5
SLOPE = 0.2
ABSENT = -1.0e30
BANK = 512


class Chain:

    def __init__(self, eng, sem, links=0, turn=0):
        self.eng, self.sem, self.links, self.turn, self.n = eng, sem, links, turn, 0

    def __call__(self, instruction):
        instruction.then_inc(self.sem, 1)
        self.n += 1
        self.eng.wait_ge(self.sem, self.turn * self.links + self.n)

    def end(self):
        assert self.n == self.links, self.n


def scope(nc, ctx):
    sems = []

    def clear():
        if sems:
            with nc.Block() as block:
                @block.gpsimd
                def _(pool):
                    nc.clear_and_free_semaphores(sems)

    ctx.callback(clear)

    def sb(name, shape, dt):
        return ctx.enter_context(nc.sbuf_tensor(name, shape, dt))

    def ps(name, shape, dt=FP32):
        return ctx.enter_context(nc.psum_tensor(name, shape, dt))

    def sem(name):
        sems.append(nc.alloc_semaphore(name))
        return sems[-1]

    return sb, ps, sem


def blocks_by_two(eng):
    with eng.Fori(0, NB // 2) as turn:
        for u in (0, 1):
            yield turn * 2 + u, u, turn


def x_loads(b, u):
    return (b - u) * 8 + 16


def one_ahead(eng, early, late):
    early(0, 0)
    with eng.Fori(0, NB // 2 - 1) as turn:
        early(turn * 2 + 1, 1)
        late(turn * 2, 0)
        early(turn * 2 + 2, 0)
        late(turn * 2 + 1, 1)
    early(NB - 1, 1)
    late(NB - 2, 0)
    late(NB - 1, 1)


def count_edges(nc, src, dst, counts):
    with ExitStack() as ctx:
        sb, ps, sem = scope(nc, ctx)
        src_i, dst_i = sb("src_i", [EDGE_P, CHUNKS], I32), sb("dst_i", [EDGE_P, CHUNKS], I32)
        src_f, dst_f = sb("src_f", [EDGE_P, CHUNKS], FP32), sb("dst_f", [EDGE_P, CHUNKS], FP32)
        block_i, block_f = sb("block_i", [EDGE_P, CHUNKS], I32), sb("block_f", [EDGE_P, CHUNKS], FP32)
        upward, downward = sb("upward", [EDGE_P, CHUNKS], FP32), sb("downward", [EDGE_P, CHUNKS], FP32)
        member, masked = sb("member", [EDGE_P, CHUNKS], FP32), sb("masked", [EDGE_P, CHUNKS], FP32)
        node_ids = sb("node_ids", [P, NPAD], FP16)
        span, span_all = sb("span", [P, 2 * NB], FP32), sb("span_all", [P, 2 * NB], FP32)
        row = sb("row", [1, 4, NB], FP32)
        table = sb("table", [1, 3, NB], I32)
        shifted = sb("shifted", [P, NPAD + (NB - 1) * P], BF16)
        AT = (NB - 1) * P
        src_hot = sb("src_hot", [P, 2 * GROUP, NPAD], BF16)
        dst_hot = sb("dst_hot", [P, 2 * GROUP, P], BF16)
        sums = [ps(f"sums{u}", [P, 3 * BANK]) for u in (0, 1)]
        edges_in, consts, ids_ready = sem("edges_in"), sem("consts"), sem("ids_ready")
        span_ready, span_reduced, table_ready = sem("span_ready"), sem("span_reduced"), sem("table_ready")
        hot_ready, slots_free = sem("hot_ready"), sem("slots_free")
        sums_free, order = sem("sums_free"), sem("order0")
        block = ctx.enter_context(nc.Block())

        def bounds(eng, b):
            return [eng.value_load(table[0:1, i, bass.ds(b, 1)], min_val=0, max_val=m)
                    for i, m in enumerate((GROUPS - 1, GROUPS, GROUPS * (NB - 1)))]

        def first_chunk(eng, first, i):
            return nc.s_assert_within(
                eng.snap((first + i) * GROUP), 0, CHUNKS - GROUP,
                skip_runtime_bounds_check_because="the table's ends lie within the groups")

        @block.sync
        def _(sp):
            sp.dma_start(src_i[:, :], src).then_inc(edges_in, 16)
            sp.dma_start(dst_i[:, :], dst).then_inc(edges_in, 16)

        @block.gpsimd
        def _(pool):
            pool.iota(upward[:, :], pattern=[[1, GROUPS], [0, GROUP]], base=1, channel_multiplier=0,
                      allow_small_or_imprecise_dtypes=True).then_inc(consts, 1)
            pool.iota(downward[:, :], pattern=[[-1, GROUPS], [0, GROUP]], base=GROUPS,
                      channel_multiplier=0, allow_small_or_imprecise_dtypes=True).then_inc(consts, 1)
            pool.iota(node_ids[:, :], pattern=[[1, NPAD]], base=0, channel_multiplier=0,
                      allow_small_or_imprecise_dtypes=True).then_inc(ids_ready, 1)
            pool.memset(shifted[:, :], 0.0).then_inc(ids_ready, 1)
            pool.wait_ge(ids_ready, 2)
            pool.affine_select(out=shifted[:, AT:AT + P], in_=shifted[:, AT:AT + P],
                               compare_op=ALU.not_equal, fill=1.0, base=0, pattern=[[-1, P]],
                               channel_multiplier=1).then_inc(ids_ready, 1)
            pool.wait_ge(span_ready, 1)
            pool.partition_all_reduce(span_all[0:EDGE_P, :], span[0:EDGE_P, :], EDGE_P,
                                      bass.bass_isa.ReduceOp.max).then_inc(span_reduced, 1)

        @block.vector
        def _(dve):
            link = Chain(dve, order)
            dve.wait_ge(edges_in, 32)
            link(dve.tensor_copy(src_f[:, :], src_i[:, :]))
            link(dve.tensor_copy(dst_f[:, :], dst_i[:, :]))
            link(dve.tensor_single_scalar(block_i[:, :], dst_i[:, :], 7, ALU.arith_shift_right))
            link(dve.tensor_copy(block_f[:, :], block_i[:, :]))
            dve.wait_ge(consts, 2)
            for b in range(NB):
                link(dve.tensor_scalar(member[:, :], block_f[:, :], float(b), None, ALU.is_equal))
                for i, number in enumerate((upward, downward)):
                    link(dve.tensor_tensor_reduce(
                        out=masked[:, :], in0=member[:, :], in1=number[:, :], scale=1.0, scalar=0.0,
                        op0=ALU.mult, op1=ALU.max, accum_out=span[0:EDGE_P, i * NB + b:i * NB + b + 1]))
            dve.sem_inc(span_ready, 1)
            dve.wait_ge(span_reduced, 1)
            end, start, groups, total = (row[0:1, i, :] for i in range(4))
            link(dve.tensor_scalar(end, span_all[0:1, 0:NB], 1.0, None, ALU.max))
            link(dve.tensor_scalar(start, span_all[0:1, NB:2 * NB], -1.0, float(GROUPS), ALU.mult, ALU.add))
            link(dve.scalar_tensor_tensor(out=start, in0=end, scalar=-1.0, in1=start, op0=ALU.add, op1=ALU.min))
            link(dve.tensor_tensor(groups, end, start, ALU.subtract))
            link(dve.tensor_copy(total, groups))
            for b in range(1, NB):
                link(dve.tensor_tensor(total[:, b:b + 1], total[:, b:b + 1], total[:, b - 1:b], ALU.add))
            link(dve.tensor_tensor(total, total, groups, ALU.subtract))
            dve.tensor_copy(table[0:1, 0, :], start)
            dve.tensor_copy(table[0:1, 1, :], groups)
            dve.tensor_copy(table[0:1, 2, :], total).then_inc(table_ready, 1)
            dve.wait_ge(table_ready, 1)
            dve.wait_ge(ids_ready, 1)
            with dve.Fori(0, NB) as b:
                first, groups, before = bounds(dve, b)
                with dve.Fori(0, groups) as i:
                    turn = before + i
                    slot = dve.snap((turn % 2) * GROUP)
                    chunk = first_chunk(dve, first, i)
                    dve.wait_ge(slots_free, turn + 1)
                    for j in range(GROUP):
                        dve.tensor_scalar(
                            dst_hot[0:EDGE_P, bass.ds(slot + j, 1), :], node_ids[0:EDGE_P, bass.ds(b * P, P)],
                            dst_f[:, bass.ds(chunk + j, 1)], None, ALU.is_equal)
                        last = dve.tensor_scalar(
                            src_hot[0:EDGE_P, bass.ds(slot + j, 1), :], node_ids[0:EDGE_P, :],
                            src_f[:, bass.ds(chunk + j, 1)], None, ALU.is_equal)
                    last.then_inc(hot_ready, 1)

        @block.tensor
        def _(pe):
            pe.sem_inc(slots_free, 2)
            pe.wait_ge(ids_ready, 3)
            pe.wait_ge(table_ready, 1)
            for b, u, _ in blocks_by_two(pe):
                first, groups, before = bounds(pe, b)
                pe.wait_ge(sums_free, b + 1)
                for n in range(0, NPAD, BANK):
                    w = min(BANK, NPAD - n)
                    pe.matmul(sums[u][:, n:n + w], shifted[:, AT:AT + P],
                              shifted[:, bass.ds(AT - b * P + n, w)], start=True, stop=False,
                              skip_group_check=True)
                with pe.Fori(0, groups) as i:
                    turn = before + i
                    slot = pe.snap((turn % 2) * GROUP)
                    pe.wait_ge(hot_ready, turn + 1)
                    for j in range(GROUP):
                        for n in range(0, NPAD, BANK):
                            w = min(BANK, NPAD - n)
                            last = pe.matmul(sums[u][:, n:n + w], dst_hot[0:EDGE_P, bass.ds(slot + j, 1), :],
                                             src_hot[0:EDGE_P, bass.ds(slot + j, 1), n:n + w],
                                             start=False, stop=True, skip_group_check=True)
                    last.then_inc(slots_free, 1)

        @block.scalar
        def _(act):
            act.sem_inc(sums_free, 2)
            act.wait_ge(table_ready, 1)
            for b, u, _ in blocks_by_two(act):
                first, groups, before = bounds(act, b)
                act.wait_ge(slots_free, before + groups + 2)
                act.activation(counts[:, bass.ds(b, 1), :], sums[u][:, 0:NPAD], ACT.Copy).then_inc(sums_free, 1)


def split_wait(eng, passed):
    eng.sem_inc(passed, 1)


def normalize(nc, dve, pool_sems, link, value, stats, out, width):
    stats_ready, root_ready, passed, count = pool_sems
    parts = width // 2 if width // 2 <= BANK else BANK
    n = width // parts
    for i in range(n):
        link(dve.bn_stats(stats[:, 8 + 6 * i:14 + 6 * i], value[:, i * parts:(i + 1) * parts]))
    split_wait(dve, passed)
    dve.bn_aggr(stats[:, 0:2], stats[:, 8:8 + 6 * n]).then_inc(stats_ready, 1)
    dve.wait_ge(root_ready, count)
    return dve.tensor_scalar(out, value, stats[:, 0:1], stats[:, 3:4], ALU.subtract, ALU.mult)


def root(nc, pool, stats, eps_half, chain):
    chain(pool.tensor_tensor(stats[:, 2:3], stats[:, 1:2], eps_half[:, 0:1], ALU.add))
    return pool.tensor_tensor(stats[:, 3:4], stats[:, 2:3], eps_half[:, 1:2], ALU.pow)


def project(nc, kt, heads, width, normalized, x, residual, w, w_skip, b_skip, a_src, a_dst, ident, ones, eps_half,
            xl, src_row, dst_col, skip):
    F, C = heads * width, kt * P
    PARTS = [(n, min(BANK, F - n)) for n in range(0, F, BANK)]
    with ExitStack() as ctx:
        sb, ps, sem = scope(nc, ctx)
        L = f"_p{heads}"
        weights = sb("weights" + L, [P, kt, F], FP32)
        skips = sb("skips" + L, [P, kt, F], FP32)
        skip_bias = sb("skip_bias" + L, [P, F], FP32)
        att = sb("att" + L, [P, 2, F], FP32)
        xt = [sb(f"xt{L}{u}", [P, C], FP32) for u in (0, 1)]
        xn = [sb(f"xn{L}{u}", [P, C], FP32) for u in (0, 1)] if normalized else xt
        xT = [sb(f"xT{L}{u}", [P, kt, P], FP32) for u in (0, 1)]
        res = [sb(f"res{L}{u}", [P, F], FP32) for u in (0, 1)] if residual is not None else None
        stats = [sb(f"stats{L}{u}", [P, 24], FP32) for u in (0, 1)]
        terms = [sb(f"terms{L}{u}", [P, 2 * heads], FP32) for u in (0, 1)]
        diag = [sb(f"diag{L}{u}", [P, heads, P], FP32) for u in (0, 1)]
        unused = sb("unused" + L, [P, 2, heads, width], FP32)
        out = [sb(f"out{L}{u}", [P, F], FP32) for u in (0, 1)]
        ps_t = ps("ps_t" + L, [P, 2 * BANK])
        ps_w = ps("ps_w" + L, [P, 2 * BANK])
        ps_s = ps("ps_s" + L, [P, 2 * BANK])
        ps_a = ps("ps_a" + L, [P, BANK])
        (w_in, skip_w_in, rows_in, x_free, stats_ready, root_ready, pool_order, xn_ready, turned, xT_moved,
         product, product_free, skipped, skip_free, terms_done, diag_ready, row_ready, row_free, biased,
         out_ready, order, passed) = (
            sem(n + L) for n in (
                "w_in", "skip_w_in", "rows_in", "x_free", "stats_ready", "root_ready", "pool_order",
                "xn_ready", "turned", "xT_moved", "product", "product_free", "skipped", "skip_free",
                "terms_done", "diag_ready", "row_ready", "row_free", "biased", "out_ready", "order", "passed"))
        x_in, res_in, skip_out = ([sem(f"{n}{L}{u}") for u in (0, 1)] for n in ("x_in", "res_in", "skip_out"))
        block = ctx.enter_context(nc.Block())

        def rows_of(dram, b):
            return dram[bass.ds(b, 1), :, :].rearrange("b p c -> (b p) c")

        @block.sync
        def _(sp):
            for b, u, _ in blocks_by_two(sp):
                sp.wait_ge(x_free, b + 1)
                sp.dma_start(xt[u][:, :], rows_of(x, b)).then_inc(x_in[u], 16)
                if res:
                    sp.wait_ge(out_ready, b + 1)
                    sp.dma_start(res[u][:, :], rows_of(residual, b)).then_inc(res_in[u], 16)

        @block.gpsimd
        def _(pool):
            pool.dma_start(skip_bias[:, :], b_skip.partition_broadcast(P)).then_inc(rows_in, 16)
            for i, a in enumerate((a_src, a_dst)):
                pool.dma_start(att[:, i, :], a.rearrange("h c -> (h c)").partition_broadcast(P)).then_inc(rows_in, 16)
            if normalized:
                for b, u, _ in blocks_by_two(pool):
                    chain = Chain(pool, pool_order, 1, b)
                    pool.wait_ge(stats_ready, b + 1)
                    root(nc, pool, stats[u], eps_half, chain).then_inc(root_ready, 1)
                    chain.end()

        @block.vector
        def _(dve):
            dve.sem_inc(out_ready, 2)
            if normalized:
                dve.sem_inc(x_free, 2)
            dve.wait_ge(rows_in, 48)

            def norm(b, u):
                if not normalized:
                    return
                link = Chain(dve, order, 2, b)
                dve.wait_ge(x_in[u], x_loads(b, u))
                dve.wait_ge(turned, b + 1)
                normalize(nc, dve, (stats_ready, root_ready, passed, b + 1), link, xt[u][:, :], stats[u],
                          xn[u][:, :], C).then_inc(xn_ready, 1)
                link.end()
                dve.wait_ge(xn_ready, b + 1)
                dve.sem_inc(x_free, 1)

            def finish(b, u):
                dve.wait_ge(product, b + 1)
                for h in range(heads):
                    for i in (0, 1):
                        last = dve.tensor_tensor_reduce(
                            out=unused[:, i, h, :], in0=ps_w[:, h * width:(h + 1) * width],
                            in1=att[:, i, h * width:(h + 1) * width], scale=1.0, scalar=0.0, op0=ALU.mult,
                            op1=ALU.add, accum_out=terms[u][:, i * heads + h:i * heads + h + 1])
                last.then_inc(terms_done, 1)
                dve.wait_ge(terms_done, b + 1)
                dve.tensor_copy(dst_col[:, bass.ds(b, 1), :], terms[u][:, heads:2 * heads].unsqueeze(1))
                for h in range(heads):
                    last = dve.tensor_scalar(diag[u][:, h, :], ident[:, :], terms[u][:, h:h + 1], None, ALU.mult)
                last.then_inc(diag_ready, 1)
                dve.wait_ge(skip_out[u], x_loads(b, u))
                dve.wait_ge(skipped, b + 1)
                last = dve.tensor_tensor(out[u][:, :], ps_s[:, 0:F], skip_bias[:, :], ALU.add)
                last.then_inc(skip_free, 1)
                if res:
                    dve.wait_ge(skip_free, b + 2)
                    dve.wait_ge(res_in[u], x_loads(b, u))
                    last = dve.tensor_tensor(out[u][:, :], out[u][:, :], res[u][:, :], ALU.add)
                    last.then_inc(out_ready, 1)

            one_ahead(dve, norm, finish)

        @block.scalar
        def _(act):
            for k in range(kt):
                act.dma_start(weights[:, k, :], w[k * P:(k + 1) * P, :]).then_inc(w_in, 16)
            for k in range(kt):
                act.dma_start(skips[:, k, :], w_skip[k * P:(k + 1) * P, :]).then_inc(skip_w_in, 16)
            act.sem_inc(xT_moved, 1)
            act.sem_inc(product_free, 1)
            act.sem_inc(skip_free, 1)
            act.sem_inc(row_free, 1)
            for u in (0, 1):
                act.sem_inc(skip_out[u], 16)

            def move_xT(b, u):
                act.wait_ge(turned, b + 3)
                act.activation(xT[u][:, :, :], ps_t[:, 0:C].rearrange("p (k c) -> p k c", k=kt), ACT.Copy).then_inc(xT_moved, 1)

            def keep(b, u):
                act.wait_ge(terms_done, b + 1)
                act.activation(xl[:, bass.ds(b, 1), :], ps_w[:, 0:F].unsqueeze(1), ACT.Copy).then_inc(product_free, 1)
                act.wait_ge(row_ready, b + 1)
                act.activation(src_row[:, :, bass.ds(b * P, P)], ps_a[:, 0:heads * P].rearrange("p (h c) -> p h c", h=heads),
                               ACT.Copy).then_inc(row_free, 1)
                if res:
                    act.wait_ge(out_ready, b + 3)
                else:
                    act.wait_ge(skip_free, b + 2)
                act.dma_start(rows_of(skip, b), out[u][:, :]).then_inc(skip_out[u], 16)

            one_ahead(act, move_xT, keep)
            for u in (0, 1):
                act.wait_ge(skip_out[u], 16 * (NB // 2 + 1))

        @block.tensor
        def _(pe):
            pe.sem_inc(turned, 2)

            def transposes(b, u):
                if normalized:
                    pe.wait_ge(xn_ready, b + 1)
                else:
                    pe.wait_ge(x_in[u], x_loads(b, u))
                pe.wait_ge(xT_moved, b + 1)
                for k in range(kt):
                    last = pe.transpose(ps_t[:, k * P:(k + 1) * P], xn[u][:, k * P:(k + 1) * P], ident[:, :])
                last.then_inc(turned, 1)
                if not normalized:
                    pe.wait_ge(turned, b + 3)
                    pe.sem_inc(x_free, 1)

            def products(b, u):
                pe.wait_ge(xT_moved, b + 2)
                for to, of, free, done in ((ps_w, weights, product_free, product), (ps_s, skips, skip_free, skipped)):
                    pe.wait_ge(free, b + 1)
                    for n, wide in PARTS:
                        for k in range(kt):
                            last = pe.matmul(to[:, n:n + wide], xT[u][:, k, :], of[:, k, n:n + wide],
                                             start=(k == 0), stop=(k == kt - 1))
                    last.then_inc(done, 1)
                pe.wait_ge(diag_ready, b + 1)
                pe.wait_ge(row_free, b + 1)
                pe.matmul(ps_a[:, 0:heads * P], ones[:, :], diag[u][:, :, :].rearrange("p h c -> p (h c)"),
                          start=True, stop=True).then_inc(row_ready, 1)

            if not normalized:
                pe.sem_inc(x_free, 2)
            pe.wait_ge(w_in, 16 * kt)
            pe.wait_ge(skip_w_in, 16 * kt)
            one_ahead(pe, transposes, products)


def attend(nc, heads, width, relu, counts, xl, src_row, dst_col, bias, gain, shift, eps_half, ident, skip, out):
    UNITS = 2 * heads
    F = heads * width
    PARTS = [(n, min(BANK, width - n)) for n in range(0, width, BANK)]
    PAIR = 2 if heads > 1 else 1
    TAKES = heads // PAIR

    def staged(eng, steps):
        longest = max(lag for lag, _ in steps)

        def tick(turn, j, first=-longest, end=UNITS):
            for lag, step in steps:
                k = j - lag
                if first <= k < end:
                    step(turn * 2 + k // heads, k % heads, turn * UNITS + k, k % UNITS)

        peeled = -(-longest // UNITS)
        for turn in range(peeled):
            for j in range(UNITS):
                tick(turn, j, first=-turn * UNITS)
        with eng.Fori(peeled, NB // 2) as turn:
            for j in range(UNITS):
                tick(turn, j)
        for j in range(UNITS, UNITS + longest):
            tick(NB // 2 - 1, j)

    with ExitStack() as ctx:
        sb, ps, sem = scope(nc, ctx)
        L = f"_{heads}"
        rows = sb("rows" + L, [P, 3, F], FP32)
        bias_row, gain_row, shift_row = (rows[:, i, :] for i in range(3))
        slope_dst = sb("slope_dst" + L, [P, NB, heads], FP32)
        absent = [sb(f"absent{L}{u}", [P, NPAD], FP32) for u in (0, 1)]
        present = [sb(f"present{L}{u}", [P, NPAD], FP32) for u in (0, 1)]
        leaky = [sb(f"leaky{L}{u}", [P, NPAD], FP32) for u in (0, 1)]
        weight = [sb(f"weight{L}{u}", [P, NPAD], FP32) for u in (0, 1)]
        weight_T = [sb(f"weight_T{L}{u}", [P, NB, P], FP32) for u in (0, 1)]
        cols = [sb(f"cols{L}{u}", [P, 4], FP32) for u in (0, 1)]
        total, inverse = sb("total" + L, [P, UNITS], FP32), sb("inverse" + L, [P, UNITS], FP32)
        h = [sb(f"h{L}{u}", [P, F], FP32) for u in (0, 1)]
        skip_t = [sb(f"skip_t{L}{u}", [P, F], FP32) for u in (0, 1)]
        stats = [sb(f"stats{L}{u}", [P, 24], FP32) for u in (0, 1)]
        ps_t = [ps(f"ps_t{L}{u}", [P, 3 * BANK]) for u in (0, 1)]
        ps_o = ps("ps_o" + L, [P, 2 * BANK])

        (rows_in, slopes_ready, absent_ready, present_ready, scaled, leaky_ready, exp_ready, weight_ready,
         turned, T_ready, summed, sums_free, order_max, order_take, order_stats, passed, stats_ready,
         root_ready, scaled_out, gained, shifted_out, h_free, pool_order, h_ready) = (
            sem(n + L) for n in (
                "rows_in", "slopes_ready", "absent_ready", "present_ready", "scaled", "leaky_ready",
                "exp_ready", "weight_ready", "turned", "T_ready", "summed", "sums_free", "order_max",
                "order_take", "order_stats", "passed", "stats_ready", "root_ready", "scaled_out", "gained",
                "shifted_out", "h_free", "pool_order", "h_ready"))
        skip_in = [sem(f"skip_in{L}{u}") for u in (0, 1)]
        h_out = [sem(f"h_out{L}{u}") for u in (0, 1)]
        block = ctx.enter_context(nc.Block())

        @block.sync
        def _(sp):
            for i, r in enumerate((bias, gain, shift)):
                sp.dma_start(rows[:, i, :], r.partition_broadcast(P)).then_inc(rows_in, 16)
            for u in (0, 1):
                sp.sem_inc(h_out[u], 16)
            for b, u, _ in blocks_by_two(sp):
                sp.wait_ge(h_free, b + 1)
                sp.dma_start(skip_t[u][:, :], skip[bass.ds(b, 1), :, :].rearrange("b p c -> (b p) c")).then_inc(skip_in[u], 16)
                sp.wait_ge(h_ready, b + 1)
                sp.dma_start(out[bass.ds(b, 1), :, :].rearrange("b p c -> (b p) c"), h[u][:, :]).then_inc(h_out[u], 16)
            for u in (0, 1):
                sp.wait_ge(h_out[u], 16 * (NB // 2 + 1))

        @block.gpsimd
        def _(pool):
            pool.wait_ge(rows_in, 48)
            for b, u, _ in blocks_by_two(pool):
                chain = Chain(pool, pool_order, 1, b)
                pool.wait_ge(stats_ready, b + 1)
                root(nc, pool, stats[u], eps_half, chain).then_inc(root_ready, 1)
                chain.end()
                pool.wait_ge(scaled_out, b + 1)
                pool.tensor_tensor(h[u][:, :], h[u][:, :], gain_row, ALU.mult).then_inc(gained, 1)
                pool.wait_ge(gained, b + 1)
                pool.tensor_tensor(h[u][:, :], h[u][:, :], shift_row, ALU.add).then_inc(shifted_out, 1)

        @block.vector
        def _(dve):
            dve.sem_inc(h_free, 2)
            dve.sem_inc(sums_free, TAKES)
            dve.tensor_scalar(slope_dst[:, :, :], dst_col[:, :, :], SLOPE, None, ALU.mult).then_inc(slopes_ready, 1)
            dve.wait_ge(rows_in, 48)

            def term(b, head):
                return dst_col[:, bass.ds(b, 1), head:head + 1].rearrange("p b h -> p (b h)")

            def edges(b):
                return counts[:, bass.ds(b, 1), :].rearrange("p b n -> p (b n)")

            def largest(b, head, unit, j):
                u, bu, c = j % 2, j // heads % 2, cols[j % 2]
                if head == 0:
                    dve.tensor_scalar(absent[bu][:, :], edges(b), 0.0, ABSENT, ALU.is_equal, ALU.mult).then_inc(absent_ready, 1)
                    dve.wait_ge(absent_ready, b + 1)
                    split_wait(dve, passed)
                dve.tensor_tensor_reduce(out=present[u][:, :], in0=src_row[:, head, :], in1=absent[bu][:, :],
                                         scale=1.0, scalar=2 * ABSENT, op0=ALU.add, op1=ALU.max,
                                         accum_out=c[:, 0:1]).then_inc(present_ready, 1)
                dve.wait_ge(present_ready, unit + 1)
                dve.scalar_tensor_tensor(out=c[:, 1:2], in0=c[:, 0:1], scalar=-1.0, in1=term(b, head),
                                         op0=ALU.mult, op1=ALU.subtract).then_inc(order_max, 1)
                dve.wait_ge(order_max, unit + 1)
                dve.scalar_tensor_tensor(out=c[:, 2:3], in0=c[:, 1:2], scalar=SLOPE, in1=c[:, 1:2],
                                         op0=ALU.mult, op1=ALU.min)

            def leak(b, head, unit, j):
                u = j % 2
                dve.wait_ge(scaled, unit + 1)
                dve.scalar_tensor_tensor(out=leaky[u][:, :], in0=present[u][:, :], scalar=term(b, head),
                                         in1=leaky[u][:, :], op0=ALU.add, op1=ALU.max).then_inc(leaky_ready, 1)

            def weigh(b, head, unit, j):
                u = j % 2
                dve.wait_ge(exp_ready, unit + 1)
                dve.scalar_tensor_tensor(out=weight[u][:, :], in0=weight[u][:, :], scalar=1.0, in1=edges(b),
                                         op0=ALU.mult, op1=ALU.mult, accum_out=total[:, j:j + 1]).then_inc(weight_ready, 1)

            def take(b, head, unit, j):
                if head % PAIR != PAIR - 1:
                    return
                bu, first, n = j // heads % 2, j - PAIR + 1, b * TAKES + head // PAIR
                dve.wait_ge(summed, unit + 3)
                dve.tensor_scalar(inverse[:, first:j + 1], total[:, first:j + 1], 1e-16, None, ALU.add).then_inc(order_take, 1)
                dve.wait_ge(order_take, n * 2 + 1)
                dve.reciprocal(inverse[:, first:j + 1], inverse[:, first:j + 1]).then_inc(order_take, 1)
                dve.wait_ge(order_take, n * 2 + 2)
                if head == PAIR - 1:
                    dve.wait_ge(h_out[bu], x_loads(b, bu))
                for i in range(PAIR):
                    at = (head - PAIR + 1 + i) * width
                    last = dve.scalar_tensor_tensor(out=h[bu][:, at:at + width], in0=ps_o[:, at:at + width],
                                                    scalar=inverse[:, first + i:first + i + 1],
                                                    in1=bias_row[:, at:at + width], op0=ALU.mult, op1=ALU.add)
                last.then_inc(sums_free, 1)
                if head == heads - 1:
                    dve.wait_ge(sums_free, b * TAKES + 2 * TAKES)
                    n = -(-F // BANK)
                    part = F // n
                    for i in range(n):
                        last = dve.bn_stats(stats[bu][:, 8 + 6 * i:14 + 6 * i], h[bu][:, i * part:(i + 1) * part])
                    last.then_inc(order_stats, 1)
                    dve.wait_ge(order_stats, b + 1)
                    split_wait(dve, passed)
                    dve.bn_aggr(stats[bu][:, 0:2], stats[bu][:, 8:8 + 6 * n]).then_inc(stats_ready, 1)

            def scale(b, head, unit, j):
                if head != heads - 1:
                    return
                bu = j // heads % 2
                dve.wait_ge(root_ready, b + 1)
                dve.tensor_scalar(h[bu][:, :], h[bu][:, :], stats[bu][:, 0:1], stats[bu][:, 3:4],
                                  ALU.subtract, ALU.mult).then_inc(scaled_out, 1)

            def close(b, head, unit, j):
                if head != heads - 1:
                    return
                bu = j // heads % 2
                dve.wait_ge(shifted_out, b + 1)
                dve.wait_ge(skip_in[bu], x_loads(b, bu))
                if relu:
                    last = dve.scalar_tensor_tensor(out=h[bu][:, :], in0=h[bu][:, :], scalar=0.0, in1=skip_t[bu][:, :],
                                                    op0=ALU.max, op1=ALU.add)
                else:
                    last = dve.tensor_tensor(h[bu][:, :], h[bu][:, :], skip_t[bu][:, :], ALU.add)
                last.then_inc(h_ready, 1)
                dve.wait_ge(h_ready, b + 1)
                dve.sem_inc(h_free, 1)

            if heads > 1:
                staged(dve, [(6, close), (5, scale), (4, take), (2, weigh), (0, largest), (1, leak)])
            else:
                staged(dve, [(5, close), (4, take), (2, weigh), (0, largest), (1, leak), (4, scale)])

        @block.scalar
        def _(act):
            act.sem_inc(T_ready, 2)
            act.wait_ge(slopes_ready, 1)

            def scaled_sum(b, head, unit, j):
                u = j % 2
                act.wait_ge(present_ready, unit + 1)
                act.activation(leaky[u][:, :], present[u][:, :], ACT.Identity, scale=SLOPE,
                               bias=slope_dst[:, bass.ds(b, 1), head:head + 1].rearrange("p b h -> p (b h)")).then_inc(scaled, 1)

            def exponential(b, head, unit, j):
                u = j % 2
                act.wait_ge(turned, unit + 1)
                act.wait_ge(leaky_ready, unit + 1)
                act.activation(weight[u][:, :], leaky[u][:, :], ACT.Exp, bias=cols[u][:, 2:3]).then_inc(exp_ready, 1)

            def move_T(b, head, unit, j):
                u = j % 2
                act.wait_ge(summed, unit + 1)
                act.wait_ge(turned, unit + 3)
                act.activation(weight_T[u][:, :, :], ps_t[u][:, 0:NPAD].rearrange("p (s d) -> p s d", d=P), ACT.Copy).then_inc(T_ready, 1)

            staged(act, [(3, move_T), (0, scaled_sum), (1, exponential)])

        @block.tensor
        def _(pe):
            pe.sem_inc(turned, 2)
            pe.sem_inc(summed, 2)

            def turn_weights(b, head, unit, j):
                u = j % 2
                pe.wait_ge(weight_ready, unit + 1)
                pe.wait_ge(T_ready, unit + 1)
                for s in range(NB):
                    last = pe.transpose(ps_t[u][:, s * P:(s + 1) * P], weight[u][:, s * P:(s + 1) * P], ident[:, :])
                last.then_inc(turned, 1)

            def sum_up(b, head, unit, j):
                u = j % 2
                pe.wait_ge(T_ready, unit + 3)
                if head % PAIR == 0:
                    pe.wait_ge(sums_free, b * TAKES + head // PAIR + 1)
                for n, w in PARTS:
                    for s in range(NB):
                        last = pe.matmul(ps_o[:, head * width + n:head * width + n + w], weight_T[u][:, s, :],
                                         xl[:, s, head * width + n:head * width + n + w],
                                         start=(s == 0), stop=(s == NB - 1))
                last.then_inc(summed, 1)

            staged(pe, [(2, turn_weights), (3, sum_up)])


def turn_tokens(nc, x, ident, eps_half, xnT):
    with ExitStack() as ctx:
        sb, ps, sem = scope(nc, ctx)
        xt = [sb(f"xt_n{u}", [P, C_IN], FP32) for u in (0, 1)]
        xn = [sb(f"xn_n{u}", [P, C_IN], FP32) for u in (0, 1)]
        stats = [sb(f"stats_n{u}", [P, 24], FP32) for u in (0, 1)]
        ps_t = [ps(f"ps_t_n{u}", [P, 2 * BANK]) for u in (0, 1)]
        x_free, stats_ready, root_ready, pool_order, xn_ready, turned, moved, order, passed = (
            sem(n + "_n") for n in ("x_free", "stats_ready", "root_ready", "pool_order", "xn_ready",
                                    "turned", "moved", "order", "passed"))
        x_in = [sem(f"x_in_n{u}") for u in (0, 1)]
        block = ctx.enter_context(nc.Block())

        @block.sync
        def _(sp):
            for b, u, _ in blocks_by_two(sp):
                sp.wait_ge(x_free, b + 1)
                sp.dma_start(xt[u][:, :], x[bass.ds(b, 1), :, :].rearrange("b p c -> (b p) c")).then_inc(x_in[u], 16)

        @block.gpsimd
        def _(pool):
            for b, u, _ in blocks_by_two(pool):
                chain = Chain(pool, pool_order, 1, b)
                pool.wait_ge(stats_ready, b + 1)
                root(nc, pool, stats[u], eps_half, chain).then_inc(root_ready, 1)
                chain.end()

        @block.vector
        def _(dve):
            dve.sem_inc(x_free, 2)
            for b, u, _ in blocks_by_two(dve):
                link = Chain(dve, order, 2, b)
                dve.wait_ge(x_in[u], x_loads(b, u))
                dve.wait_ge(turned, b + 1)
                normalize(nc, dve, (stats_ready, root_ready, passed, b + 1), link, xt[u][:, :], stats[u],
                          xn[u][:, :], C_IN).then_inc(xn_ready, 1)
                link.end()
                dve.wait_ge(xn_ready, b + 1)
                dve.sem_inc(x_free, 1)

        @block.tensor
        def _(pe):
            pe.sem_inc(turned, 2)
            for b, u, _ in blocks_by_two(pe):
                pe.wait_ge(xn_ready, b + 1)
                pe.wait_ge(moved, b + 1)
                for k in range(KT):
                    last = pe.transpose(ps_t[u][:, k * P:(k + 1) * P], xn[u][:, k * P:(k + 1) * P], ident[:, :])
                last.then_inc(turned, 1)

        @block.scalar
        def _(act):
            act.sem_inc(moved, 2)
            for b, u, _ in blocks_by_two(act):
                act.wait_ge(turned, b + 3)
                act.activation(xnT[:, :, bass.ds(b * P, P)], ps_t[u][:, 0:C_IN].rearrange("p (k c) -> p k c", k=KT),
                               ACT.Copy).then_inc(moved, 1)


def choose_experts(nc, xnT, w1, b1, w2, b2, share):
    with ExitStack() as ctx:
        sb, ps, sem = scope(nc, ctx)
        gate_w1 = sb("gate_w1", [P, KT, GATE], FP32)
        gate_b1 = sb("gate_b1", [GATE, 1], FP32)
        gate_w2 = sb("gate_w2", [GATE, EXPERTS], FP32)
        gate_b2 = sb("gate_b2", [P, 1, EXPERTS], FP32)
        hidden = sb("gate_hidden", [GATE, NPAD], FP32)
        gate = sb("gate", [P, NB, EXPERTS], FP32)
        expd = sb("gate_exp", [P, NB, EXPERTS], FP32)
        largest, total = sb("gate_max", [P, NB, 1], FP32), sb("gate_sum", [P, NB, 1], FP32)
        keep = sb("gate_keep", [P, NB, EXPERTS], FP32)
        above = sb("gate_above", [P, 6, NB], FP32)
        ps_h = ps("ps_hidden", [GATE, 3 * BANK])
        ps_g = ps("ps_gate", [P, BANK])
        loaded, hidden_done, hidden_ready, logits_done, shifted, exp_ready, order = (
            sem(n) for n in ("gate_loaded", "hidden_done", "hidden_ready", "logits_done", "gate_shifted",
                             "gate_exp_ready", "gate_order"))
        block = ctx.enter_context(nc.Block())

        @block.sync
        def _(sp):
            sp.dma_start(gate_w1[:, :, :], w1.rearrange("(k p) n -> p k n", p=P)).then_inc(loaded, 16)
            sp.dma_start(gate_b1[:, :], b1.unsqueeze(1)).then_inc(loaded, 16)
            sp.dma_start(gate_w2[:, :], w2).then_inc(loaded, 16)
            sp.dma_start(gate_b2[:, 0, :], b2.partition_broadcast(P)).then_inc(loaded, 16)

        @block.tensor
        def _(pe):
            pe.wait_ge(loaded, 64)
            for n in range(0, NPAD, BANK):
                wide = min(BANK, NPAD - n)
                for k in range(KT):
                    last = pe.matmul(ps_h[:, n:n + wide], gate_w1[:, k, :], xnT[:, k, n:n + wide],
                                     start=(k == 0), stop=(k == KT - 1))
            last.then_inc(hidden_done, 1)
            pe.wait_ge(hidden_ready, 1)
            for b in range(NB):
                last = pe.matmul(ps_g[:, b * EXPERTS:(b + 1) * EXPERTS], hidden[:, b * P:(b + 1) * P],
                                 gate_w2[:, :], start=True, stop=True)
            last.then_inc(logits_done, 1)

        @block.scalar
        def _(act):
            act.wait_ge(hidden_done, 1)
            act.activation(hidden[:, :], ps_h[:, 0:NPAD], ACT.Relu, bias=gate_b1[:, :]).then_inc(hidden_ready, 1)
            for i in (0, 1):
                act.wait_ge(shifted, i + 1)
                act.activation(expd[:, :, :], gate[:, :, :], ACT.Exp).then_inc(exp_ready, 1)

        @block.vector
        def _(dve):
            link = Chain(dve, order)

            def of(t):
                return t[:, :, :].broadcast_to([P, NB, EXPERTS])

            dve.wait_ge(loaded, 64)
            dve.wait_ge(logits_done, 1)
            link(dve.tensor_tensor(gate[:, :, :], ps_g[:, 0:NB * EXPERTS].rearrange("p (b e) -> p b e", b=NB),
                                   of(gate_b2), ALU.add))
            link(dve.tensor_reduce(largest[:, :, :], gate[:, :, :], axis=AX.X, op=ALU.max))
            dve.tensor_tensor(gate[:, :, :], gate[:, :, :], of(largest), ALU.subtract).then_inc(shifted, 1)
            dve.wait_ge(exp_ready, 1)
            link(dve.tensor_reduce(total[:, :, :], expd[:, :, :], axis=AX.X, op=ALU.add))
            link(dve.reciprocal(total[:, :, :], total[:, :, :]))
            link(dve.tensor_tensor(gate[:, :, :], expd[:, :, :], of(total), ALU.mult))
            g = [gate[:, :, e] for e in range(EXPERTS)]
            for i, (x, y, op) in enumerate(((g[1], g[0], ALU.is_gt), (g[2], g[0], ALU.is_gt),
                                            (g[0], g[1], ALU.is_ge), (g[2], g[1], ALU.is_gt),
                                            (g[0], g[2], ALU.is_ge), (g[1], g[2], ALU.is_ge))):
                link(dve.tensor_tensor(above[:, i, :], x, y, op))
            for e in range(EXPERTS):
                link(dve.tensor_tensor(keep[:, :, e], above[:, 2 * e, :], above[:, 2 * e + 1, :], ALU.mult))
            link(dve.tensor_scalar(keep[:, :, :], keep[:, :, :], -1.0, 1.0, ALU.mult, ALU.add))
            link(dve.tensor_reduce(largest[:, :, :], gate[:, :, :], axis=AX.X, op=ALU.max))
            dve.tensor_tensor(gate[:, :, :], gate[:, :, :], of(largest), ALU.subtract).then_inc(shifted, 1)
            dve.wait_ge(exp_ready, 2)
            link(dve.tensor_tensor(keep[:, :, :], keep[:, :, :], expd[:, :, :], ALU.mult))
            link(dve.tensor_reduce(total[:, :, :], keep[:, :, :], axis=AX.X, op=ALU.add))
            link(dve.reciprocal(total[:, :, :], total[:, :, :]))
            link(dve.tensor_tensor(share[:, :, :].rearrange("p e b -> p b e"), keep[:, :, :], of(total), ALU.mult))


def run_experts(nc, xnT, wqk, bqk, wv, bv, conv_w, conv_b, share, ident, y):
    CT = HD // P
    SCALE = HD ** -0.5
    MINE = CT + CT + NB
    with ExitStack() as ctx:
        sb, ps, sem = scope(nc, ctx)
        w = sb("w_expert", [P, 3, KT, HD], FP32)
        qk_bias = sb("qk_bias", [P, 2, EXPERTS, CT], FP32)
        v_bias = sb("v_bias", [P, EXPERTS, HD], FP32)
        taps = sb("taps", [P, EXPERTS, CT, 3], FP32)
        tap_bias = sb("tap_bias", [P, EXPERTS, CT], FP32)
        raw = sb("raw_q", [P, CT, NODES + 2], FP32)
        qT, kT = sb("qT", [P, CT, NPAD], FP32), sb("kT", [P, CT, NPAD], FP32)
        v = sb("v", [P, NB, HD], FP32)
        future = sb("future", [P, P], FP32)
        prob = [sb(f"prob{u}", [P, NPAD], FP32) for u in (0, 1)]
        prob_T = [sb(f"prob_T{u}", [P, NB, P], FP32) for u in (0, 1)]
        cols = [sb(f"softmax{u}", [P, 4], FP32) for u in (0, 1)]
        ps_a, ps_b = ps("ps_scores", [P, 3 * BANK]), ps("ps_turned", [P, 3 * BANK])
        ps_y = [ps(f"ps_y{u}", [P, BANK]) for u in (0, 1)]
        (loaded, consts, w_in, projected, a_free, b_free, y_free, q_raw, q_tap, order, tap_order, q_ready, k_ready, v_ready,
         scored, masked, max_ready, prob_ready, turned, summed, taken, values_done) = (
            sem(n + "_x") for n in (
                "loaded", "consts", "w_in", "projected", "a_free", "b_free", "y_free", "q_raw", "q_tap",
                "order", "tap_order", "q_ready", "k_ready", "v_ready", "scored", "masked", "max_ready", "prob_ready",
                "turned", "summed", "taken", "values_done"))
        block = ctx.enter_context(nc.Block())

        @block.sync
        def _(sp):
            sp.dma_start(qk_bias[:, :, :, :], bqk.rearrange("(g e c p) -> p g e c", g=2, e=EXPERTS, c=CT, p=P),
                         allow_slow_non_contiguous=True).then_inc(loaded, 16)
            sp.dma_start(v_bias[:, :, :].rearrange("p e c -> p (e c)"), bv.rearrange("e c -> (e c)").partition_broadcast(P)).then_inc(loaded, 16)
            sp.dma_start(taps[:, 0, :, :], conv_w.rearrange("(c p) o t -> p c (o t)", p=P)).then_inc(loaded, 16)
            sp.dma_start(tap_bias[:, 0, :], conv_b.rearrange("(c p) -> p c", p=P),
                         allow_slow_non_contiguous=True).then_inc(loaded, 16)
            with sp.Fori(0, EXPERTS) as e:
                sp.wait_ge(values_done, e + 1)
                for g in (0, 1):
                    sp.dma_start(w[:, g, :, :], wqk.rearrange("(k p) (g e c) -> g p k e c", p=P, g=2, e=EXPERTS)
                                 [g, :, :, bass.ds(e, 1), :].rearrange("p k e c -> p k (e c)")).then_inc(w_in, 16)
                sp.dma_start(w[:, 2, :, :], wv.rearrange("e (k p) c -> p k e c", p=P)
                             [:, :, bass.ds(e, 1), :].rearrange("p k e c -> p k (e c)")).then_inc(w_in, 16)

        @block.gpsimd
        def _(pool):
            pool.memset(taps[:, 1:EXPERTS, :, 0:1], 0.0)
            pool.memset(taps[:, 1:EXPERTS, :, 1:2], 1.0)
            pool.memset(taps[:, 1:EXPERTS, :, 2:3], 0.0)
            pool.memset(tap_bias[:, 1:EXPERTS, :], 0.0)
            pool.memset(raw[:, :, 0:1], 0.0)
            pool.memset(raw[:, :, NODES + 1:NODES + 2], 0.0)
            pool.memset(qT[:, :, NODES:NPAD], 0.0)
            pool.memset(future[:, :], 0.0).then_inc(consts, 1)
            pool.wait_ge(consts, 1)
            pool.affine_select(out=future[:, :], in_=future[:, :], compare_op=ALU.is_ge, fill=ABSENT, base=0,
                               pattern=[[-1, P]], channel_multiplier=1).then_inc(consts, 1)

        @block.tensor
        def _(pe):
            pe.sem_inc(y_free, 2)
            pe.sem_inc(values_done, 1)
            pe.wait_ge(consts, 2)
            with pe.Fori(0, EXPERTS) as e:
                pe.wait_ge(w_in, (e + 1) * 48)
                for i in range(2 * CT):
                    g, c = divmod(i, CT)
                    to = (ps_a, ps_b)[i % 2]
                    if i % 2 == 0:
                        pe.wait_ge(a_free, e * (NB + CT) + i // 2 + 1)
                    else:
                        pe.wait_ge(b_free, e * (NB + CT) + i // 2 + 1)
                    for n in range(0, NPAD, BANK):
                        wide = min(BANK, NPAD - n)
                        for k in range(KT):
                            last = pe.matmul(to[:, n:n + wide], w[:, g, k, c * P:(c + 1) * P],
                                             xnT[:, k, n:n + wide], start=(k == 0), stop=(k == KT - 1))
                    last.then_inc(projected, 1)
                for b in range(NB):
                    pe.wait_ge(y_free, e * 2 * NB + b + 1)
                    for k in range(KT):
                        last = pe.matmul(ps_y[b % 2][:, 0:HD], xnT[:, k, b * P:(b + 1) * P], w[:, 2, k, :],
                                         start=(k == 0), stop=(k == KT - 1))
                    last.then_inc(projected, 1)
                pe.wait_ge(projected, (e + 1) * MINE)
                pe.sem_inc(values_done, 1)

                def score(i):
                    pe.wait_ge(a_free, e * (NB + CT) + CT + i + 1)
                    for n in range(0, (i + 1) * P, BANK):
                        wide = min(BANK, (i + 1) * P - n)
                        for c in range(CT):
                            last = pe.matmul(ps_a[:, n:n + wide], qT[:, c, i * P:(i + 1) * P], kT[:, c, n:n + wide],
                                             start=(c == 0), stop=(c == CT - 1))
                    last.then_inc(scored, 1)

                def turn(i):
                    pe.wait_ge(prob_ready, e * NB + i + 1)
                    pe.wait_ge(b_free, e * (NB + CT) + CT + i + 1)
                    for s in range(i + 1):
                        last = pe.transpose(ps_b[:, s * P:(s + 1) * P], prob[i % 2][:, s * P:(s + 1) * P], ident[:, :])
                    last.then_inc(turned, 1)

                def average(i):
                    pe.wait_ge(b_free, e * (NB + CT) + CT + i + 2)
                    pe.wait_ge(v_ready, e * NB + i + 1)
                    pe.wait_ge(y_free, e * 2 * NB + NB + i + 1)
                    for s in range(i + 1):
                        last = pe.matmul(ps_y[i % 2][:, 0:HD], prob_T[i % 2][:, s, :], v[:, s, :],
                                         start=(s == 0), stop=(s == i))
                    last.then_inc(summed, 1)

                pe.wait_ge(q_ready, (e + 1) * CT)
                pe.wait_ge(b_free, e * (NB + CT) + CT + 1)
                score(0)
                for i in range(1, NB):
                    turn(i - 1)
                    score(i)
                    average(i - 1)
                turn(NB - 1)
                average(NB - 1)

        @block.scalar
        def _(act):
            act.sem_inc(a_free, 1)
            act.sem_inc(b_free, 1)
            act.wait_ge(loaded, 64)
            act.wait_ge(consts, 2)
            with act.Fori(0, EXPERTS) as e:
                for i in range(2 * CT):
                    g, c = divmod(i, CT)
                    of, free = ((ps_a, a_free), (ps_b, b_free))[i % 2]
                    bias = qk_bias[:, g, bass.ds(e, 1), c:c + 1].rearrange("p e c -> p (e c)")
                    act.wait_ge(projected, e * MINE + i + 1)
                    if g == 0:
                        act.activation(raw[:, c, 1:NODES + 1], of[:, 0:NODES], ACT.Identity, bias=bias).then_inc(free, 1)
                        act.wait_ge(free, e * (NB + CT) + 2)
                        act.activation(qT[:, c, 0:NODES], raw[:, c, 0:NODES], ACT.Identity,
                                       scale=taps[:, bass.ds(e, 1), c, 0:1].rearrange("p e t -> p (e t)"),
                                       bias=tap_bias[:, bass.ds(e, 1), c:c + 1].rearrange("p e c -> p (e c)")
                                       ).then_inc(q_tap, 1)
                    else:
                        act.activation(kT[:, c, :], of[:, 0:NPAD], ACT.Identity, bias=bias).then_inc(free, 1)
                for i in range(NB):
                    wide = (i + 1) * P
                    act.wait_ge(max_ready, e * NB + i + 1)
                    act.activation(prob[i % 2][:, 0:wide], ps_a[:, 0:wide], ACT.Exp, scale=SCALE,
                                   bias=cols[i % 2][:, 1:2], accum_out=cols[i % 2][:, 2:3]).then_inc(prob_ready, 1)
                    act.wait_ge(prob_ready, e * NB + i + 1)
                    act.sem_inc(a_free, 1)
                    act.wait_ge(turned, e * NB + i + 1)
                    act.activation(prob_T[i % 2][:, 0:i + 1, :], ps_b[:, 0:wide].rearrange("p (s t) -> p s t", t=P),
                                   ACT.Copy).then_inc(b_free, 1)

        @block.vector
        def _(dve):
            dve.wait_ge(loaded, 64)
            dve.wait_ge(consts, 2)
            with dve.Fori(0, EXPERTS) as e:
                for c in range(CT):
                    dve.wait_ge(q_tap, e * CT + c + 1)
                    for t in (1, 2):
                        last = dve.scalar_tensor_tensor(
                            out=qT[:, c, 0:NODES], in0=raw[:, c, t:t + NODES],
                            scalar=taps[:, bass.ds(e, 1), c, t:t + 1].rearrange("p e t -> p (e t)"),
                            in1=qT[:, c, 0:NODES], op0=ALU.mult, op1=ALU.add)
                        last.then_inc(tap_order, 1)
                        dve.wait_ge(tap_order, e * 2 * CT + 2 * c + t)
                    dve.sem_inc(q_ready, 1)
                for b in range(NB):
                    dve.wait_ge(projected, e * MINE + 2 * CT + b + 1)
                    dve.tensor_tensor(v[:, b, :], ps_y[b % 2][:, 0:HD],
                                      v_bias[:, bass.ds(e, 1), :].rearrange("p e c -> p (e c)"), ALU.add).then_inc(v_ready, 1)
                    dve.wait_ge(v_ready, e * NB + b + 1)
                    dve.sem_inc(y_free, 1)

                def softmax_max(i):
                    c = cols[i % 2]
                    dve.wait_ge(scored, e * NB + i + 1)
                    dve.tensor_tensor(ps_a[:, i * P:(i + 1) * P], ps_a[:, i * P:(i + 1) * P], future[:, :],
                                      ALU.add).then_inc(masked, 1)
                    dve.wait_ge(masked, e * NB + i + 1)
                    dve.tensor_reduce(c[:, 0:1], ps_a[:, 0:(i + 1) * P], axis=AX.X, op=ALU.max).then_inc(order, 1)
                    dve.wait_ge(order, e * 3 * NB + LINKS[i][0])
                    dve.tensor_scalar(c[:, 1:2], c[:, 0:1], -SCALE, None, ALU.mult).then_inc(max_ready, 1)

                def take(i):
                    c = cols[i % 2]
                    dve.wait_ge(summed, e * NB + i + 1)
                    dve.reciprocal(c[:, 3:4], c[:, 2:3]).then_inc(order, 1)
                    dve.wait_ge(order, e * 3 * NB + LINKS[i][1])
                    dve.tensor_tensor(c[:, 3:4], c[:, 3:4], share[:, bass.ds(e, 1), i:i + 1].rearrange("p e b -> p (e b)"),
                                      ALU.mult).then_inc(order, 1)
                    dve.wait_ge(order, e * 3 * NB + LINKS[i][1] + 1)
                    dve.tensor_scalar(y[:, i, bass.ds(e * HD, HD)], ps_y[i % 2][:, 0:HD], c[:, 3:4], None,
                                      ALU.mult).then_inc(taken, 1)
                    dve.wait_ge(taken, e * NB + i + 1)
                    dve.sem_inc(y_free, 1)

                LINKS = [(1 if i == 0 else 3 * i - 1, 3 * i + 3 if i < NB - 1 else 3 * NB - 1) for i in range(NB)]
                softmax_max(0)
                for i in range(1, NB):
                    softmax_max(i)
                    take(i - 1)
                take(NB - 1)


def project_out(nc, y, w, bias, x, ident, out):
    PARTS = [(n, min(BANK, C_IN - n)) for n in range(0, C_IN, BANK)]
    with ExitStack() as ctx:
        sb, ps, sem = scope(nc, ctx)
        weights = sb("out_weights", [P, KT, C_IN], FP32)
        bias_row = sb("out_bias", [P, C_IN], FP32)
        yt = [sb(f"yt{u}", [P, C_IN], FP32) for u in (0, 1)]
        yT = [sb(f"yT{u}", [P, KT, P], FP32) for u in (0, 1)]
        xt = [sb(f"xt_o{u}", [P, C_IN], FP32) for u in (0, 1)]
        out_t = [sb(f"out_t{u}", [P, C_IN], FP32) for u in (0, 1)]
        ps_t, ps_o = ps("ps_t_o", [P, 2 * BANK]), [ps(f"ps_o_o{u}", [P, 2 * BANK]) for u in (0, 1)]
        loaded, y_ready, turned, moved, product, taken, out_ready = (
            sem(n + "_o") for n in ("loaded", "y_ready", "turned", "moved", "product", "taken", "out_ready"))
        x_in, stored = ([sem(f"{n}_o{u}") for u in (0, 1)] for n in ("x_in", "stored"))
        block = ctx.enter_context(nc.Block())

        def rows_of(dram, b):
            return dram[bass.ds(b, 1), :, :].rearrange("b p c -> (b p) c")

        @block.sync
        def _(sp):
            sp.dma_start(weights[:, :, :], w.rearrange("(k p) n -> p k n", p=P)).then_inc(loaded, 16)
            sp.dma_start(bias_row[:, :], bias.partition_broadcast(P)).then_inc(loaded, 16)
            for u in (0, 1):
                sp.sem_inc(stored[u], 16)
            for b, u, _ in blocks_by_two(sp):
                sp.wait_ge(out_ready, b + 1)
                sp.dma_start(xt[u][:, :], rows_of(x, b)).then_inc(x_in[u], 16)

        @block.gpsimd
        def _(pool):
            for b, u, _ in blocks_by_two(pool):
                pool.wait_ge(turned, b + 1)
                pool.tensor_copy(yt[u][:, :], y[:, bass.ds(b, 1), :].rearrange("p b c -> p (b c)")).then_inc(y_ready, 1)

        @block.tensor
        def _(pe):
            pe.sem_inc(turned, 2)

            def transposes(b, u):
                pe.wait_ge(y_ready, b + 1)
                pe.wait_ge(moved, b + 1)
                for k in range(KT):
                    last = pe.transpose(ps_t[:, k * P:(k + 1) * P], yt[u][:, k * P:(k + 1) * P], ident[:, :])
                last.then_inc(turned, 1)

            def products(b, u):
                pe.wait_ge(moved, b + 2)
                pe.wait_ge(taken, b + 1)
                for n, wide in PARTS:
                    for k in range(KT):
                        last = pe.matmul(ps_o[u][:, n:n + wide], yT[u][:, k, :], weights[:, k, n:n + wide],
                                         start=(k == 0), stop=(k == KT - 1))
                last.then_inc(product, 1)

            pe.wait_ge(loaded, 32)
            one_ahead(pe, transposes, products)

        @block.scalar
        def _(act):
            act.sem_inc(moved, 1)
            act.sem_inc(product, 2)

            def move_yT(b, u):
                act.wait_ge(turned, b + 3)
                act.wait_ge(product, b + 1)
                act.activation(yT[u][:, :, :], ps_t[:, 0:C_IN].rearrange("p (k c) -> p k c", k=KT), ACT.Copy).then_inc(moved, 1)

            def store(b, u):
                act.wait_ge(out_ready, b + 3)
                act.dma_start(rows_of(out, b), out_t[u][:, :]).then_inc(stored[u], 16)

            one_ahead(act, move_yT, store)
            for u in (0, 1):
                act.wait_ge(stored[u], 16 * (NB // 2 + 1))

        @block.vector
        def _(dve):
            dve.sem_inc(taken, 2)
            dve.sem_inc(out_ready, 2)
            dve.wait_ge(loaded, 32)
            for b, u, _ in blocks_by_two(dve):
                dve.wait_ge(stored[u], x_loads(b, u))
                dve.wait_ge(product, b + 3)
                dve.tensor_tensor(out_t[u][:, :], ps_o[u][:, 0:C_IN], bias_row[:, :], ALU.add).then_inc(taken, 1)
                dve.wait_ge(taken, b + 3)
                dve.wait_ge(x_in[u], x_loads(b, u))
                dve.tensor_tensor(out_t[u][:, :], out_t[u][:, :], xt[u][:, :], ALU.add).then_inc(out_ready, 1)




def gnn_then_experts(nc, x, src, dst, W1, a_src1, a_dst1, b1, g1, be1, Wr1, br1, W2, a_src2, a_dst2, b2, g2, be2,
                     Wr2, br2, Wqk, bqk, Wv, bv, conv_w, conv_b, Wg1, bg1, Wg2, bg2, Wp, bp, out):
    def blocks(dram):
        return dram.rearrange("(b p) c -> b p c", p=P)

    x, out = blocks(x), blocks(out)
    skip1, h1, skip2, x2 = (blocks(nc.dram_tensor(name, [NPAD, c], FP32).ap()) for name, c in (
        ("skip1", HC), ("h1", HC), ("skip2", C_IN), ("x2", C_IN)))
    with ExitStack() as ctx:
        sb, _, sem = scope(nc, ctx)
        ident, ones, eps_half = sb("ident", [P, P], FP32), sb("ones", [P, P], FP32), sb("eps_half", [P, 2], FP32)
        cleared = sem("cleared")
        with nc.Block() as block:
            @block.gpsimd
            def _(pool):
                pool.memset(ident[:, :], 0.0).then_inc(cleared, 1)
                pool.memset(ones[:, :], 1.0)
                pool.memset(eps_half[:, 0:1], LN_EPS)
                pool.memset(eps_half[:, 1:2], -0.5)
                pool.wait_ge(cleared, 1)
                pool.affine_select(out=ident[:, :], in_=ident[:, :], compare_op=ALU.not_equal, fill=1.0, base=0,
                                   pattern=[[-1, P]], channel_multiplier=1)

        with ExitStack() as graph:
            g_sb, _, _ = scope(nc, graph)
            counts = g_sb("counts", [P, NB, NPAD], U16)
            count_edges(nc, src, dst, counts)
            for (layer, kt, heads, width, feats, residual, w, a_src, a_dst, bias, gain, shift, w_skip, b_skip, skip,
                 result) in (
                    (1, KT, HEADS, HID, x, None, W1, a_src1, a_dst1, b1, g1, be1, Wr1, br1, skip1, h1),
                    (2, HKT, 1, C_IN, h1, x, W2, a_src2, a_dst2, b2, g2, be2, Wr2, br2, skip2, x2)):
                with ExitStack() as one:
                    l_sb, _, _ = scope(nc, one)
                    xl = l_sb(f"xl{layer}", [P, NB, heads * width], FP32)
                    src_row = l_sb(f"src_row{layer}", [P, heads, NPAD], FP32)
                    dst_col = l_sb(f"dst_col{layer}", [P, NB, heads], FP32)
                    project(nc, kt, heads, width, layer == 1, feats, residual, w, w_skip, b_skip, a_src, a_dst,
                            ident, ones, eps_half, xl, src_row, dst_col, skip)
                    attend(nc, heads, width, layer == 1, counts, xl, src_row, dst_col, bias, gain, shift,
                           eps_half, ident, skip, result)

        xnT = sb("xnT", [P, KT, NPAD], FP32)
        share = sb("share", [P, EXPERTS, NB], FP32)
        y = sb("y", [P, NB, C_IN], FP32)
        turn_tokens(nc, x2, ident, eps_half, xnT)
        choose_experts(nc, xnT, Wg1, bg1, Wg2, bg2, share)
        run_experts(nc, xnT, Wqk, bqk, Wv, bv, conv_w, conv_b, share, ident, y)
        project_out(nc, y, Wp, bp, x2, ident, out)


_INS = (["x", "src", "dst"] + ["L0_gnn_" + n for n in (
    "W1", "a_src1", "a_dst1", "b1", "g1", "be1", "Wr1", "br1", "W2", "a_src2", "a_dst2", "b2", "g2", "be2", "Wr2",
    "br2")] + ["L0_ffn_" + n for n in ("Wqk", "bqk", "Wv", "bv", "conv_w", "conv_b", "Wg1", "bg1", "Wg2", "bg2",
                                       "Wp", "bp")])


def kernel(**inputs):
    import numpy as np
    import concourse.bacc as bacc
    from concourse.bass_utils import run_bass_kernel_spmd

    nc = bacc.Bacc("TRN2", target_bir_lowering=False, num_devices=1)
    arrays, args = {}, []
    for name in _INS:
        a = np.ascontiguousarray(inputs[name])
        if name == "x":
            a = np.pad(a, ((0, NPAD - NODES), (0, 0)))
        elif name in ("src", "dst"):
            a = np.ascontiguousarray(a.reshape(CHUNKS, EDGE_P).T)
        arrays[f"in_{name}"] = a
        args.append(nc.dram_tensor(f"in_{name}", a.shape, mybir.dt.from_np(a.dtype), kind="ExternalInput").ap())
    args.append(nc.dram_tensor("out_0", (NPAD, C_IN), FP32, kind="ExternalOutput").ap())
    gnn_then_experts(nc, *args)
    r = run_bass_kernel_spmd(nc, [arrays], core_ids=[0])
    return r.results[0]["out_0"][:NODES]
```

```python
import concourse.bass as bass
from concourse import mybir
from contextlib import ExitStack

FP32 = mybir.dt.float32
FP32R = mybir.dt.float32r
FP16 = mybir.dt.float16
BF16 = mybir.dt.bfloat16
I32 = mybir.dt.int32
U16 = mybir.dt.uint16
ALU = mybir.AluOpType
ACT = mybir.ActivationFunctionType
AX = mybir.AxisListType

NODES, C_IN = 1250, 768
P = 128
NB = 10
NPAD = NB * P
KT = C_IN // P
HEADS, HID = 4, 256
HC = HEADS * HID
HKT = HC // P
EDGES, EDGE_P = 40000, 125
CHUNKS = EDGES // EDGE_P
GROUP = 4
GROUPS = CHUNKS // GROUP
EXPERTS, HD = 3, 256
GATE = 32
LN_EPS = 1e-5
SLOPE = 0.2
ABSENT = -1.0e30
BANK = 512


class Chain:

    def __init__(self, eng, sem, links=0, turn=0):
        self.eng, self.sem, self.links, self.turn, self.n = eng, sem, links, turn, 0

    def __call__(self, instruction):
        instruction.then_inc(self.sem, 1)
        self.n += 1
        self.eng.wait_ge(self.sem, self.turn * self.links + self.n)

    def end(self):
        assert self.n == self.links, self.n


def scope(nc, ctx):
    sems = []

    def clear():
        if sems:
            with nc.Block() as block:
                @block.gpsimd
                def _(pool):
                    nc.clear_and_free_semaphores(sems)

    ctx.callback(clear)

    def sb(name, shape, dt):
        return ctx.enter_context(nc.sbuf_tensor(name, shape, dt))

    def ps(name, shape, dt=FP32):
        return ctx.enter_context(nc.psum_tensor(name, shape, dt))

    def sem(name):
        sems.append(nc.alloc_semaphore(name))
        return sems[-1]

    return sb, ps, sem


def blocks_by_two(eng):
    with eng.Fori(0, NB // 2) as turn:
        for u in (0, 1):
            yield turn * 2 + u, u, turn


def x_loads(b, u):
    return (b - u) * 8 + 16


def one_ahead(eng, early, late, done=0, peel=False):
    if not done:
        early(0, 0)
    if peel:
        for b in (0, 1):
            early(b + 1, 1 - b)
            late(b, b)
    with eng.Fori(1 if peel else 0, NB // 2 - 1) as turn:
        early(turn * 2 + 1, 1)
        late(turn * 2, 0)
        early(turn * 2 + 2, 0)
        late(turn * 2 + 1, 1)
    early(NB - 1, 1)
    late(NB - 2, 0)
    late(NB - 1, 1)


class PartedWeight:

    def __init__(self, sem, name, w, buffers, parts, kt):
        self.tiles = w.rearrange("(k p) n -> k p n", p=P)
        self.buffers, self.parts, self.kt = buffers, parts, kt
        self.loaded = [sem(f"{name}_loaded{u}") for u in (0, 1)]
        self.high_done, self.split = sem(name + "_high_done"), sem(name + "_split")

    def each(self, eng):
        with eng.Fori(0, self.kt // 2) as turn:
            for u in (0, 1):
                yield turn * 2 + u, u

    def load(self, eng):
        eng.sem_inc(self.split, 2)
        for k, u in self.each(eng):
            eng.wait_ge(self.split, k + 1)
            eng.dma_start(self.buffers[u], self.tiles[bass.ds(k, 1), :, :].rearrange("k p n -> (k p) n")
                          ).then_inc(self.loaded[u], 16)

    def high(self, act):
        for k, u in self.each(act):
            act.wait_ge(self.loaded[u], x_loads(k, u))
            act.activation(self.parts[0][:, bass.ds(k, 1), :], self.buffers[u].unsqueeze(1), ACT.Copy
                           ).then_inc(self.high_done, 1)

    def low(self, eng):
        for k, u in self.each(eng):
            eng.wait_ge(self.high_done, k + 1)
            eng.tensor_tensor(self.parts[1][:, bass.ds(k, 1), :], self.buffers[u].unsqueeze(1),
                              self.parts[0][:, bass.ds(k, 1), :], ALU.subtract).then_inc(self.split, 1)

    def wait(self, pe):
        pe.wait_ge(self.split, self.kt + 2)


def count_edges(nc, src, dst, counts, weights, buffers):
    with ExitStack() as ctx:
        sb, ps, sem = scope(nc, ctx)
        src_i, dst_i = sb("src_i", [EDGE_P, CHUNKS], I32), sb("dst_i", [EDGE_P, CHUNKS], I32)
        src_f, dst_f = sb("src_f", [EDGE_P, CHUNKS], FP32), sb("dst_f", [EDGE_P, CHUNKS], FP32)
        block_i, block_f = sb("block_i", [EDGE_P, CHUNKS], I32), sb("block_f", [EDGE_P, CHUNKS], FP32)
        upward, downward = sb("upward", [EDGE_P, CHUNKS], FP32), sb("downward", [EDGE_P, CHUNKS], FP32)
        member, masked = sb("member", [EDGE_P, CHUNKS], FP32), sb("masked", [EDGE_P, CHUNKS], FP32)
        node_ids = sb("node_ids", [P, NPAD], FP16)
        span, span_all = sb("span", [P, 2 * NB], FP32), sb("span_all", [P, 2 * NB], FP32)
        row = sb("row", [1, 4, NB], FP32)
        table = sb("table", [1, 3, NB], I32)
        shifted = sb("shifted", [P, NPAD + (NB - 1) * P], BF16)
        AT = (NB - 1) * P
        src_hot = sb("src_hot", [P, 2 * GROUP, NPAD], BF16)
        dst_hot = sb("dst_hot", [P, 2 * GROUP, P], BF16)
        count_t = [sb(f"count_t{u}", [P, NPAD], U16) for u in (0, 1)]
        parted = [PartedWeight(sem, f"weight{i}", w, buffers, parts, w.shape[0] // P)
                  for i, (w, parts) in enumerate(weights)]
        sums = [ps(f"sums{u}", [P, 3 * BANK]) for u in (0, 1)]
        stored = [sem(f"stored{u}") for u in (0, 1)]
        edges_in, consts, ids_ready = sem("edges_in"), sem("consts"), sem("ids_ready")
        span_ready, span_reduced, table_ready = sem("span_ready"), sem("span_reduced"), sem("table_ready")
        hot_ready, slots_free = sem("hot_ready"), sem("slots_free")
        sums_free, order = sem("sums_free"), sem("order0")
        block = ctx.enter_context(nc.Block())

        def bounds(eng, b):
            return [eng.value_load(table[0:1, i, bass.ds(b, 1)], min_val=0, max_val=m)
                    for i, m in enumerate((GROUPS - 1, GROUPS, GROUPS * (NB - 1)))]

        def first_chunk(eng, first, i):
            return nc.s_assert_within(
                eng.snap((first + i) * GROUP), 0, CHUNKS - GROUP,
                skip_runtime_bounds_check_because="the table's ends lie within the groups")

        @block.sync
        def _(sp):
            sp.dma_start(src_i[:, :], src).then_inc(edges_in, 16)
            sp.dma_start(dst_i[:, :], dst).then_inc(edges_in, 16)
            for i, weight in enumerate(parted):
                if i > 0:
                    parted[i - 1].wait(sp)
                weight.load(sp)
            for u in (0, 1):
                sp.sem_inc(stored[u], 16)
            for b, u, _ in blocks_by_two(sp):
                sp.wait_ge(sums_free, b + 3)
                sp.dma_start(counts[bass.ds(b, 1), :, :].rearrange("b p s -> (b p) s"), count_t[u][:, :]
                             ).then_inc(stored[u], 16)
            for u in (0, 1):
                sp.wait_ge(stored[u], 16 * (NB // 2 + 1))

        @block.gpsimd
        def _(pool):
            pool.iota(upward[:, :], pattern=[[1, GROUPS], [0, GROUP]], base=1, channel_multiplier=0,
                      allow_small_or_imprecise_dtypes=True).then_inc(consts, 1)
            pool.iota(downward[:, :], pattern=[[-1, GROUPS], [0, GROUP]], base=GROUPS,
                      channel_multiplier=0, allow_small_or_imprecise_dtypes=True).then_inc(consts, 1)
            pool.iota(node_ids[:, :], pattern=[[1, NPAD]], base=0, channel_multiplier=0,
                      allow_small_or_imprecise_dtypes=True).then_inc(ids_ready, 1)
            pool.memset(shifted[:, :], 0.0).then_inc(ids_ready, 1)
            pool.wait_ge(ids_ready, 2)
            pool.affine_select(out=shifted[:, AT:AT + P], in_=shifted[:, AT:AT + P],
                               compare_op=ALU.not_equal, fill=1.0, base=0, pattern=[[-1, P]],
                               channel_multiplier=1).then_inc(ids_ready, 1)
            pool.wait_ge(span_ready, 1)
            pool.partition_all_reduce(span_all[0:EDGE_P, :], span[0:EDGE_P, :], EDGE_P,
                                      bass.bass_isa.ReduceOp.max).then_inc(span_reduced, 1)
            for weight in parted:
                weight.low(pool)

        @block.vector
        def _(dve):
            link = Chain(dve, order)
            dve.wait_ge(edges_in, 32)
            link(dve.tensor_copy(src_f[:, :], src_i[:, :]))
            link(dve.tensor_copy(dst_f[:, :], dst_i[:, :]))
            link(dve.tensor_single_scalar(block_i[:, :], dst_i[:, :], 7, ALU.arith_shift_right))
            link(dve.tensor_copy(block_f[:, :], block_i[:, :]))
            dve.wait_ge(consts, 2)
            for b in range(NB):
                link(dve.tensor_scalar(member[:, :], block_f[:, :], float(b), None, ALU.is_equal))
                for i, number in enumerate((upward, downward)):
                    link(dve.tensor_tensor_reduce(
                        out=masked[:, :], in0=member[:, :], in1=number[:, :], scale=1.0, scalar=0.0,
                        op0=ALU.mult, op1=ALU.max, accum_out=span[0:EDGE_P, i * NB + b:i * NB + b + 1]))
            dve.sem_inc(span_ready, 1)
            dve.wait_ge(span_reduced, 1)
            end, start, groups, total = (row[0:1, i, :] for i in range(4))
            link(dve.tensor_scalar(end, span_all[0:1, 0:NB], 1.0, None, ALU.max))
            link(dve.tensor_scalar(start, span_all[0:1, NB:2 * NB], -1.0, float(GROUPS), ALU.mult, ALU.add))
            link(dve.scalar_tensor_tensor(out=start, in0=end, scalar=-1.0, in1=start, op0=ALU.add, op1=ALU.min))
            link(dve.tensor_tensor(groups, end, start, ALU.subtract))
            link(dve.tensor_copy(total, groups))
            for b in range(1, NB):
                link(dve.tensor_tensor(total[:, b:b + 1], total[:, b:b + 1], total[:, b - 1:b], ALU.add))
            link(dve.tensor_tensor(total, total, groups, ALU.subtract))
            dve.tensor_copy(table[0:1, 0, :], start)
            dve.tensor_copy(table[0:1, 1, :], groups)
            dve.tensor_copy(table[0:1, 2, :], total).then_inc(table_ready, 1)
            dve.wait_ge(table_ready, 1)
            dve.wait_ge(ids_ready, 1)
            with dve.Fori(0, NB) as b:
                first, groups, before = bounds(dve, b)
                with dve.Fori(0, groups) as i:
                    turn = before + i
                    slot = dve.snap((turn % 2) * GROUP)
                    chunk = first_chunk(dve, first, i)
                    dve.wait_ge(slots_free, turn + 1)
                    for j in range(GROUP):
                        dve.tensor_scalar(
                            dst_hot[0:EDGE_P, bass.ds(slot + j, 1), :], node_ids[0:EDGE_P, bass.ds(b * P, P)],
                            dst_f[:, bass.ds(chunk + j, 1)], None, ALU.is_equal)
                        last = dve.tensor_scalar(
                            src_hot[0:EDGE_P, bass.ds(slot + j, 1), :], node_ids[0:EDGE_P, :],
                            src_f[:, bass.ds(chunk + j, 1)], None, ALU.is_equal)
                    last.then_inc(hot_ready, 1)

        @block.tensor
        def _(pe):
            pe.sem_inc(slots_free, 2)
            pe.wait_ge(ids_ready, 3)
            pe.wait_ge(table_ready, 1)
            for b, u, _ in blocks_by_two(pe):
                first, groups, before = bounds(pe, b)
                pe.wait_ge(sums_free, b + 1)
                for n in range(0, NPAD, BANK):
                    w = min(BANK, NPAD - n)
                    pe.matmul(sums[u][:, n:n + w], shifted[:, AT:AT + P],
                              shifted[:, bass.ds(AT - b * P + n, w)], start=True, stop=False,
                              skip_group_check=True)
                with pe.Fori(0, groups) as i:
                    turn = before + i
                    slot = pe.snap((turn % 2) * GROUP)
                    pe.wait_ge(hot_ready, turn + 1)
                    for j in range(GROUP):
                        for n in range(0, NPAD, BANK):
                            w = min(BANK, NPAD - n)
                            last = pe.matmul(sums[u][:, n:n + w], dst_hot[0:EDGE_P, bass.ds(slot + j, 1), :],
                                             src_hot[0:EDGE_P, bass.ds(slot + j, 1), n:n + w],
                                             start=False, stop=True, skip_group_check=True)
                    last.then_inc(slots_free, 1)

        @block.scalar
        def _(act):
            act.sem_inc(sums_free, 2)
            for weight in parted:
                weight.high(act)
            act.wait_ge(table_ready, 1)
            for b, u, _ in blocks_by_two(act):
                first, groups, before = bounds(act, b)
                act.wait_ge(slots_free, before + groups + 2)
                act.wait_ge(stored[u], x_loads(b, u))
                act.activation(count_t[u][:, :], sums[u][:, 0:NPAD], ACT.Copy).then_inc(sums_free, 1)


def split_wait(eng, passed):
    eng.sem_inc(passed, 1)


def normalize(nc, dve, pool_sems, link, value, stats, out, width):
    stats_ready, root_ready, passed, count = pool_sems
    parts = width // 2 if width // 2 <= BANK else BANK
    n = width // parts
    for i in range(n):
        link(dve.bn_stats(stats[:, 8 + 6 * i:14 + 6 * i], value[:, i * parts:(i + 1) * parts]))
    split_wait(dve, passed)
    dve.bn_aggr(stats[:, 0:2], stats[:, 8:8 + 6 * n]).then_inc(stats_ready, 1)
    dve.wait_ge(root_ready, count)
    return dve.tensor_scalar(out, value, stats[:, 0:1], stats[:, 3:4], ALU.subtract, ALU.mult)


def root(nc, pool, stats, eps_half, chain):
    chain(pool.tensor_tensor(stats[:, 2:3], stats[:, 1:2], eps_half[:, 0:1], ALU.add))
    return pool.tensor_tensor(stats[:, 3:4], stats[:, 2:3], eps_half[:, 1:2], ALU.pow)


def split_products(a, b):
    if len(a) == 1:
        return [(a[0], b[0])]
    return [(a[0], b[0]), (a[0], b[1]), (a[1], b[0])]


def split_weight(nc, w, parts):
    with ExitStack() as ctx:
        sb, ps, sem = scope(nc, ctx)
        raw_w = [sb(f"raw{u}", [P, w.shape[1]], FP32) for u in (0, 1)]
        parted = PartedWeight(sem, "alone", w, [t[:, :] for t in raw_w], parts, w.shape[0] // P)
        block = ctx.enter_context(nc.Block())

        @block.sync
        def _(sp):
            parted.load(sp)
            parted.wait(sp)

        @block.scalar
        def _(act):
            parted.high(act)

        @block.vector
        def _(dve):
            parted.low(dve)


def project(nc, kt, heads, width, normalized, x, residual, weights, skips, late_skips, b_skip, a_src, a_dst, ident,
            ones, eps_half, xl, src_row, dst_col, skip):
    F, C = heads * width, kt * P
    PARTS = [(n, min(BANK, F - n)) for n in range(0, F, BANK)]
    with ExitStack() as ctx:
        sb, ps, sem = scope(nc, ctx)
        L = f"_p{heads}"
        skip_bias = sb("skip_bias" + L, [P, F], FP32)
        att = sb("att" + L, [P, 2, F], FP32)
        xt = [sb(f"xt{L}{u}", [P, C], FP32) for u in (0, 1)]
        xT = [[sb(f"xT{part}{L}{u}", [P, kt, P], FP32R) for part in (0, 1)] for u in (0, 1)]
        stats = [sb(f"stats{L}{u}", [P, 24], FP32) for u in (0, 1)]
        terms = [sb(f"terms{L}{u}", [P, 2 * heads], FP32) for u in (0, 1)]
        diag = [sb(f"diag{L}{u}", [P, heads, P], FP32) for u in (0, 1)]
        unused = sb("unused" + L, [P, 2, heads, width], BF16)
        out = [sb(f"out{L}{u}", [P, F], FP32) for u in (0, 1)]
        parted = PartedWeight(sem, "late" + L, late_skips, [t[:, :] for t in out], skips, kt) if late_skips is not None else None
        ps_t = ps("ps_t" + L, [P, 2 * BANK])
        ps_w = ps("ps_w" + L, [P, 2 * BANK])
        ps_s = ps("ps_s" + L, [P, 2 * BANK])
        ps_a = ps("ps_a" + L, [P, BANK])
        (rows_in, x_free, stats_ready, root_ready, pool_order, xn_ready, turned, high_moved, xT_moved,
         product, product_free, low_kept, skipped, skip_free, terms_done, diag_ready, row_ready, row_free,
         biased, order, passed) = (
            sem(n + L) for n in (
                "rows_in", "x_free", "stats_ready", "root_ready", "pool_order", "xn_ready", "turned",
                "high_moved", "xT_moved", "product", "product_free", "low_kept", "skipped", "skip_free",
                "terms_done", "diag_ready", "row_ready", "row_free", "biased", "order", "passed"))
        x_in, res_in, skip_out = ([sem(f"{n}{L}{u}") for u in (0, 1)] for n in ("x_in", "res_in", "skip_out"))
        block = ctx.enter_context(nc.Block())

        def rows_of(dram, b):
            return dram[bass.ds(b, 1), :, :].rearrange("b p c -> (b p) c")

        @block.sync
        def _(sp):
            for b, u, _ in blocks_by_two(sp):
                sp.wait_ge(x_free, b + 1)
                sp.dma_start(xt[u][:, :], rows_of(x, b)).then_inc(x_in[u], 16)

        @block.gpsimd
        def _(pool):
            pool.dma_start(skip_bias[:, :], b_skip.partition_broadcast(P)).then_inc(rows_in, 16)
            for i, a in enumerate((a_src, a_dst)):
                pool.dma_start(att[:, i, :], a.rearrange("h c -> (h c)").partition_broadcast(P)).then_inc(rows_in, 16)
            if parted:
                parted.load(pool)
                parted.wait(pool)
            if normalized:
                for b, u, _ in blocks_by_two(pool):
                    chain = Chain(pool, pool_order, 1, b)
                    pool.wait_ge(stats_ready, b + 1)
                    root(nc, pool, stats[u], eps_half, chain).then_inc(root_ready, 1)
                    chain.end()
            if residual is not None:
                for b, u, _ in blocks_by_two(pool):
                    pool.wait_ge(skip_out[u], x_loads(b, u))
                    pool.dma_start(out[u][:, :], rows_of(residual, b)).then_inc(res_in[u], 16)
                    pool.wait_ge(res_in[u], x_loads(b, u))
                    pool.tensor_tensor(out[u][:, :], out[u][:, :], skip_bias[:, :], ALU.add).then_inc(biased, 1)

        @block.vector
        def _(dve):
            if normalized:
                dve.sem_inc(x_free, 2)
            dve.wait_ge(rows_in, 48)

            def prepare(b, u):
                if normalized:
                    link = Chain(dve, order, 2, b)
                    dve.wait_ge(x_in[u], x_loads(b, u))
                    normalize(nc, dve, (stats_ready, root_ready, passed, b + 1), link, xt[u][:, :], stats[u],
                              xt[u][:, :], C).then_inc(xn_ready, 1)
                    link.end()
                low_part(b, u)

            def low_part(b, u):
                dve.wait_ge(high_moved, b + 1)
                dve.tensor_tensor(xT[u][1][:, :, :], ps_t[:, 0:C].rearrange("p (k c) -> p k c", k=kt),
                                  xT[u][0][:, :, :], ALU.subtract).then_inc(xT_moved, 1)

            def finish(b, u):
                dve.wait_ge(product, b + 1)
                for h in range(heads):
                    for i in (0, 1):
                        last = dve.tensor_tensor_reduce(
                            out=unused[:, i, h, :], in0=ps_w[:, h * width:(h + 1) * width],
                            in1=att[:, i, h * width:(h + 1) * width], scale=1.0, scalar=0.0, op0=ALU.mult,
                            op1=ALU.add, accum_out=terms[u][:, i * heads + h:i * heads + h + 1])
                last.then_inc(terms_done, 1)
                dve.wait_ge(terms_done, b + 1)
                dve.tensor_copy(dst_col[:, bass.ds(b, 1), :], terms[u][:, heads:2 * heads].unsqueeze(1))
                for h in range(heads):
                    last = dve.tensor_scalar(diag[u][:, h, :], ident[:, :], terms[u][:, h:h + 1], None, ALU.mult)
                last.then_inc(diag_ready, 1)
                if len(xl) == 2:
                    dve.wait_ge(low_kept, b + 1)
                    dve.tensor_tensor(xl[1][:, bass.ds(b, 1), :], ps_w[:, 0:F].unsqueeze(1),
                                      xl[0][:, bass.ds(b, 1), :], ALU.subtract).then_inc(product_free, 1)
                dve.wait_ge(skipped, b + 1)
                if residual is None:
                    dve.wait_ge(skip_out[u], x_loads(b, u))
                    dve.tensor_tensor(out[u][:, :], ps_s[:, 0:F], skip_bias[:, :], ALU.add).then_inc(skip_free, 1)
                else:
                    dve.wait_ge(biased, b + 1)
                    dve.tensor_tensor(out[u][:, :], ps_s[:, 0:F], out[u][:, :], ALU.add).then_inc(skip_free, 1)

            if parted:
                prepare(0, 0)
                parted.low(dve)
                one_ahead(dve, prepare, finish, done=1)
            else:
                one_ahead(dve, prepare, finish)

        @block.scalar
        def _(act):
            act.sem_inc(xT_moved, 1)
            act.sem_inc(product_free, 1)
            act.sem_inc(skip_free, 1)
            act.sem_inc(row_free, 1)

            def move_xT(b, u):
                act.wait_ge(turned, b + 3)
                act.activation(xT[u][0][:, :, :], ps_t[:, 0:C].rearrange("p (k c) -> p k c", k=kt), ACT.Copy).then_inc(high_moved, 1)

            def keep(b, u):
                act.wait_ge(terms_done, b + 1)
                act.activation(xl[0][:, bass.ds(b, 1), :], ps_w[:, 0:F].unsqueeze(1), ACT.Copy
                               ).then_inc(product_free if len(xl) == 1 else low_kept, 1)
                act.wait_ge(row_ready, b + 1)
                act.activation(src_row[:, :, bass.ds(b * P, P)], ps_a[:, 0:heads * P].rearrange("p (h c) -> p h c", h=heads),
                               ACT.Copy).then_inc(row_free, 1)
                act.wait_ge(skip_free, b + 2)
                act.dma_start(rows_of(skip, b), out[u][:, :]).then_inc(skip_out[u], 16)

            if parted:
                move_xT(0, 0)
                parted.high(act)
            for u in (0, 1):
                act.sem_inc(skip_out[u], 16)
            one_ahead(act, move_xT, keep, done=1 if parted else 0)
            for u in (0, 1):
                act.wait_ge(skip_out[u], 16 * (NB // 2 + 1))

        @block.tensor
        def _(pe):
            pe.sem_inc(turned, 2)

            def transposes(b, u):
                if normalized:
                    pe.wait_ge(xn_ready, b + 1)
                else:
                    pe.wait_ge(x_in[u], x_loads(b, u))
                pe.wait_ge(xT_moved, b + 1)
                for k in range(kt):
                    last = pe.transpose(ps_t[:, k * P:(k + 1) * P], xt[u][:, k * P:(k + 1) * P], ident[:, :])
                last.then_inc(turned, 1)
                pe.wait_ge(turned, b + 3)
                pe.sem_inc(x_free, 1)

            def products(b, u):
                pe.wait_ge(xT_moved, b + 2)
                for to, of, free, done in ((ps_w, weights, product_free, product), (ps_s, skips, skip_free, skipped)):
                    pe.wait_ge(free, b + 1)
                    if parted and of is skips and isinstance(b, int) and b == 0:
                        parted.wait(pe)
                    pairs = split_products(xT[u], of)
                    for n, wide in PARTS:
                        for k in range(kt):
                            for i, (left, right) in enumerate(pairs):
                                last = pe.matmul(to[:, n:n + wide], left[:, k, :], right[:, k, n:n + wide],
                                                 start=(k == 0 and i == 0), stop=(k == kt - 1 and i == len(pairs) - 1))
                    last.then_inc(done, 1)
                pe.wait_ge(diag_ready, b + 1)
                pe.wait_ge(row_free, b + 1)
                pe.matmul(ps_a[:, 0:heads * P], ones[:, :], diag[u][:, :, :].rearrange("p h c -> p (h c)"),
                          start=True, stop=True).then_inc(row_ready, 1)

            if not normalized:
                pe.sem_inc(x_free, 2)
            one_ahead(pe, transposes, products, peel=True)


def attend(nc, heads, width, relu, counts, xl, src_row, dst_col, bias, gain, shift, eps_half, ident, skip, out):
    UNITS = 2 * heads
    F = heads * width
    BANKS = -(-F // BANK)
    PER_UNIT = -(-width // BANK)
    PER_BANK = max(1, BANK // width)
    SPLIT = len(xl) == 2

    def staged(eng, steps):
        longest = max(lag for lag, _ in steps)

        def tick(turn, j, first=-longest, end=UNITS):
            for lag, step in steps:
                k = j - lag
                if first <= k < end:
                    step(turn * 2 + k // heads, k % heads, turn * UNITS + k, k % UNITS)

        peeled = -(-longest // UNITS)
        for turn in range(peeled):
            for j in range(UNITS):
                tick(turn, j, first=-turn * UNITS)
        with eng.Fori(peeled, NB // 2) as turn:
            for j in range(UNITS):
                tick(turn, j)
        for j in range(UNITS, UNITS + longest):
            tick(NB // 2 - 1, j)

    def banks_done(head):
        if heads == 1:
            return range(BANKS)
        return [head // PER_BANK] if head % PER_BANK == PER_BANK - 1 else []

    def rows_of(dram, b):
        return dram[bass.ds(b, 1), :, :].rearrange("b p c -> (b p) c")

    with ExitStack() as ctx:
        sb, ps, sem = scope(nc, ctx)
        L = f"_{heads}"
        rows = sb("rows" + L, [P, 3, F], FP32)
        bias_row, gain_row, shift_row = (rows[:, i, :] for i in range(3))
        edge_t = [sb(f"edge_t{L}{u}", [P, NPAD], U16) for u in (0, 1)]
        absent = [sb(f"absent{L}{u}", [P, NPAD], FP32) for u in range(min(2, heads))]
        present = [sb(f"present{L}{u}", [P, NPAD], FP32) for u in (0, 1)]
        steep = [sb(f"steep{L}{u}", [P, NPAD], FP32) for u in (0, 1)]
        flat = [sb(f"flat{L}{u}", [P, NPAD], FP32) for u in (0, 1)]
        weight = [sb(f"weight{L}{u}", [P, NPAD], FP32) for u in (0, 1)]
        weight_T = [[sb(f"weight_T{part}{L}{u}", [P, NB, P], FP32R if SPLIT else FP32)
                     for part in range(len(xl))] for u in (0, 1)]
        cols = [sb(f"cols{L}{u}", [P, 5], FP32) for u in (0, 1)]
        total, inverse = sb("total" + L, [P, UNITS], FP32), sb("inverse" + L, [P, UNITS], FP32)
        h = [sb(f"h{L}{u}", [P, F], FP32) for u in (0, 1)]
        skip_t = [sb(f"skip_t{L}{u}", [P, F], FP32) for u in (0, 1)]
        stats = [sb(f"stats{L}{u}", [P, 24], FP32) for u in (0, 1)]
        ps_t = [ps(f"ps_t{L}{u}", [P, 3 * BANK]) for u in (0, 1)]
        ps_o = ps("ps_o" + L, [P, 2 * BANK])

        (rows_in, absent_ready, present_ready, order_max, max_ready, steep_ready, flat_ready, larger_ready,
         weight_ready, order_total, inverse_ready, turned, high_ready, T_ready, summed, sums_free, biased,
         order_stats, passed, stats_ready, pool_order, root_ready, scaled_out, gained, shifted_out, h_free,
         h_ready) = (
            sem(n + L) for n in (
                "rows_in", "absent_ready", "present_ready", "order_max", "max_ready", "steep_ready",
                "flat_ready", "larger_ready", "weight_ready", "order_total", "inverse_ready", "turned",
                "high_ready", "T_ready", "summed", "sums_free", "biased", "order_stats", "passed",
                "stats_ready", "pool_order", "root_ready", "scaled_out", "gained", "shifted_out", "h_free",
                "h_ready"))
        skip_in = [sem(f"skip_in{L}{u}") for u in (0, 1)]
        h_out = [sem(f"h_out{L}{u}") for u in (0, 1)]
        edges_in = [sem(f"edges_in{L}{u}") for u in (0, 1)]
        block = ctx.enter_context(nc.Block())

        @block.sync
        def _(sp):
            for i, r in enumerate((bias, gain, shift)):
                sp.dma_start(rows[:, i, :], r.partition_broadcast(P)).then_inc(rows_in, 16)

            def load_edges(b, u):
                sp.dma_start(edge_t[u][:, :], rows_of(counts, b)).then_inc(edges_in[u], 16)

            def load_skip(b, u):
                sp.wait_ge(h_free, b + 1)
                sp.dma_start(skip_t[u][:, :], rows_of(skip, b)).then_inc(skip_in[u], 16)

            for b in (0, 1):
                load_edges(b, b)
            with sp.Fori(1, NB // 2) as turn:
                for u in (0, 1):
                    b = turn * 2 + u
                    sp.wait_ge(weight_ready, (b - 1) * heads + 2)
                    load_edges(b, u)
                    load_skip(b - 2, u)
            for b in (NB - 2, NB - 1):
                load_skip(b, b % 2)

        @block.gpsimd
        def _(pool):
            pool.wait_ge(rows_in, 48)

            def finish(b, u, then_bias):
                chain = Chain(pool, pool_order, 3, b)
                pool.wait_ge(stats_ready, b + 1)
                chain(root(nc, pool, stats[u], eps_half, chain))
                chain(pool.tensor_tensor(stats[u][:, 4:5], stats[u][:, 0:1], stats[u][:, 3:4], ALU.mult))
                chain.end()
                pool.tensor_tensor(stats[u][:, 5:6], stats[u][:, 4:5], eps_half[:, 2:3], ALU.mult).then_inc(root_ready, 1)
                pool.wait_ge(scaled_out, b + 1)
                pool.tensor_tensor(h[u][:, :], h[u][:, :], gain_row, ALU.mult).then_inc(gained, 1)
                pool.wait_ge(gained, b + 1)
                pool.tensor_tensor(h[u][:, :], h[u][:, :], shift_row, ALU.add).then_inc(shifted_out, 1)
                then_bias()

            def add_bias(b, u):
                pool.wait_ge(sums_free, (b + 2) * BANKS)
                pool.tensor_tensor(h[u][:, :], h[u][:, :], bias_row, ALU.add).then_inc(biased, 1)

            add_bias(0, 0)
            with pool.Fori(0, NB // 2 - 1) as turn:
                for u in (0, 1):
                    b = turn * 2 + u
                    finish(b, u, lambda: add_bias(b + 1, 1 - u))
            finish(NB - 2, 0, lambda: add_bias(NB - 1, 1))
            finish(NB - 1, 1, lambda: None)

        @block.vector
        def _(dve):
            dve.sem_inc(h_free, 2)
            dve.sem_inc(flat_ready, 2)
            dve.wait_ge(rows_in, 48)

            def term(b, head):
                return dst_col[:, bass.ds(b, 1), head:head + 1].rearrange("p b h -> p (b h)")

            def largest(b, head, unit, j):
                u, bu, c = j % 2, j // heads % 2, cols[j % 2]
                no_edge = absent[bu % len(absent)]
                if head == 0:
                    dve.wait_ge(edges_in[bu], x_loads(b, bu))
                    dve.tensor_scalar(no_edge[:, :], edge_t[bu][:, :], 0.0, ABSENT, ALU.is_equal, ALU.mult).then_inc(absent_ready, 1)
                    dve.wait_ge(absent_ready, b + 1)
                    split_wait(dve, passed)
                dve.wait_ge(flat_ready, unit + 1)
                split_wait(dve, passed)
                dve.tensor_tensor_reduce(out=present[u][:, :], in0=src_row[:, head, :], in1=no_edge[:, :],
                                         scale=1.0, scalar=2 * ABSENT, op0=ALU.add, op1=ALU.max,
                                         accum_out=c[:, 0:1]).then_inc(present_ready, 1)

            def biases(b, head, unit, j):
                c = cols[j % 2]
                dve.wait_ge(present_ready, unit + 1)
                link = Chain(dve, order_max, 2, unit)
                link(dve.scalar_tensor_tensor(out=c[:, 1:2], in0=c[:, 0:1], scalar=-1.0, in1=term(b, head),
                                              op0=ALU.mult, op1=ALU.subtract))
                link(dve.scalar_tensor_tensor(out=c[:, 2:3], in0=c[:, 1:2], scalar=SLOPE, in1=c[:, 1:2],
                                              op0=ALU.mult, op1=ALU.min))
                link.end()
                dve.tensor_tensor(c[:, 3:4], term(b, head), c[:, 2:3], ALU.add)
                dve.scalar_tensor_tensor(out=c[:, 4:5], in0=term(b, head), scalar=SLOPE, in1=c[:, 2:3],
                                         op0=ALU.mult, op1=ALU.add).then_inc(max_ready, 1)

            def larger(b, head, unit, j):
                u = j % 2
                dve.wait_ge(flat_ready, unit + 3)
                dve.tensor_tensor(flat[u][:, :], steep[u][:, :], flat[u][:, :], ALU.max).then_inc(larger_ready, 1)

            def weigh(b, head, unit, j):
                u = j % 2
                dve.wait_ge(turned, unit + 1)
                dve.wait_ge(larger_ready, unit + 1)
                dve.scalar_tensor_tensor(out=weight[u][:, :], in0=flat[u][:, :], scalar=1.0, in1=edge_t[j // heads % 2][:, :],
                                         op0=ALU.mult, op1=ALU.mult, accum_out=total[:, j:j + 1]).then_inc(weight_ready, 1)

            def invert(b, head, unit, j):
                if head != heads - 1 and head % PER_BANK != PER_BANK - 1:
                    return
                n = min(PER_BANK, heads)
                first, turn = j - n + 1, b * (heads // n) + head // n
                if heads == 1 and not (isinstance(b, int) and b == 0):
                    dve.wait_ge(sums_free, b * BANKS)
                dve.wait_ge(weight_ready, unit + 3)
                dve.tensor_scalar(inverse[:, first:j + 1], total[:, first:j + 1], 1e-16, None, ALU.add).then_inc(order_total, 1)
                dve.wait_ge(order_total, turn + 1)
                dve.reciprocal(inverse[:, first:j + 1], inverse[:, first:j + 1]).then_inc(inverse_ready, 1)

            def low_part(b, head, unit, j):
                u = j % 2
                dve.wait_ge(high_ready, unit + 1)
                dve.tensor_tensor(weight_T[u][1][:, :, :], ps_t[u][:, 0:NPAD].rearrange("p (s d) -> p s d", d=P),
                                  weight_T[u][0][:, :, :], ALU.subtract).then_inc(T_ready, 1)

            def statistics(b, head, unit, j):
                if head != heads - 1:
                    return
                bu = j // heads % 2
                dve.wait_ge(biased, b + 1)
                part = F // BANKS
                for i in range(BANKS):
                    last = dve.bn_stats(stats[bu][:, 8 + 6 * i:14 + 6 * i], h[bu][:, i * part:(i + 1) * part])
                last.then_inc(order_stats, 1)
                dve.wait_ge(order_stats, b + 1)
                split_wait(dve, passed)
                dve.bn_aggr(stats[bu][:, 0:2], stats[bu][:, 8:8 + 6 * BANKS]).then_inc(stats_ready, 1)

            def close(b, head, unit, j):
                if head != heads - 1:
                    return
                bu = j // heads % 2
                dve.wait_ge(shifted_out, b + 1)
                dve.wait_ge(skip_in[bu], x_loads(b, bu))
                if relu:
                    last = dve.scalar_tensor_tensor(out=h[bu][:, :], in0=h[bu][:, :], scalar=0.0, in1=skip_t[bu][:, :],
                                                    op0=ALU.max, op1=ALU.add)
                else:
                    last = dve.tensor_tensor(h[bu][:, :], h[bu][:, :], skip_t[bu][:, :], ALU.add)
                last.then_inc(h_ready, 1)
                dve.wait_ge(h_ready, b + 1)
                dve.sem_inc(h_free, 1)

            if heads == 1:
                staged(dve, [(0, largest), (1, larger), (0, biases), (1, weigh), (4, close), (2, invert),
                             (3, statistics)] + ([(1, low_part)] if SPLIT else []))
            else:
                staged(dve, [(0, largest), (2, larger), (0, biases), (2, weigh), (7, close), (2, invert),
                             (5, statistics)])

        @block.scalar
        def _(act):
            act.sem_inc(T_ready, 2)
            act.sem_inc(sums_free, BANKS)
            for u in (0, 1):
                act.sem_inc(h_out[u], 16)
            act.sem_inc(weight_ready, 2)

            def exponentials(b, head, unit, j):
                u = j % 2
                act.wait_ge(max_ready, unit + 1)
                act.activation(steep[u][:, :], present[u][:, :], ACT.Exp, bias=cols[u][:, 3:4]).then_inc(steep_ready, 1)
                act.wait_ge(weight_ready, unit + 1)
                act.activation(flat[u][:, :], present[u][:, :], ACT.Exp, bias=cols[u][:, 4:5], scale=SLOPE).then_inc(flat_ready, 1)

            def move_T(b, head, unit, j):
                u = j % 2
                act.wait_ge(summed, unit * PER_UNIT + PER_UNIT)
                act.wait_ge(turned, unit + 3)
                act.activation(weight_T[u][0][:, :, :], ps_t[u][:, 0:NPAD].rearrange("p (s d) -> p s d", d=P),
                               ACT.Copy).then_inc(high_ready if SPLIT else T_ready, 1)

            def take(b, head, unit, j):
                bu = j // heads % 2
                for i, bank in enumerate(banks_done(head)):
                    act.wait_ge(summed, unit * PER_UNIT + 2 * PER_UNIT + i + 1)
                    if i == 0:
                        act.wait_ge(inverse_ready, b * (heads // min(PER_BANK, heads)) + head // PER_BANK + 1)
                    if bank == 0:
                        act.wait_ge(h_out[bu], x_loads(b, bu))
                    at, end = bank * BANK, min(F, bank * BANK + BANK)
                    for n in range(at, end, min(width, end - at)):
                        wide = min(width, end - at)
                        unit_at = j - head + n // width
                        last = act.activation(h[bu][:, n:n + wide], ps_o[:, n:n + wide], ACT.Identity,
                                              scale=inverse[:, unit_at:unit_at + 1])
                    last.then_inc(sums_free, 1)

            def store(b, head, unit, j):
                if head != heads - 1:
                    return
                bu = j // heads % 2
                act.wait_ge(h_ready, b + 1)
                act.dma_start(rows_of(out, b), h[bu][:, :]).then_inc(h_out[bu], 16)

            def scale(b, head, unit, j):
                if head != heads - 1:
                    return
                bu = j // heads % 2
                act.wait_ge(root_ready, b + 1)
                act.activation(h[bu][:, :], h[bu][:, :], ACT.Identity, scale=stats[bu][:, 3:4],
                               bias=stats[bu][:, 5:6]).then_inc(scaled_out, 1)

            if heads == 1:
                staged(act, [(4, scale), (0, exponentials), (1, move_T), (4, store), (2, take)])
            else:
                staged(act, [(3, move_T), (6, scale), (0, exponentials), (4, take), (7, store)])
            for u in (0, 1):
                act.wait_ge(h_out[u], 16 * (NB // 2 + 1))

        @block.tensor
        def _(pe):
            pe.sem_inc(turned, 2)
            pe.sem_inc(summed, 2 * PER_UNIT)

            def turn_weights(b, head, unit, j):
                u = j % 2
                pe.wait_ge(weight_ready, unit + 3)
                pe.wait_ge(T_ready, unit + 1)
                for s in range(NB):
                    last = pe.transpose(ps_t[u][:, s * P:(s + 1) * P], weight[u][:, s * P:(s + 1) * P], ident[:, :])
                last.then_inc(turned, 1)

            def sum_up(b, head, unit, j):
                u = j % 2
                pe.wait_ge(T_ready, unit + 3)
                for i, n in enumerate(range(0, width, BANK)):
                    at = head * width + n
                    w = min(BANK, width - n)
                    if at % BANK == 0:
                        pe.wait_ge(sums_free, b * BANKS + at // BANK + 1)
                    pairs = split_products(weight_T[u], xl)
                    for s in range(NB):
                        for k, (of, to) in enumerate(pairs):
                            last = pe.matmul(ps_o[:, at:at + w], of[:, s, :], to[:, s, at:at + w],
                                             start=(s == 0 and k == 0), stop=(s == NB - 1 and k == len(pairs) - 1))
                    last.then_inc(summed, 1)

            lag = 1 if heads == 1 else 2
            staged(pe, [(lag, turn_weights), (lag + 1, sum_up)])


def turn_tokens(nc, x, ident, eps_half, xnT):
    with ExitStack() as ctx:
        sb, ps, sem = scope(nc, ctx)
        xt = [sb(f"xt_n{u}", [P, C_IN], FP32) for u in (0, 1)]
        xn = [sb(f"xn_n{u}", [P, C_IN], FP32) for u in (0, 1)]
        stats = [sb(f"stats_n{u}", [P, 24], FP32) for u in (0, 1)]
        ps_t = [ps(f"ps_t_n{u}", [P, 2 * BANK]) for u in (0, 1)]
        x_free, stats_ready, root_ready, pool_order, xn_ready, turned, moved, order, passed = (
            sem(n + "_n") for n in ("x_free", "stats_ready", "root_ready", "pool_order", "xn_ready",
                                    "turned", "moved", "order", "passed"))
        x_in = [sem(f"x_in_n{u}") for u in (0, 1)]
        block = ctx.enter_context(nc.Block())

        @block.sync
        def _(sp):
            for b, u, _ in blocks_by_two(sp):
                sp.wait_ge(x_free, b + 1)
                sp.dma_start(xt[u][:, :], x[bass.ds(b, 1), :, :].rearrange("b p c -> (b p) c")).then_inc(x_in[u], 16)

        @block.gpsimd
        def _(pool):
            for b, u, _ in blocks_by_two(pool):
                chain = Chain(pool, pool_order, 1, b)
                pool.wait_ge(stats_ready, b + 1)
                root(nc, pool, stats[u], eps_half, chain).then_inc(root_ready, 1)
                chain.end()

        @block.vector
        def _(dve):
            dve.sem_inc(x_free, 2)
            for b, u, _ in blocks_by_two(dve):
                link = Chain(dve, order, 2, b)
                dve.wait_ge(x_in[u], x_loads(b, u))
                dve.wait_ge(turned, b + 1)
                normalize(nc, dve, (stats_ready, root_ready, passed, b + 1), link, xt[u][:, :], stats[u],
                          xn[u][:, :], C_IN).then_inc(xn_ready, 1)
                link.end()
                dve.wait_ge(xn_ready, b + 1)
                dve.sem_inc(x_free, 1)

        @block.tensor
        def _(pe):
            pe.sem_inc(turned, 2)
            for b, u, _ in blocks_by_two(pe):
                pe.wait_ge(xn_ready, b + 1)
                pe.wait_ge(moved, b + 1)
                for k in range(KT):
                    last = pe.transpose(ps_t[u][:, k * P:(k + 1) * P], xn[u][:, k * P:(k + 1) * P], ident[:, :])
                last.then_inc(turned, 1)

        @block.scalar
        def _(act):
            act.sem_inc(moved, 2)
            for b, u, _ in blocks_by_two(act):
                act.wait_ge(turned, b + 3)
                act.activation(xnT[:, :, bass.ds(b * P, P)], ps_t[u][:, 0:C_IN].rearrange("p (k c) -> p k c", k=KT),
                               ACT.Copy).then_inc(moved, 1)


def choose_experts(nc, xnT, w1, b1, w2, b2, share):
    with ExitStack() as ctx:
        sb, ps, sem = scope(nc, ctx)
        gate_w1 = sb("gate_w1", [P, KT, GATE], FP32)
        gate_b1 = sb("gate_b1", [GATE, 1], FP32)
        gate_w2 = sb("gate_w2", [GATE, EXPERTS], FP32)
        gate_b2 = sb("gate_b2", [P, 1, EXPERTS], FP32)
        hidden = sb("gate_hidden", [GATE, NPAD], FP32)
        gate = sb("gate", [P, NB, EXPERTS], FP32)
        expd = sb("gate_exp", [P, NB, EXPERTS], FP32)
        largest, total = sb("gate_max", [P, NB, 1], FP32), sb("gate_sum", [P, NB, 1], FP32)
        keep = sb("gate_keep", [P, NB, EXPERTS], FP32)
        above = sb("gate_above", [P, 6, NB], FP32)
        ps_h = ps("ps_hidden", [GATE, 3 * BANK])
        ps_g = ps("ps_gate", [P, BANK])
        loaded, hidden_done, hidden_ready, logits_done, shifted, exp_ready, order = (
            sem(n) for n in ("gate_loaded", "hidden_done", "hidden_ready", "logits_done", "gate_shifted",
                             "gate_exp_ready", "gate_order"))
        block = ctx.enter_context(nc.Block())

        @block.sync
        def _(sp):
            sp.dma_start(gate_w1[:, :, :], w1.rearrange("(k p) n -> p k n", p=P)).then_inc(loaded, 16)
            sp.dma_start(gate_b1[:, :], b1.unsqueeze(1)).then_inc(loaded, 16)
            sp.dma_start(gate_w2[:, :], w2).then_inc(loaded, 16)
            sp.dma_start(gate_b2[:, 0, :], b2.partition_broadcast(P)).then_inc(loaded, 16)

        @block.tensor
        def _(pe):
            pe.wait_ge(loaded, 64)
            for n in range(0, NPAD, BANK):
                wide = min(BANK, NPAD - n)
                for k in range(KT):
                    last = pe.matmul(ps_h[:, n:n + wide], gate_w1[:, k, :], xnT[:, k, n:n + wide],
                                     start=(k == 0), stop=(k == KT - 1))
            last.then_inc(hidden_done, 1)
            pe.wait_ge(hidden_ready, 1)
            for b in range(NB):
                last = pe.matmul(ps_g[:, b * EXPERTS:(b + 1) * EXPERTS], hidden[:, b * P:(b + 1) * P],
                                 gate_w2[:, :], start=True, stop=True)
            last.then_inc(logits_done, 1)

        @block.scalar
        def _(act):
            act.wait_ge(hidden_done, 1)
            act.activation(hidden[:, :], ps_h[:, 0:NPAD], ACT.Relu, bias=gate_b1[:, :]).then_inc(hidden_ready, 1)
            for i in (0, 1):
                act.wait_ge(shifted, i + 1)
                act.activation(expd[:, :, :], gate[:, :, :], ACT.Exp).then_inc(exp_ready, 1)

        @block.vector
        def _(dve):
            link = Chain(dve, order)

            def of(t):
                return t[:, :, :].broadcast_to([P, NB, EXPERTS])

            dve.wait_ge(loaded, 64)
            dve.wait_ge(logits_done, 1)
            link(dve.tensor_tensor(gate[:, :, :], ps_g[:, 0:NB * EXPERTS].rearrange("p (b e) -> p b e", b=NB),
                                   of(gate_b2), ALU.add))
            link(dve.tensor_reduce(largest[:, :, :], gate[:, :, :], axis=AX.X, op=ALU.max))
            dve.tensor_tensor(gate[:, :, :], gate[:, :, :], of(largest), ALU.subtract).then_inc(shifted, 1)
            dve.wait_ge(exp_ready, 1)
            link(dve.tensor_reduce(total[:, :, :], expd[:, :, :], axis=AX.X, op=ALU.add))
            link(dve.reciprocal(total[:, :, :], total[:, :, :]))
            link(dve.tensor_tensor(gate[:, :, :], expd[:, :, :], of(total), ALU.mult))
            g = [gate[:, :, e] for e in range(EXPERTS)]
            for i, (x, y, op) in enumerate(((g[1], g[0], ALU.is_gt), (g[2], g[0], ALU.is_gt),
                                            (g[0], g[1], ALU.is_ge), (g[2], g[1], ALU.is_gt),
                                            (g[0], g[2], ALU.is_ge), (g[1], g[2], ALU.is_ge))):
                link(dve.tensor_tensor(above[:, i, :], x, y, op))
            for e in range(EXPERTS):
                link(dve.tensor_tensor(keep[:, :, e], above[:, 2 * e, :], above[:, 2 * e + 1, :], ALU.mult))
            link(dve.tensor_scalar(keep[:, :, :], keep[:, :, :], -1.0, 1.0, ALU.mult, ALU.add))
            link(dve.tensor_reduce(largest[:, :, :], gate[:, :, :], axis=AX.X, op=ALU.max))
            dve.tensor_tensor(gate[:, :, :], gate[:, :, :], of(largest), ALU.subtract).then_inc(shifted, 1)
            dve.wait_ge(exp_ready, 2)
            link(dve.tensor_tensor(keep[:, :, :], keep[:, :, :], expd[:, :, :], ALU.mult))
            link(dve.tensor_reduce(total[:, :, :], keep[:, :, :], axis=AX.X, op=ALU.add))
            link(dve.reciprocal(total[:, :, :], total[:, :, :]))
            link(dve.tensor_tensor(share[:, :, :].rearrange("p e b -> p b e"), keep[:, :, :], of(total), ALU.mult))


def run_experts(nc, xnT, wqk, bqk, wv, bv, conv_w, conv_b, share, ident, y):
    CT = HD // P
    SCALE = HD ** -0.5
    MINE = CT + CT + NB
    with ExitStack() as ctx:
        sb, ps, sem = scope(nc, ctx)
        w = sb("w_expert", [P, 3, KT, HD], FP32)
        qk_bias = sb("qk_bias", [P, 2, EXPERTS, CT], FP32)
        v_bias = sb("v_bias", [P, EXPERTS, HD], FP32)
        taps = sb("taps", [P, EXPERTS, CT, 3], FP32)
        tap_bias = sb("tap_bias", [P, EXPERTS, CT], FP32)
        raw = sb("raw_q", [P, CT, NODES + 2], FP32)
        qT, kT = sb("qT", [P, CT, NPAD], FP32), sb("kT", [P, CT, NPAD], FP32)
        v = sb("v", [P, NB, HD], FP32)
        future = sb("future", [P, P], FP32)
        prob = [sb(f"prob{u}", [P, NPAD], FP32) for u in (0, 1)]
        prob_T = [sb(f"prob_T{u}", [P, NB, P], FP32) for u in (0, 1)]
        cols = [sb(f"softmax{u}", [P, 4], FP32) for u in (0, 1)]
        ps_a, ps_b = ps("ps_scores", [P, 3 * BANK]), ps("ps_turned", [P, 3 * BANK])
        ps_y = [ps(f"ps_y{u}", [P, BANK]) for u in (0, 1)]
        (loaded, consts, w_in, projected, a_free, b_free, y_free, q_raw, q_tap, order, tap_order, q_ready, k_ready, v_ready,
         scored, masked, max_ready, prob_ready, turned, summed, taken, values_done) = (
            sem(n + "_x") for n in (
                "loaded", "consts", "w_in", "projected", "a_free", "b_free", "y_free", "q_raw", "q_tap",
                "order", "tap_order", "q_ready", "k_ready", "v_ready", "scored", "masked", "max_ready", "prob_ready",
                "turned", "summed", "taken", "values_done"))
        block = ctx.enter_context(nc.Block())

        @block.sync
        def _(sp):
            sp.dma_start(qk_bias[:, :, :, :], bqk.rearrange("(g e c p) -> p g e c", g=2, e=EXPERTS, c=CT, p=P),
                         allow_slow_non_contiguous=True).then_inc(loaded, 16)
            sp.dma_start(v_bias[:, :, :].rearrange("p e c -> p (e c)"), bv.rearrange("e c -> (e c)").partition_broadcast(P)).then_inc(loaded, 16)
            sp.dma_start(taps[:, 0, :, :], conv_w.rearrange("(c p) o t -> p c (o t)", p=P)).then_inc(loaded, 16)
            sp.dma_start(tap_bias[:, 0, :], conv_b.rearrange("(c p) -> p c", p=P),
                         allow_slow_non_contiguous=True).then_inc(loaded, 16)
            with sp.Fori(0, EXPERTS) as e:
                sp.wait_ge(values_done, e + 1)
                for g in (0, 1):
                    sp.dma_start(w[:, g, :, :], wqk.rearrange("(k p) (g e c) -> g p k e c", p=P, g=2, e=EXPERTS)
                                 [g, :, :, bass.ds(e, 1), :].rearrange("p k e c -> p k (e c)")).then_inc(w_in, 16)
                sp.dma_start(w[:, 2, :, :], wv.rearrange("e (k p) c -> p k e c", p=P)
                             [:, :, bass.ds(e, 1), :].rearrange("p k e c -> p k (e c)")).then_inc(w_in, 16)

        @block.gpsimd
        def _(pool):
            pool.memset(taps[:, 1:EXPERTS, :, 0:1], 0.0)
            pool.memset(taps[:, 1:EXPERTS, :, 1:2], 1.0)
            pool.memset(taps[:, 1:EXPERTS, :, 2:3], 0.0)
            pool.memset(tap_bias[:, 1:EXPERTS, :], 0.0)
            pool.memset(raw[:, :, 0:1], 0.0)
            pool.memset(raw[:, :, NODES + 1:NODES + 2], 0.0)
            pool.memset(qT[:, :, NODES:NPAD], 0.0)
            pool.memset(future[:, :], 0.0).then_inc(consts, 1)
            pool.wait_ge(consts, 1)
            pool.affine_select(out=future[:, :], in_=future[:, :], compare_op=ALU.is_ge, fill=ABSENT, base=0,
                               pattern=[[-1, P]], channel_multiplier=1).then_inc(consts, 1)

        @block.tensor
        def _(pe):
            pe.sem_inc(y_free, 2)
            pe.sem_inc(values_done, 1)
            pe.wait_ge(consts, 2)
            with pe.Fori(0, EXPERTS) as e:
                pe.wait_ge(w_in, (e + 1) * 48)
                for i in range(2 * CT):
                    g, c = divmod(i, CT)
                    to = (ps_a, ps_b)[i % 2]
                    if i % 2 == 0:
                        pe.wait_ge(a_free, e * (NB + CT) + i // 2 + 1)
                    else:
                        pe.wait_ge(b_free, e * (NB + CT) + i // 2 + 1)
                    for n in range(0, NPAD, BANK):
                        wide = min(BANK, NPAD - n)
                        for k in range(KT):
                            last = pe.matmul(to[:, n:n + wide], w[:, g, k, c * P:(c + 1) * P],
                                             xnT[:, k, n:n + wide], start=(k == 0), stop=(k == KT - 1))
                    last.then_inc(projected, 1)
                for b in range(NB):
                    pe.wait_ge(y_free, e * 2 * NB + b + 1)
                    for k in range(KT):
                        last = pe.matmul(ps_y[b % 2][:, 0:HD], xnT[:, k, b * P:(b + 1) * P], w[:, 2, k, :],
                                         start=(k == 0), stop=(k == KT - 1))
                    last.then_inc(projected, 1)
                pe.wait_ge(projected, (e + 1) * MINE)
                pe.sem_inc(values_done, 1)

                def score(i):
                    pe.wait_ge(a_free, e * (NB + CT) + CT + i + 1)
                    for n in range(0, (i + 1) * P, BANK):
                        wide = min(BANK, (i + 1) * P - n)
                        for c in range(CT):
                            last = pe.matmul(ps_a[:, n:n + wide], qT[:, c, i * P:(i + 1) * P], kT[:, c, n:n + wide],
                                             start=(c == 0), stop=(c == CT - 1))
                    last.then_inc(scored, 1)

                def turn(i):
                    pe.wait_ge(prob_ready, e * NB + i + 1)
                    pe.wait_ge(b_free, e * (NB + CT) + CT + i + 1)
                    for s in range(i + 1):
                        last = pe.transpose(ps_b[:, s * P:(s + 1) * P], prob[i % 2][:, s * P:(s + 1) * P], ident[:, :])
                    last.then_inc(turned, 1)

                def average(i):
                    pe.wait_ge(b_free, e * (NB + CT) + CT + i + 2)
                    pe.wait_ge(v_ready, e * NB + i + 1)
                    pe.wait_ge(y_free, e * 2 * NB + NB + i + 1)
                    for s in range(i + 1):
                        last = pe.matmul(ps_y[i % 2][:, 0:HD], prob_T[i % 2][:, s, :], v[:, s, :],
                                         start=(s == 0), stop=(s == i))
                    last.then_inc(summed, 1)

                pe.wait_ge(q_ready, (e + 1) * CT)
                pe.wait_ge(b_free, e * (NB + CT) + CT + 1)
                score(0)
                for i in range(1, NB):
                    turn(i - 1)
                    score(i)
                    average(i - 1)
                turn(NB - 1)
                average(NB - 1)

        @block.scalar
        def _(act):
            act.sem_inc(a_free, 1)
            act.sem_inc(b_free, 1)
            act.wait_ge(loaded, 64)
            act.wait_ge(consts, 2)
            with act.Fori(0, EXPERTS) as e:
                for i in range(2 * CT):
                    g, c = divmod(i, CT)
                    of, free = ((ps_a, a_free), (ps_b, b_free))[i % 2]
                    bias = qk_bias[:, g, bass.ds(e, 1), c:c + 1].rearrange("p e c -> p (e c)")
                    act.wait_ge(projected, e * MINE + i + 1)
                    if g == 0:
                        act.activation(raw[:, c, 1:NODES + 1], of[:, 0:NODES], ACT.Identity, bias=bias).then_inc(free, 1)
                        act.wait_ge(free, e * (NB + CT) + 2)
                        act.activation(qT[:, c, 0:NODES], raw[:, c, 0:NODES], ACT.Identity,
                                       scale=taps[:, bass.ds(e, 1), c, 0:1].rearrange("p e t -> p (e t)"),
                                       bias=tap_bias[:, bass.ds(e, 1), c:c + 1].rearrange("p e c -> p (e c)")
                                       ).then_inc(q_tap, 1)
                    else:
                        act.activation(kT[:, c, :], of[:, 0:NPAD], ACT.Identity, bias=bias).then_inc(free, 1)
                for i in range(NB):
                    wide = (i + 1) * P
                    act.wait_ge(max_ready, e * NB + i + 1)
                    act.activation(prob[i % 2][:, 0:wide], ps_a[:, 0:wide], ACT.Exp, scale=SCALE,
                                   bias=cols[i % 2][:, 1:2], accum_out=cols[i % 2][:, 2:3]).then_inc(prob_ready, 1)
                    act.wait_ge(prob_ready, e * NB + i + 1)
                    act.sem_inc(a_free, 1)
                    act.wait_ge(turned, e * NB + i + 1)
                    act.activation(prob_T[i % 2][:, 0:i + 1, :], ps_b[:, 0:wide].rearrange("p (s t) -> p s t", t=P),
                                   ACT.Copy).then_inc(b_free, 1)

        @block.vector
        def _(dve):
            dve.wait_ge(loaded, 64)
            dve.wait_ge(consts, 2)
            with dve.Fori(0, EXPERTS) as e:
                for c in range(CT):
                    dve.wait_ge(q_tap, e * CT + c + 1)
                    for t in (1, 2):
                        last = dve.scalar_tensor_tensor(
                            out=qT[:, c, 0:NODES], in0=raw[:, c, t:t + NODES],
                            scalar=taps[:, bass.ds(e, 1), c, t:t + 1].rearrange("p e t -> p (e t)"),
                            in1=qT[:, c, 0:NODES], op0=ALU.mult, op1=ALU.add)
                        last.then_inc(tap_order, 1)
                        dve.wait_ge(tap_order, e * 2 * CT + 2 * c + t)
                    dve.sem_inc(q_ready, 1)
                for b in range(NB):
                    dve.wait_ge(projected, e * MINE + 2 * CT + b + 1)
                    dve.tensor_tensor(v[:, b, :], ps_y[b % 2][:, 0:HD],
                                      v_bias[:, bass.ds(e, 1), :].rearrange("p e c -> p (e c)"), ALU.add).then_inc(v_ready, 1)
                    dve.wait_ge(v_ready, e * NB + b + 1)
                    dve.sem_inc(y_free, 1)

                def softmax_max(i):
                    c = cols[i % 2]
                    dve.wait_ge(scored, e * NB + i + 1)
                    dve.tensor_tensor(ps_a[:, i * P:(i + 1) * P], ps_a[:, i * P:(i + 1) * P], future[:, :],
                                      ALU.add).then_inc(masked, 1)
                    dve.wait_ge(masked, e * NB + i + 1)
                    dve.tensor_reduce(c[:, 0:1], ps_a[:, 0:(i + 1) * P], axis=AX.X, op=ALU.max).then_inc(order, 1)
                    dve.wait_ge(order, e * 3 * NB + LINKS[i][0])
                    dve.tensor_scalar(c[:, 1:2], c[:, 0:1], -SCALE, None, ALU.mult).then_inc(max_ready, 1)

                def take(i):
                    c = cols[i % 2]
                    dve.wait_ge(summed, e * NB + i + 1)
                    dve.reciprocal(c[:, 3:4], c[:, 2:3]).then_inc(order, 1)
                    dve.wait_ge(order, e * 3 * NB + LINKS[i][1])
                    dve.tensor_tensor(c[:, 3:4], c[:, 3:4], share[:, bass.ds(e, 1), i:i + 1].rearrange("p e b -> p (e b)"),
                                      ALU.mult).then_inc(order, 1)
                    dve.wait_ge(order, e * 3 * NB + LINKS[i][1] + 1)
                    dve.tensor_scalar(y[:, i, bass.ds(e * HD, HD)], ps_y[i % 2][:, 0:HD], c[:, 3:4], None,
                                      ALU.mult).then_inc(taken, 1)
                    dve.wait_ge(taken, e * NB + i + 1)
                    dve.sem_inc(y_free, 1)

                LINKS = [(1 if i == 0 else 3 * i - 1, 3 * i + 3 if i < NB - 1 else 3 * NB - 1) for i in range(NB)]
                softmax_max(0)
                for i in range(1, NB):
                    softmax_max(i)
                    take(i - 1)
                take(NB - 1)


def project_out(nc, y, w, bias, x, ident, out):
    PARTS = [(n, min(BANK, C_IN - n)) for n in range(0, C_IN, BANK)]
    with ExitStack() as ctx:
        sb, ps, sem = scope(nc, ctx)
        weights = sb("out_weights", [P, KT, C_IN], FP32)
        bias_row = sb("out_bias", [P, C_IN], FP32)
        yt = [sb(f"yt{u}", [P, C_IN], FP32) for u in (0, 1)]
        yT = [sb(f"yT{u}", [P, KT, P], FP32) for u in (0, 1)]
        xt = [sb(f"xt_o{u}", [P, C_IN], FP32) for u in (0, 1)]
        out_t = [sb(f"out_t{u}", [P, C_IN], FP32) for u in (0, 1)]
        ps_t, ps_o = ps("ps_t_o", [P, 2 * BANK]), [ps(f"ps_o_o{u}", [P, 2 * BANK]) for u in (0, 1)]
        loaded, y_ready, turned, moved, product, taken, out_ready = (
            sem(n + "_o") for n in ("loaded", "y_ready", "turned", "moved", "product", "taken", "out_ready"))
        x_in, stored = ([sem(f"{n}_o{u}") for u in (0, 1)] for n in ("x_in", "stored"))
        block = ctx.enter_context(nc.Block())

        def rows_of(dram, b):
            return dram[bass.ds(b, 1), :, :].rearrange("b p c -> (b p) c")

        @block.sync
        def _(sp):
            sp.dma_start(weights[:, :, :], w.rearrange("(k p) n -> p k n", p=P)).then_inc(loaded, 16)
            sp.dma_start(bias_row[:, :], bias.partition_broadcast(P)).then_inc(loaded, 16)
            for u in (0, 1):
                sp.sem_inc(stored[u], 16)
            for b, u, _ in blocks_by_two(sp):
                sp.wait_ge(out_ready, b + 1)
                sp.dma_start(xt[u][:, :], rows_of(x, b)).then_inc(x_in[u], 16)

        @block.gpsimd
        def _(pool):
            for b, u, _ in blocks_by_two(pool):
                pool.wait_ge(turned, b + 1)
                pool.tensor_copy(yt[u][:, :], y[:, bass.ds(b, 1), :].rearrange("p b c -> p (b c)")).then_inc(y_ready, 1)

        @block.tensor
        def _(pe):
            pe.sem_inc(turned, 2)

            def transposes(b, u):
                pe.wait_ge(y_ready, b + 1)
                pe.wait_ge(moved, b + 1)
                for k in range(KT):
                    last = pe.transpose(ps_t[:, k * P:(k + 1) * P], yt[u][:, k * P:(k + 1) * P], ident[:, :])
                last.then_inc(turned, 1)

            def products(b, u):
                pe.wait_ge(moved, b + 2)
                pe.wait_ge(taken, b + 1)
                for n, wide in PARTS:
                    for k in range(KT):
                        last = pe.matmul(ps_o[u][:, n:n + wide], yT[u][:, k, :], weights[:, k, n:n + wide],
                                         start=(k == 0), stop=(k == KT - 1))
                last.then_inc(product, 1)

            pe.wait_ge(loaded, 32)
            one_ahead(pe, transposes, products)

        @block.scalar
        def _(act):
            act.sem_inc(moved, 1)
            act.sem_inc(product, 2)

            def move_yT(b, u):
                act.wait_ge(turned, b + 3)
                act.wait_ge(product, b + 1)
                act.activation(yT[u][:, :, :], ps_t[:, 0:C_IN].rearrange("p (k c) -> p k c", k=KT), ACT.Copy).then_inc(moved, 1)

            def store(b, u):
                act.wait_ge(out_ready, b + 3)
                act.dma_start(rows_of(out, b), out_t[u][:, :]).then_inc(stored[u], 16)

            one_ahead(act, move_yT, store)
            for u in (0, 1):
                act.wait_ge(stored[u], 16 * (NB // 2 + 1))

        @block.vector
        def _(dve):
            dve.sem_inc(taken, 2)
            dve.sem_inc(out_ready, 2)
            dve.wait_ge(loaded, 32)
            for b, u, _ in blocks_by_two(dve):
                dve.wait_ge(stored[u], x_loads(b, u))
                dve.wait_ge(product, b + 3)
                dve.tensor_tensor(out_t[u][:, :], ps_o[u][:, 0:C_IN], bias_row[:, :], ALU.add).then_inc(taken, 1)
                dve.wait_ge(taken, b + 3)
                dve.wait_ge(x_in[u], x_loads(b, u))
                dve.tensor_tensor(out_t[u][:, :], out_t[u][:, :], xt[u][:, :], ALU.add).then_inc(out_ready, 1)




def gnn_then_experts(nc, x, src, dst, W1, a_src1, a_dst1, b1, g1, be1, Wr1, br1, W2, a_src2, a_dst2, b2, g2, be2,
                     Wr2, br2, Wqk, bqk, Wv, bv, conv_w, conv_b, Wg1, bg1, Wg2, bg2, Wp, bp, out):
    def blocks(dram):
        return dram.rearrange("(b p) c -> b p c", p=P)

    x, out = blocks(x), blocks(out)
    skip1, h1, skip2, x2 = (blocks(nc.dram_tensor(name, [NPAD, c], FP32).ap()) for name, c in (
        ("skip1", HC), ("h1", HC), ("skip2", C_IN), ("x2", C_IN)))
    with ExitStack() as ctx:
        sb, _, sem = scope(nc, ctx)
        ident, ones, eps_half = sb("ident", [P, P], FP32), sb("ones", [P, P], FP32), sb("eps_half", [P, 3], FP32)
        cleared = sem("cleared")
        with nc.Block() as block:
            @block.gpsimd
            def _(pool):
                pool.memset(ident[:, :], 0.0).then_inc(cleared, 1)
                pool.memset(ones[:, :], 1.0)
                pool.memset(eps_half[:, 0:1], LN_EPS)
                pool.memset(eps_half[:, 1:2], -0.5)
                pool.memset(eps_half[:, 2:3], -1.0)
                pool.wait_ge(cleared, 1)
                pool.affine_select(out=ident[:, :], in_=ident[:, :], compare_op=ALU.not_equal, fill=1.0, base=0,
                                   pattern=[[-1, P]], channel_multiplier=1)

        counts = nc.dram_tensor("counts", [NB, P, NPAD], U16).ap()
        with ExitStack() as graph:
            g_sb, _, _ = scope(nc, graph)
            shared = [g_sb(f"weight_{part}", [P, KT * HC], FP32R) for part in ("high", "low")]
            for (layer, kt, heads, width, feats, residual, w, a_src, a_dst, bias, gain, shift, w_skip, b_skip, skip,
                 result) in (
                    (1, KT, HEADS, HID, x, None, W1, a_src1, a_dst1, b1, g1, be1, Wr1, br1, skip1, h1),
                    (2, HKT, 1, C_IN, h1, x, W2, a_src2, a_dst2, b2, g2, be2, Wr2, br2, skip2, x2)):
                F = heads * width
                weights = [t[:, :].rearrange("p (k n) -> p k n", k=kt) for t in shared]
                with ExitStack() as one:
                    l_sb, _, _ = scope(nc, one)
                    xl = ([l_sb("xl1", [P, NB, F], FP32)] if layer == 1 else
                          [l_sb(f"xl2_{part}", [P, NB, F], FP32R) for part in ("high", "low")])
                    src_row = l_sb(f"src_row{layer}", [P, heads, NPAD], FP32)
                    dst_col = l_sb(f"dst_col{layer}", [P, NB, heads], FP32)
                    with ExitStack() as skip_weights:
                        s_sb, _, _ = scope(nc, skip_weights)
                        skips = [s_sb(f"skips{layer}_{part}", [P, kt, F], FP32R) for part in ("high", "low")]
                        if layer == 1:
                            count_edges(nc, src, dst, counts, [(w, weights), (w_skip, skips)],
                                        [xl[0][:, u, :] for u in (0, 1)])
                        else:
                            split_weight(nc, w, weights)
                        project(nc, kt, heads, width, layer == 1, feats, residual, weights, skips,
                                None if layer == 1 else w_skip, b_skip, a_src, a_dst, ident, ones, eps_half,
                                xl, src_row, dst_col, skip)
                    attend(nc, heads, width, layer == 1, counts, xl, src_row, dst_col, bias, gain, shift,
                           eps_half, ident, skip, result)

        xnT = sb("xnT", [P, KT, NPAD], FP32)
        share = sb("share", [P, EXPERTS, NB], FP32)
        y = sb("y", [P, NB, C_IN], FP32)
        turn_tokens(nc, x2, ident, eps_half, xnT)
        choose_experts(nc, xnT, Wg1, bg1, Wg2, bg2, share)
        run_experts(nc, xnT, Wqk, bqk, Wv, bv, conv_w, conv_b, share, ident, y)
        project_out(nc, y, Wp, bp, x2, ident, out)


_INS = (["x", "src", "dst"] + ["L0_gnn_" + n for n in (
    "W1", "a_src1", "a_dst1", "b1", "g1", "be1", "Wr1", "br1", "W2", "a_src2", "a_dst2", "b2", "g2", "be2", "Wr2",
    "br2")] + ["L0_ffn_" + n for n in ("Wqk", "bqk", "Wv", "bv", "conv_w", "conv_b", "Wg1", "bg1", "Wg2", "bg2",
                                       "Wp", "bp")])


def kernel(**inputs):
    import numpy as np
    import concourse.bacc as bacc
    from concourse.bass_utils import run_bass_kernel_spmd

    nc = bacc.Bacc("TRN2", target_bir_lowering=False, num_devices=1)
    arrays, args = {}, []
    for name in _INS:
        a = np.ascontiguousarray(inputs[name])
        if name == "x":
            a = np.pad(a, ((0, NPAD - NODES), (0, 0)))
        elif name in ("src", "dst"):
            a = np.ascontiguousarray(a.reshape(CHUNKS, EDGE_P).T)
        arrays[f"in_{name}"] = a
        args.append(nc.dram_tensor(f"in_{name}", a.shape, mybir.dt.from_np(a.dtype), kind="ExternalInput").ap())
    args.append(nc.dram_tensor("out_0", (NPAD, C_IN), FP32, kind="ExternalOutput").ap())
    gnn_then_experts(nc, *args)
    r = run_bass_kernel_spmd(nc, [arrays], core_ids=[0])
    return r.results[0]["out_0"][:NODES]
```

```python
import concourse.bass as bass
from concourse import mybir
from contextlib import ExitStack

FP32 = mybir.dt.float32
FP32R = mybir.dt.float32r
FP16 = mybir.dt.float16
BF16 = mybir.dt.bfloat16
I32 = mybir.dt.int32
U16 = mybir.dt.uint16
ALU = mybir.AluOpType
ACT = mybir.ActivationFunctionType
AX = mybir.AxisListType

NODES, C_IN = 1250, 768
P = 128
NB = 10
NPAD = NB * P
KT = C_IN // P
HEADS, HID = 4, 256
HC = HEADS * HID
HKT = HC // P
EDGES = 40000
GROUP = 5
GROUPS = -(-EDGES // (P * GROUP))
CHUNKS = GROUPS * GROUP
DIGIT = 64
SLOTS = 3
EXPERTS, HD = 3, 256
GATE = 32
LN_EPS = 1e-5
SLOPE = 0.2
ABSENT = -1.0e30
BANK = 512


class Chain:

    def __init__(self, eng, sem, links=0, turn=0):
        self.eng, self.sem, self.links, self.turn, self.n = eng, sem, links, turn, 0

    def __call__(self, instruction):
        instruction.then_inc(self.sem, 1)
        self.n += 1
        self.eng.wait_ge(self.sem, self.turn * self.links + self.n)

    def end(self):
        assert self.n == self.links, self.n


def scope(nc, ctx):
    sems = []

    def clear():
        if sems:
            with nc.Block() as block:
                @block.gpsimd
                def _(pool):
                    nc.clear_and_free_semaphores(sems)

    ctx.callback(clear)

    def sb(name, shape, dt):
        return ctx.enter_context(nc.sbuf_tensor(name, shape, dt))

    def ps(name, shape, dt=FP32):
        return ctx.enter_context(nc.psum_tensor(name, shape, dt))

    def sem(name):
        sems.append(nc.alloc_semaphore(name))
        return sems[-1]

    return sb, ps, sem


def blocks_by_two(eng):
    with eng.Fori(0, NB // 2) as turn:
        for u in (0, 1):
            yield turn * 2 + u, u, turn


def x_loads(b, u):
    return (b - u) * 8 + 16


def one_ahead(eng, early, late, done=0, peel=False):
    if not done:
        early(0, 0)
    if peel:
        for b in (0, 1):
            early(b + 1, 1 - b)
            late(b, b)
    with eng.Fori(1 if peel else 0, NB // 2 - 1) as turn:
        early(turn * 2 + 1, 1)
        late(turn * 2, 0)
        early(turn * 2 + 2, 0)
        late(turn * 2 + 1, 1)
    early(NB - 1, 1)
    late(NB - 2, 0)
    late(NB - 1, 1)


class PartedWeight:

    def __init__(self, sem, name, w, buffers, parts, kt):
        self.tiles = w.rearrange("(k p) n -> k p n", p=P)
        self.buffers, self.parts, self.kt = buffers, parts, kt
        self.loaded = [sem(f"{name}_loaded{u}") for u in (0, 1)]
        self.high_done, self.split = sem(name + "_high_done"), sem(name + "_split")

    def each(self, eng, step):
        with eng.Fori(0, self.kt // 2) as turn:
            for u in (0, 1):
                step(eng, turn * 2 + u, u)

    def load_tile(self, eng, k, u):
        eng.wait_ge(self.split, k + 1)
        eng.dma_start(self.buffers[u], self.tiles[bass.ds(k, 1), :, :].rearrange("k p n -> (k p) n")
                      ).then_inc(self.loaded[u], 16)

    def high_tile(self, act, k, u):
        act.wait_ge(self.loaded[u], x_loads(k, u))
        act.activation(self.parts[0][:, bass.ds(k, 1), :], self.buffers[u].unsqueeze(1), ACT.Copy
                       ).then_inc(self.high_done, 1)

    def low_tile(self, eng, k, u):
        eng.wait_ge(self.high_done, k + 1)
        eng.tensor_tensor(self.parts[1][:, bass.ds(k, 1), :], self.buffers[u].unsqueeze(1),
                          self.parts[0][:, bass.ds(k, 1), :], ALU.subtract).then_inc(self.split, 1)

    def load(self, eng):
        eng.sem_inc(self.split, 2)
        self.each(eng, self.load_tile)

    def high(self, act):
        self.each(act, self.high_tile)

    def low(self, eng):
        self.each(eng, self.low_tile)

    def wait(self, pe):
        pe.wait_ge(self.split, self.kt + 2)


def count_edges(nc, src, dst, counts, w, w_parts):
    with ExitStack() as ctx:
        sb, ps, sem = scope(nc, ctx)
        src_i, dst_i = sb("src_i", [P, CHUNKS], I32), sb("dst_i", [P, CHUNKS], I32)
        src_f, dst_f = sb("src_f", [P, CHUNKS], FP32), sb("dst_f", [P, CHUNKS], FP32)
        block_i, block_f = sb("block_i", [P, CHUNKS], I32), sb("block_f", [P, CHUNKS], BF16)
        span, span_all = sb("span", [P, 2, GROUPS], FP32), sb("span_all", [P, 2, GROUPS], FP32)
        block_ids = sb("block_ids", [1, NB, GROUPS], FP32)
        upward, downward = sb("upward", [1, NB, GROUPS], FP32), sb("downward", [1, NB, GROUPS], FP32)
        above, member = sb("above", [1, NB, GROUPS], FP32), sb("member", [1, NB, GROUPS], FP32)
        node_ids = sb("node_ids", [P, NPAD], FP16)
        row = sb("row", [1, 4, NB], FP32)
        table = sb("table", [1, NB], I32)
        shifted = sb("shifted", [P, NPAD + (NB - 1) * P], BF16)
        AT = (NB - 1) * P
        src_hot = sb("src_hot", [P, SLOTS * GROUP, NPAD], BF16)
        dst_hot = sb("dst_hot", [P, SLOTS * GROUP, P], BF16)
        minus_dst, one = sb("minus_dst", [P, CHUNKS], FP32), sb("one", [P, 1], FP32)
        distance = sb("distance", [P, SLOTS * GROUP, P], BF16)
        count_t = [sb(f"count_t{u}", [P, NPAD], U16) for u in (0, 1)]
        raw_w = [sb(f"raw_w{u}", [P, w.shape[1]], FP32)[:, :] for u in (0, 1)]
        parted = PartedWeight(sem, "weight", w, raw_w, w_parts, w.shape[0] // P)
        sums = [ps(f"sums{u}", [P, 3 * BANK]) for u in (0, 1)]
        stored = [sem(f"stored{u}") for u in (0, 1)]
        edges_in, consts, ids_ready = sem("edges_in"), sem("consts"), sem("ids_ready")
        span_ready, span_reduced, table_ready = sem("span_ready"), sem("span_reduced"), sem("table_ready")
        hot_ready, slots_free = sem("hot_ready"), sem("slots_free")
        distance_ready, dst_ready, minus_ready = sem("distance_ready"), sem("dst_ready"), sem("minus_ready")
        sums_free, order = sem("sums_free"), sem("order0")
        block = ctx.enter_context(nc.Block())

        def bounds(eng, b):
            entry = eng.value_load(table[0:1, bass.ds(b, 1)], min_val=0, max_val=NB * GROUPS * DIGIT ** 2 - 1)
            return [nc.s_assert_within(eng.snap(digit), 0, most,
                                       skip_runtime_bounds_check_because="the table is made of such digits")
                    for digit, most in ((entry % DIGIT, GROUPS - 1), (entry // DIGIT % DIGIT, GROUPS),
                                        (entry // DIGIT ** 2, GROUPS * (NB - 1)))]

        def first_chunk(eng, first, i):
            return nc.s_assert_within(
                eng.snap((first + i) * GROUP), 0, CHUNKS - GROUP,
                skip_runtime_bounds_check_because="the table's ends lie within the groups")

        @block.sync
        def _(sp):
            sp.dma_start(src_i[:, :], src).then_inc(edges_in, 16)
            sp.dma_start(dst_i[:, :], dst).then_inc(edges_in, 16)
            parted.load(sp)
            for u in (0, 1):
                sp.sem_inc(stored[u], 16)
            for b, u, _ in blocks_by_two(sp):
                sp.wait_ge(sums_free, b + 3)
                sp.dma_start(counts[bass.ds(b, 1), :, :].rearrange("b p s -> (b p) s"), count_t[u][:, :]
                             ).then_inc(stored[u], 16)
            for u in (0, 1):
                sp.wait_ge(stored[u], 16 * (NB // 2 + 1))

        @block.gpsimd
        def _(pool):
            pool.iota(upward[:, :, :], pattern=[[0, NB], [1, GROUPS]], base=1, channel_multiplier=0,
                      allow_small_or_imprecise_dtypes=True).then_inc(consts, 1)
            pool.iota(downward[:, :, :], pattern=[[0, NB], [-1, GROUPS]], base=GROUPS,
                      channel_multiplier=0, allow_small_or_imprecise_dtypes=True).then_inc(consts, 1)
            pool.iota(block_ids[:, :, :], pattern=[[1, NB], [0, GROUPS]], base=0, channel_multiplier=0,
                      allow_small_or_imprecise_dtypes=True).then_inc(consts, 1)
            pool.iota(node_ids[:, :], pattern=[[1, NPAD]], base=0, channel_multiplier=0,
                      allow_small_or_imprecise_dtypes=True).then_inc(ids_ready, 1)
            pool.memset(one[:, :], 1.0)
            pool.memset(shifted[:, :], 0.0).then_inc(ids_ready, 1)
            pool.wait_ge(ids_ready, 2)
            pool.affine_select(out=shifted[:, AT:AT + P], in_=shifted[:, AT:AT + P],
                               compare_op=ALU.not_equal, fill=1.0, base=0, pattern=[[-1, P]],
                               channel_multiplier=1).then_inc(ids_ready, 1)
            pool.wait_ge(span_ready, 2)
            pool.partition_all_reduce(span_all[:, :, :].rearrange("p i g -> p (i g)"),
                                      span[:, :, :].rearrange("p i g -> p (i g)"), P,
                                      bass.bass_isa.ReduceOp.max).then_inc(span_reduced, 1)
            parted.low(pool)

        @block.vector
        def _(dve):
            link = Chain(dve, order)
            dve.wait_ge(edges_in, 32)
            link(dve.tensor_copy(src_f[:, :], src_i[:, :]))
            dve.tensor_copy(dst_f[:, :], dst_i[:, :])
            dve.tensor_scalar(minus_dst[:, :], dst_i[:, :], -1.0, None, ALU.mult).then_inc(minus_ready, 1)
            link(dve.tensor_single_scalar(block_i[:, :], dst_i[:, :], 7, ALU.arith_shift_right))
            link(dve.tensor_copy(block_f[:, :], block_i[:, :]))
            by_group = block_f[:, :].rearrange("p (g c) -> p g c", c=GROUP)
            dve.tensor_reduce(span[:, 0, :], by_group, axis=AX.X, op=ALU.max).then_inc(span_ready, 1)
            link(dve.tensor_reduce(span[:, 1, :], by_group, axis=AX.X, op=ALU.min))
            dve.tensor_scalar(span[:, 1, :], span[:, 1, :], -1.0, None, ALU.mult).then_inc(span_ready, 1)
            dve.wait_ge(consts, 3)
            dve.wait_ge(span_reduced, 1)
            highest, lowest = (span_all[0:1, i:i + 1, :].broadcast_to([1, NB, GROUPS]) for i in (0, 1))
            link(dve.tensor_tensor(member[:, :, :], lowest, block_ids[:, :, :], ALU.add))
            link(dve.tensor_scalar(member[:, :, :], member[:, :, :], 0.0, None, ALU.is_ge))
            link(dve.tensor_tensor(above[:, :, :], highest, block_ids[:, :, :], ALU.is_ge))
            link(dve.tensor_tensor(member[:, :, :], member[:, :, :], above[:, :, :], ALU.mult))
            for i, number in enumerate((upward, downward)):
                link(dve.tensor_tensor(above[:, :, :], member[:, :, :], number[:, :, :], ALU.mult))
                link(dve.tensor_reduce(row[0:1, i, :], above[:, :, :], axis=AX.X, op=ALU.max))
            end, start, groups, total = (row[0:1, i, :] for i in range(4))
            link(dve.tensor_scalar(end, end, 1.0, None, ALU.max))
            link(dve.tensor_scalar(start, start, -1.0, float(GROUPS), ALU.mult, ALU.add))
            link(dve.scalar_tensor_tensor(out=start, in0=end, scalar=-1.0, in1=start, op0=ALU.add, op1=ALU.min))
            link(dve.tensor_tensor(groups, end, start, ALU.subtract))
            link(dve.tensor_copy(total, groups))
            for b in range(1, NB):
                link(dve.tensor_tensor(total[:, b:b + 1], total[:, b:b + 1], total[:, b - 1:b], ALU.add))
            link(dve.tensor_tensor(total, total, groups, ALU.subtract))
            link(dve.scalar_tensor_tensor(out=groups, in0=total, scalar=float(DIGIT), in1=groups, op0=ALU.mult, op1=ALU.add))
            dve.scalar_tensor_tensor(out=table[:, :], in0=groups, scalar=float(DIGIT), in1=start, op0=ALU.mult,
                                     op1=ALU.add).then_inc(table_ready, 1)
            dve.wait_ge(table_ready, 1)
            dve.wait_ge(ids_ready, 1)
            with dve.Fori(0, NB) as b:
                first, groups, before = bounds(dve, b)
                with dve.Fori(0, groups) as i:
                    turn = before + i
                    slot = dve.snap((turn % SLOTS) * GROUP)
                    chunk = first_chunk(dve, first, i)
                    dve.wait_ge(slots_free, turn + 1)
                    dve.tensor_scalar(
                        dst_hot[:, bass.ds(slot + GROUP - 1, 1), :], node_ids[:, bass.ds(b * P, P)],
                        dst_f[:, bass.ds(chunk + GROUP - 1, 1)], None, ALU.is_equal)
                    for j in range(GROUP):
                        if j == GROUP - 1:
                            dve.wait_ge(dst_ready, turn + 1)
                        last = dve.tensor_scalar(
                            src_hot[:, bass.ds(slot + j, 1), :], node_ids[:, :],
                            src_f[:, bass.ds(chunk + j, 1)], None, ALU.is_equal)
                    last.then_inc(hot_ready, 1)

        @block.tensor
        def _(pe):
            pe.sem_inc(slots_free, SLOTS)
            pe.wait_ge(ids_ready, 3)
            pe.wait_ge(table_ready, 1)
            for b, u, _ in blocks_by_two(pe):
                _, groups, before = bounds(pe, b)
                pe.wait_ge(sums_free, b + 1)
                for n in range(0, NPAD, BANK):
                    w = min(BANK, NPAD - n)
                    pe.matmul(sums[u][:, n:n + w], shifted[:, AT:AT + P],
                              shifted[:, bass.ds(AT - b * P + n, w)], start=True, stop=False,
                              skip_group_check=True)
                with pe.Fori(0, groups) as i:
                    turn = before + i
                    slot = pe.snap((turn % SLOTS) * GROUP)
                    pe.wait_ge(hot_ready, turn + 1)
                    for j in range(GROUP):
                        for n in range(0, NPAD, BANK):
                            w = min(BANK, NPAD - n)
                            last = pe.matmul(sums[u][:, n:n + w], dst_hot[:, bass.ds(slot + j, 1), :],
                                             src_hot[:, bass.ds(slot + j, 1), n:n + w],
                                             start=False, stop=True, skip_group_check=True)
                    last.then_inc(slots_free, 1)

        @block.scalar
        def _(act):
            act.sem_inc(sums_free, 2)
            parted.high(act)
            act.wait_ge(table_ready, 1)
            act.wait_ge(minus_ready, 1)
            act.wait_ge(ids_ready, 3)

            def destinations(b, u):
                first, groups, before = bounds(act, b)
                with act.Fori(0, groups) as i:
                    turn = before + i
                    slot = act.snap((turn % SLOTS) * GROUP)
                    chunk = first_chunk(act, first, i)
                    act.wait_ge(slots_free, turn + 1)
                    for j in range(GROUP - 1):
                        last = act.activation(
                            distance[:, bass.ds(slot + j, 1), :], node_ids[:, bass.ds(b * P, P)].unsqueeze(1),
                            ACT.Square, bias=minus_dst[:, bass.ds(chunk + j, 1)])
                    last.then_inc(distance_ready, 1)
                    act.wait_ge(distance_ready, turn + 1)
                    act.activation(dst_hot[:, bass.ds(slot, GROUP - 1), :], distance[:, bass.ds(slot, GROUP - 1), :],
                                   ACT.Relu, bias=one[:, :], scale=-1.0).then_inc(dst_ready, 1)

                return before, before + groups

            def take(b, u, groups_done):
                act.wait_ge(slots_free, groups_done + SLOTS)
                act.wait_ge(stored[u], x_loads(b, u))
                act.activation(count_t[u][:, :], sums[u][:, 0:NPAD], ACT.Copy).then_inc(sums_free, 1)

            destinations(0, 0)
            with act.Fori(0, NB // 2 - 1) as turn:
                for u in (0, 1):
                    before, _ = destinations(turn * 2 + u + 1, 1 - u)
                    take(turn * 2 + u, u, before)
            before, after = destinations(NB - 1, 1)
            take(NB - 2, 0, before)
            take(NB - 1, 1, after)


def split_wait(eng, passed):
    eng.sem_inc(passed, 1)


def normalize(nc, dve, pool_sems, link, value, stats, out, width):
    stats_ready, root_ready, passed, count = pool_sems
    parts = width // 2 if width // 2 <= BANK else BANK
    n = width // parts
    for i in range(n):
        link(dve.bn_stats(stats[:, 8 + 6 * i:14 + 6 * i], value[:, i * parts:(i + 1) * parts]))
    split_wait(dve, passed)
    dve.bn_aggr(stats[:, 0:2], stats[:, 8:8 + 6 * n]).then_inc(stats_ready, 1)
    dve.wait_ge(root_ready, count)
    return dve.tensor_scalar(out, value, stats[:, 0:1], stats[:, 3:4], ALU.subtract, ALU.mult)


def root(nc, pool, stats, eps_half, chain):
    chain(pool.tensor_tensor(stats[:, 2:3], stats[:, 1:2], eps_half[:, 0:1], ALU.add))
    return pool.tensor_tensor(stats[:, 3:4], stats[:, 2:3], eps_half[:, 1:2], ALU.pow)


def split_products(a, b):
    if len(a) == 1:
        return [(a[0], b[0])]
    return [(a[0], b[0]), (a[0], b[1]), (a[1], b[0])]


def project(nc, kt, heads, width, normalized, x, residual, weights, skips, w_skip, b_skip, a_src, a_dst, ident,
            ones, eps_half, xl, src_row, dst_col, skip):
    F, C = heads * width, kt * P
    PARTS = [(n, min(BANK, F - n)) for n in range(0, F, BANK)]
    with ExitStack() as ctx:
        sb, ps, sem = scope(nc, ctx)
        L = f"_p{heads}"
        skip_bias = sb("skip_bias" + L, [P, F], FP32)
        att = sb("att" + L, [P, 2, F], FP32)
        xt = [sb(f"xt{L}{u}", [P, C], FP32) for u in (0, 1)]
        xT = [[sb(f"xT{part}{L}{u}", [P, kt, P], FP32R) for part in (0, 1)] for u in (0, 1)]
        stats = [sb(f"stats{L}{u}", [P, 24], FP32) for u in (0, 1)]
        terms = [sb(f"terms{L}{u}", [P, 2 * heads], FP32) for u in (0, 1)]
        diag = [sb(f"diag{L}{u}", [P, heads, P], FP32) for u in (0, 1)]
        unused = sb("unused" + L, [P, 2, heads, width], BF16)
        out = [sb(f"out{L}{u}", [P, F], FP32) for u in (0, 1)]
        parted = PartedWeight(sem, "skips" + L, w_skip, [t[:, :] for t in out], skips, kt)
        ps_t = ps("ps_t" + L, [P, 2 * BANK])
        ps_w = ps("ps_w" + L, [P, 2 * BANK])
        ps_s = ps("ps_s" + L, [P, 2 * BANK])
        ps_a = ps("ps_a" + L, [P, BANK])
        (rows_in, x_free, stats_ready, root_ready, pool_order, xn_ready, turned, high_moved, xT_moved,
         product, product_free, low_kept, skipped, skip_free, terms_done, diag_ready, row_ready, row_free,
         biased, order, passed) = (
            sem(n + L) for n in (
                "rows_in", "x_free", "stats_ready", "root_ready", "pool_order", "xn_ready", "turned",
                "high_moved", "xT_moved", "product", "product_free", "low_kept", "skipped", "skip_free",
                "terms_done", "diag_ready", "row_ready", "row_free", "biased", "order", "passed"))
        x_in, res_in, skip_out = ([sem(f"{n}{L}{u}") for u in (0, 1)] for n in ("x_in", "res_in", "skip_out"))
        block = ctx.enter_context(nc.Block())

        def rows_of(dram, b):
            return dram[bass.ds(b, 1), :, :].rearrange("b p c -> (b p) c")

        @block.sync
        def _(sp):
            def load_rows(b, u):
                sp.wait_ge(x_free, b + 1)
                sp.dma_start(xt[u][:, :], rows_of(x, b)).then_inc(x_in[u], 16)

            for b in (0, 1):
                load_rows(b, b)
            parted.load(sp)
            with sp.Fori(1, NB // 2) as turn:
                for u in (0, 1):
                    load_rows(turn * 2 + u, u)

        @block.gpsimd
        def _(pool):
            pool.dma_start(skip_bias[:, :], b_skip.partition_broadcast(P)).then_inc(rows_in, 16)
            for i, a in enumerate((a_src, a_dst)):
                pool.dma_start(att[:, i, :], a.rearrange("h c -> (h c)").partition_broadcast(P)).then_inc(rows_in, 16)
            if normalized:
                for b, u, _ in blocks_by_two(pool):
                    chain = Chain(pool, pool_order, 1, b)
                    pool.wait_ge(stats_ready, b + 1)
                    root(nc, pool, stats[u], eps_half, chain).then_inc(root_ready, 1)
                    chain.end()
            if residual is not None:
                parted.wait(pool)
                for b, u, _ in blocks_by_two(pool):
                    pool.wait_ge(skip_out[u], x_loads(b, u))
                    pool.dma_start(out[u][:, :], rows_of(residual, b)).then_inc(res_in[u], 16)
                    pool.wait_ge(res_in[u], x_loads(b, u))
                    pool.tensor_tensor(out[u][:, :], out[u][:, :], skip_bias[:, :], ALU.add).then_inc(biased, 1)

        @block.vector
        def _(dve):
            if normalized:
                dve.sem_inc(x_free, 2)
            dve.wait_ge(rows_in, 48)

            def norm(b, u):
                if normalized:
                    link = Chain(dve, order, 2, b)
                    dve.wait_ge(x_in[u], x_loads(b, u))
                    normalize(nc, dve, (stats_ready, root_ready, passed, b + 1), link, xt[u][:, :], stats[u],
                              xt[u][:, :], C).then_inc(xn_ready, 1)
                    link.end()

            def low_part(b, u):
                dve.wait_ge(high_moved, b + 1)
                dve.tensor_tensor(xT[u][1][:, :, :], ps_t[:, 0:C].rearrange("p (k c) -> p k c", k=kt),
                                  xT[u][0][:, :, :], ALU.subtract).then_inc(xT_moved, 1)

            def finish(b, u):
                dve.wait_ge(product, b + 1)
                for h in range(heads):
                    for i in (0, 1):
                        last = dve.tensor_tensor_reduce(
                            out=unused[:, i, h, :], in0=ps_w[:, h * width:(h + 1) * width],
                            in1=att[:, i, h * width:(h + 1) * width], scale=1.0, scalar=0.0, op0=ALU.mult,
                            op1=ALU.add, accum_out=terms[u][:, i * heads + h:i * heads + h + 1])
                last.then_inc(terms_done, 1)
                dve.wait_ge(terms_done, b + 1)
                dve.tensor_copy(dst_col[:, bass.ds(b, 1), :], terms[u][:, heads:2 * heads].unsqueeze(1))
                for h in range(heads):
                    last = dve.tensor_scalar(diag[u][:, h, :], ident[:, :], terms[u][:, h:h + 1], None, ALU.mult)
                last.then_inc(diag_ready, 1)
                if len(xl) == 2:
                    dve.wait_ge(low_kept, b + 1)
                    dve.tensor_tensor(xl[1][:, bass.ds(b, 1), :], ps_w[:, 0:F].unsqueeze(1),
                                      xl[0][:, bass.ds(b, 1), :], ALU.subtract).then_inc(product_free, 1)
                dve.wait_ge(skipped, b + 1)
                if residual is None:
                    dve.wait_ge(skip_out[u], x_loads(b, u))
                    dve.tensor_tensor(out[u][:, :], ps_s[:, 0:F], skip_bias[:, :], ALU.add).then_inc(skip_free, 1)
                else:
                    dve.wait_ge(biased, b + 1)
                    dve.tensor_tensor(out[u][:, :], ps_s[:, 0:F], out[u][:, :], ALU.add).then_inc(skip_free, 1)

            norm(0, 0)
            norm(1, 1)
            low_part(0, 0)
            parted.low(dve)
            with dve.Fori(0, NB // 2 - 1) as turn:
                for u in (0, 1):
                    b = turn * 2 + u
                    low_part(b + 1, 1 - u)
                    norm(b + 2, u)
                    finish(b, u)
            low_part(NB - 1, 1)
            finish(NB - 2, 0)
            finish(NB - 1, 1)

        @block.scalar
        def _(act):
            act.sem_inc(xT_moved, 1)
            act.sem_inc(product_free, 1)
            act.sem_inc(skip_free, 1)
            act.sem_inc(row_free, 1)

            def move_xT(b, u):
                act.wait_ge(turned, b + 3)
                act.activation(xT[u][0][:, :, :], ps_t[:, 0:C].rearrange("p (k c) -> p k c", k=kt), ACT.Copy).then_inc(high_moved, 1)

            def keep(b, u):
                act.wait_ge(terms_done, b + 1)
                act.activation(xl[0][:, bass.ds(b, 1), :], ps_w[:, 0:F].unsqueeze(1), ACT.Copy
                               ).then_inc(product_free if len(xl) == 1 else low_kept, 1)
                act.wait_ge(row_ready, b + 1)
                act.activation(src_row[:, :, bass.ds(b * P, P)], ps_a[:, 0:heads * P].rearrange("p (h c) -> p h c", h=heads),
                               ACT.Copy).then_inc(row_free, 1)
                act.wait_ge(skip_free, b + 2)
                act.dma_start(rows_of(skip, b), out[u][:, :]).then_inc(skip_out[u], 16)

            move_xT(0, 0)
            parted.high(act)
            for u in (0, 1):
                act.sem_inc(skip_out[u], 16)
            one_ahead(act, move_xT, keep, done=1)
            for u in (0, 1):
                act.wait_ge(skip_out[u], 16 * (NB // 2 + 1))

        @block.tensor
        def _(pe):
            pe.sem_inc(turned, 2)

            def transposes(b, u):
                if normalized:
                    pe.wait_ge(xn_ready, b + 1)
                else:
                    pe.wait_ge(x_in[u], x_loads(b, u))
                pe.wait_ge(xT_moved, b + 1)
                for k in range(kt):
                    last = pe.transpose(ps_t[:, k * P:(k + 1) * P], xt[u][:, k * P:(k + 1) * P], ident[:, :])
                last.then_inc(turned, 1)
                pe.wait_ge(turned, b + 3)
                pe.sem_inc(x_free, 1)

            def products(b, u):
                pe.wait_ge(xT_moved, b + 2)
                for to, of, free, done in ((ps_w, weights, product_free, product), (ps_s, skips, skip_free, skipped)):
                    pe.wait_ge(free, b + 1)
                    if of is skips and isinstance(b, int) and b == 0:
                        parted.wait(pe)
                    pairs = split_products(xT[u], of)
                    for n, wide in PARTS:
                        for k in range(kt):
                            for i, (left, right) in enumerate(pairs):
                                last = pe.matmul(to[:, n:n + wide], left[:, k, :], right[:, k, n:n + wide],
                                                 start=(k == 0 and i == 0), stop=(k == kt - 1 and i == len(pairs) - 1))
                    last.then_inc(done, 1)
                pe.wait_ge(diag_ready, b + 1)
                pe.wait_ge(row_free, b + 1)
                pe.matmul(ps_a[:, 0:heads * P], ones[:, :], diag[u][:, :, :].rearrange("p h c -> p (h c)"),
                          start=True, stop=True).then_inc(row_ready, 1)

            if not normalized:
                pe.sem_inc(x_free, 2)
            one_ahead(pe, transposes, products, peel=True)


def attend(nc, heads, width, relu, counts, xl, src_row, dst_col, bias, gain, shift, eps_half, ident, skip, out,
           next_weight=None, next_parts=None):
    UNITS = 2 * heads
    F = heads * width
    BANKS = -(-F // BANK)
    PER_UNIT = -(-width // BANK)
    PER_BANK = max(1, BANK // width)
    SPLIT = len(xl) == 2

    def staged(eng, steps):
        longest = max(lag for lag, _ in steps)

        def tick(turn, j, first=-longest, end=UNITS):
            for lag, step in steps:
                k = j - lag
                if first <= k < end:
                    step(turn * 2 + k // heads, k % heads, turn * UNITS + k, k % UNITS)

        peeled = -(-longest // UNITS)
        for turn in range(peeled):
            for j in range(UNITS):
                tick(turn, j, first=-turn * UNITS)
        with eng.Fori(peeled, NB // 2) as turn:
            for j in range(UNITS):
                tick(turn, j)
        for j in range(UNITS, UNITS + longest):
            tick(NB // 2 - 1, j)

    def banks_done(head):
        if heads == 1:
            return range(BANKS)
        return [head // PER_BANK] if head % PER_BANK == PER_BANK - 1 else []

    def rows_of(dram, b):
        return dram[bass.ds(b, 1), :, :].rearrange("b p c -> (b p) c")

    with ExitStack() as ctx:
        sb, ps, sem = scope(nc, ctx)
        L = f"_{heads}"
        rows = sb("rows" + L, [P, 3, F], FP32)
        bias_row, gain_row, shift_row = (rows[:, i, :] for i in range(3))
        edge_t = [sb(f"edge_t{L}{u}", [P, NPAD], U16) for u in (0, 1)]
        absent = sb("absent" + L, [P, NPAD], FP32)
        present = [sb(f"present{L}{u}", [P, NPAD], FP32) for u in (0, 1)]
        steep = [sb(f"steep{L}{u}", [P, NPAD], FP32) for u in (0, 1)]
        flat = [sb(f"flat{L}{u}", [P, NPAD], FP32) for u in (0, 1)]
        weight = [sb(f"weight{L}{u}", [P, NPAD], FP32) for u in (0, 1)]
        weight_T = [[sb(f"weight_T{part}{L}{u}", [P, NB, P], FP32R if SPLIT else FP32)
                     for part in range(len(xl))] for u in (0, 1)]
        cols = [sb(f"cols{L}{u}", [P, 5], FP32) for u in (0, 1)]
        total, inverse = sb("total" + L, [P, UNITS], FP32), sb("inverse" + L, [P, UNITS], FP32)
        h = [sb(f"h{L}{u}", [P, F], FP32) for u in (0, 1)]
        skip_t = [sb(f"skip_t{L}{u}", [P, F], FP32) for u in (0, 1)]
        stats = [sb(f"stats{L}{u}", [P, 24], FP32) for u in (0, 1)]
        ps_t = [ps(f"ps_t{L}{u}", [P, 3 * BANK]) for u in (0, 1)]
        ps_o = ps("ps_o" + L, [P, 2 * BANK])

        (rows_in, absent_ready, present_ready, order_max, max_ready, steep_ready, flat_ready, larger_ready,
         weight_ready, order_total, inverse_ready, turned, high_ready, T_ready, summed, sums_free, biased,
         order_stats, passed, stats_ready, pool_order, root_ready, scaled_out, gained, shifted_out, h_free,
         h_ready) = (
            sem(n + L) for n in (
                "rows_in", "absent_ready", "present_ready", "order_max", "max_ready", "steep_ready",
                "flat_ready", "larger_ready", "weight_ready", "order_total", "inverse_ready", "turned",
                "high_ready", "T_ready", "summed", "sums_free", "biased", "order_stats", "passed",
                "stats_ready", "pool_order", "root_ready", "scaled_out", "gained", "shifted_out", "h_free",
                "h_ready"))
        skip_in = [sem(f"skip_in{L}{u}") for u in (0, 1)]
        h_out = [sem(f"h_out{L}{u}") for u in (0, 1)]
        edges_in = [sem(f"edges_in{L}{u}") for u in (0, 1)]
        parted = None
        if next_weight is not None:
            assert next_weight.shape[0] // P == NB - 2
            raw_w = [sb(f"raw_next{u}", [P, next_weight.shape[1]], FP32)[:, :] for u in (0, 1)]
            parted = PartedWeight(sem, "next_weight", next_weight, raw_w, next_parts, NB - 2)
        block = ctx.enter_context(nc.Block())

        @block.sync
        def _(sp):

            def load_edges(b, u):
                sp.dma_start(edge_t[u][:, :], rows_of(counts, b)).then_inc(edges_in[u], 16)

            def load_skip(b, u):
                sp.wait_ge(h_free, b + 1)
                sp.dma_start(skip_t[u][:, :], rows_of(skip, b)).then_inc(skip_in[u], 16)

            for b in (0, 1):
                load_edges(b, b)
            for i, r in enumerate((bias, gain, shift)):
                sp.dma_start(rows[:, i, :], r.partition_broadcast(P)).then_inc(rows_in, 16)
            if parted:
                sp.sem_inc(parted.split, 2)
            with sp.Fori(1, NB // 2) as turn:
                for u in (0, 1):
                    b = turn * 2 + u
                    sp.wait_ge(weight_ready, (b - 1) * heads + 2)
                    load_edges(b, u)
                    load_skip(b - 2, u)
                    if parted:
                        parted.load_tile(sp, b - 2, u)
            for b in (NB - 2, NB - 1):
                load_skip(b, b % 2)

        @block.gpsimd
        def _(pool):
            pool.wait_ge(rows_in, 48)

            def finish(b, u, then_bias):
                if not relu:
                    chain = Chain(pool, pool_order, 1, b)
                    pool.wait_ge(stats_ready, b + 1)
                    root(nc, pool, stats[u], eps_half, chain).then_inc(root_ready, 1)
                    chain.end()
                    pool.wait_ge(skip_in[u], x_loads(b, u))
                    pool.tensor_tensor(skip_t[u][:, :], skip_t[u][:, :], shift_row, ALU.add).then_inc(shifted_out, 1)
                    then_bias()
                    return
                chain = Chain(pool, pool_order, 3, b)
                pool.wait_ge(stats_ready, b + 1)
                chain(root(nc, pool, stats[u], eps_half, chain))
                chain(pool.tensor_tensor(stats[u][:, 4:5], stats[u][:, 0:1], stats[u][:, 3:4], ALU.mult))
                chain.end()
                pool.tensor_tensor(stats[u][:, 5:6], stats[u][:, 4:5], eps_half[:, 2:3], ALU.mult).then_inc(root_ready, 1)
                pool.wait_ge(scaled_out, b + 1)
                pool.tensor_tensor(h[u][:, :], h[u][:, :], gain_row, ALU.mult).then_inc(gained, 1)
                pool.wait_ge(gained, b + 1)
                pool.tensor_tensor(h[u][:, :], h[u][:, :], shift_row, ALU.add).then_inc(shifted_out, 1)
                then_bias()

            def add_bias(b, u):
                pool.wait_ge(sums_free, (b + 2) * BANKS)
                pool.tensor_tensor(h[u][:, :], h[u][:, :], bias_row, ALU.add).then_inc(biased, 1)

            add_bias(0, 0)
            with pool.Fori(0, NB // 2 - 1) as turn:
                for u in (0, 1):
                    b = turn * 2 + u
                    finish(b, u, lambda: add_bias(b + 1, 1 - u))
                    if parted:
                        parted.low_tile(pool, b, u)
            finish(NB - 2, 0, lambda: add_bias(NB - 1, 1))
            finish(NB - 1, 1, lambda: None)

        @block.vector
        def _(dve):
            dve.sem_inc(h_free, 2)

            def term(b, head):
                return dst_col[:, bass.ds(b, 1), head:head + 1].rearrange("p b h -> p (b h)")

            def largest(b, head, unit, j):
                u, bu, c = j % 2, j // heads % 2, cols[j % 2]
                if head == 0:
                    dve.wait_ge(edges_in[bu], x_loads(b, bu))
                    dve.tensor_scalar(absent[:, :], edge_t[bu][:, :], 0.0, ABSENT, ALU.is_equal, ALU.mult).then_inc(absent_ready, 1)
                    dve.wait_ge(absent_ready, b + 1)
                    split_wait(dve, passed)
                dve.tensor_tensor_reduce(out=present[u][:, :], in0=src_row[:, head, :], in1=absent[:, :],
                                         scale=1.0, scalar=2 * ABSENT, op0=ALU.add, op1=ALU.max,
                                         accum_out=c[:, 0:1]).then_inc(present_ready, 1)

            def minus_sum(b, head, unit, j):
                c = cols[j % 2]
                dve.wait_ge(present_ready, unit + 1)
                dve.scalar_tensor_tensor(out=c[:, 1:2], in0=c[:, 0:1], scalar=-1.0, in1=term(b, head),
                                         op0=ALU.mult, op1=ALU.subtract).then_inc(order_max, 1)

            def minus_leaky(b, head, unit, j):
                c = cols[j % 2]
                dve.wait_ge(order_max, unit * 2 + 1)
                dve.scalar_tensor_tensor(out=c[:, 2:3], in0=c[:, 1:2], scalar=SLOPE, in1=c[:, 1:2],
                                         op0=ALU.mult, op1=ALU.min).then_inc(order_max, 1)

            def biases(b, head, unit, j):
                c = cols[j % 2]
                dve.wait_ge(order_max, unit * 2 + 2)
                dve.tensor_tensor(c[:, 3:4], term(b, head), c[:, 2:3], ALU.add)
                dve.scalar_tensor_tensor(out=c[:, 4:5], in0=term(b, head), scalar=SLOPE, in1=c[:, 2:3],
                                         op0=ALU.mult, op1=ALU.add).then_inc(max_ready, 1)

            def larger(b, head, unit, j):
                u = j % 2
                dve.wait_ge(flat_ready, unit + 1)
                dve.tensor_tensor(flat[u][:, :], steep[u][:, :], flat[u][:, :], ALU.max).then_inc(larger_ready, 1)

            def weigh(b, head, unit, j):
                u = j % 2
                dve.wait_ge(turned, unit + 1)
                dve.wait_ge(larger_ready, unit + 1)
                dve.scalar_tensor_tensor(out=weight[u][:, :], in0=flat[u][:, :], scalar=1.0, in1=edge_t[j // heads % 2][:, :],
                                         op0=ALU.mult, op1=ALU.mult, accum_out=total[:, j:j + 1]).then_inc(weight_ready, 1)

            def invert(b, head, unit, j):
                if head != heads - 1 and head % PER_BANK != PER_BANK - 1:
                    return
                n = min(PER_BANK, heads)
                first, turn = j - n + 1, b * (heads // n) + head // n
                if heads == 1 and not (isinstance(b, int) and b == 0):
                    dve.wait_ge(sums_free, b * BANKS)
                dve.wait_ge(weight_ready, unit + 3)
                dve.tensor_scalar(inverse[:, first:j + 1], total[:, first:j + 1], 1e-16, None, ALU.add).then_inc(order_total, 1)
                dve.wait_ge(order_total, turn + 1)
                dve.reciprocal(inverse[:, first:j + 1], inverse[:, first:j + 1]).then_inc(inverse_ready, 1)

            def low_part(b, head, unit, j):
                u = j % 2
                dve.wait_ge(high_ready, unit + 1)
                dve.tensor_tensor(weight_T[u][1][:, :, :], ps_t[u][:, 0:NPAD].rearrange("p (s d) -> p s d", d=P),
                                  weight_T[u][0][:, :, :], ALU.subtract).then_inc(T_ready, 1)

            def statistics(b, head, unit, j):
                if head != heads - 1:
                    return
                bu = j // heads % 2
                dve.wait_ge(biased, b + 1)
                part = F // BANKS
                for i in range(BANKS):
                    last = dve.bn_stats(stats[bu][:, 8 + 6 * i:14 + 6 * i], h[bu][:, i * part:(i + 1) * part])
                last.then_inc(order_stats, 1)
                dve.wait_ge(order_stats, b + 1)
                split_wait(dve, passed)
                dve.bn_aggr(stats[bu][:, 0:2], stats[bu][:, 8:8 + 6 * BANKS]).then_inc(stats_ready, 1)

            def close(b, head, unit, j):
                if head != heads - 1:
                    return
                bu = j // heads % 2
                dve.wait_ge(shifted_out, b + 1)
                if relu:
                    dve.wait_ge(skip_in[bu], x_loads(b, bu))
                    last = dve.scalar_tensor_tensor(out=h[bu][:, :], in0=h[bu][:, :], scalar=0.0, in1=skip_t[bu][:, :],
                                                    op0=ALU.max, op1=ALU.add)
                else:
                    dve.wait_ge(gained, b + 1)
                    last = dve.scalar_tensor_tensor(out=h[bu][:, :], in0=h[bu][:, :], scalar=stats[bu][:, 3:4],
                                                    in1=skip_t[bu][:, :], op0=ALU.mult, op1=ALU.add)
                last.then_inc(h_ready, 1)
                dve.wait_ge(h_ready, b + 1)
                dve.sem_inc(h_free, 1)

            def gain_up(b, head, unit, j):
                dve.wait_ge(rows_in, 48)
                dve.wait_ge(root_ready, b + 1)
                bu = j // heads % 2
                dve.scalar_tensor_tensor(out=h[bu][:, :], in0=h[bu][:, :], scalar=stats[bu][:, 0:1],
                                         in1=gain_row, op0=ALU.subtract, op1=ALU.mult).then_inc(gained, 1)

            if relu:
                staged(dve, [(1, biases), (2, larger), (0, largest), (2, weigh), (0, minus_sum), (7, close),
                             (2, invert), (5, statistics), (0, minus_leaky)])
            else:
                staged(dve, ([(2, low_part)] if SPLIT else []) + [
                    (0, largest), (1, larger), (0, minus_sum), (0, minus_leaky), (0, biases), (1, weigh), (4, gain_up), (2, invert), (4, close),
                    (3, statistics)])

        @block.scalar
        def _(act):
            act.sem_inc(T_ready, 2)
            act.sem_inc(sums_free, BANKS)
            for u in (0, 1):
                act.sem_inc(h_out[u], 16)
            act.sem_inc(weight_ready, 2)

            def exponentials(b, head, unit, j):
                u = j % 2
                act.wait_ge(max_ready, unit + 1)
                act.activation(steep[u][:, :], present[u][:, :], ACT.Exp, bias=cols[u][:, 3:4]).then_inc(steep_ready, 1)
                act.wait_ge(weight_ready, unit + 1)
                act.activation(flat[u][:, :], present[u][:, :], ACT.Exp, bias=cols[u][:, 4:5], scale=SLOPE).then_inc(flat_ready, 1)

            def high_weight(b, head, unit, j):
                if parted and head == 1 and not isinstance(b, int):
                    parted.high_tile(act, b - 2, j // heads % 2)

            def move_T(b, head, unit, j):
                u = j % 2
                act.wait_ge(summed, unit * PER_UNIT + PER_UNIT)
                act.wait_ge(turned, unit + 3)
                act.activation(weight_T[u][0][:, :, :], ps_t[u][:, 0:NPAD].rearrange("p (s d) -> p s d", d=P),
                               ACT.Copy).then_inc(high_ready if SPLIT else T_ready, 1)

            def take(b, head, unit, j):
                bu = j // heads % 2
                for i, bank in enumerate(banks_done(head)):
                    act.wait_ge(summed, unit * PER_UNIT + 2 * PER_UNIT + i + 1)
                    if i == 0:
                        act.wait_ge(inverse_ready, b * (heads // min(PER_BANK, heads)) + head // PER_BANK + 1)
                    if bank == 0:
                        act.wait_ge(h_out[bu], x_loads(b, bu))
                    at, end = bank * BANK, min(F, bank * BANK + BANK)
                    for n in range(at, end, min(width, end - at)):
                        wide = min(width, end - at)
                        unit_at = j - head + n // width
                        last = act.activation(h[bu][:, n:n + wide], ps_o[:, n:n + wide], ACT.Identity,
                                              scale=inverse[:, unit_at:unit_at + 1])
                    last.then_inc(sums_free, 1)

            def store(b, head, unit, j):
                if head != heads - 1:
                    return
                bu = j // heads % 2
                act.wait_ge(h_ready, b + 1)
                act.dma_start(rows_of(out, b), h[bu][:, :]).then_inc(h_out[bu], 16)

            def scale(b, head, unit, j):
                if head != heads - 1:
                    return
                bu = j // heads % 2
                act.wait_ge(root_ready, b + 1)
                act.activation(h[bu][:, :], h[bu][:, :], ACT.Identity, scale=stats[bu][:, 3:4],
                               bias=stats[bu][:, 5:6]).then_inc(scaled_out, 1)

            if heads == 1:
                staged(act, [(0, exponentials), (1, move_T), (4, store), (2, take)])
            else:
                staged(act, [(3, move_T), (6, scale), (1, exponentials), (4, take), (7, store),
                             (0, high_weight)])
            for u in (0, 1):
                act.wait_ge(h_out[u], 16 * (NB // 2 + 1))

        @block.tensor
        def _(pe):
            pe.sem_inc(turned, 2)
            pe.sem_inc(summed, 2 * PER_UNIT)

            def turn_weights(b, head, unit, j):
                u = j % 2
                pe.wait_ge(weight_ready, unit + 3)
                pe.wait_ge(T_ready, unit + 1)
                for s in range(NB):
                    last = pe.transpose(ps_t[u][:, s * P:(s + 1) * P], weight[u][:, s * P:(s + 1) * P], ident[:, :])
                last.then_inc(turned, 1)

            def sum_up(b, head, unit, j):
                u = j % 2
                pe.wait_ge(T_ready, unit + 3)
                for i, n in enumerate(range(0, width, BANK)):
                    at = head * width + n
                    w = min(BANK, width - n)
                    if at % BANK == 0:
                        pe.wait_ge(sums_free, b * BANKS + at // BANK + 1)
                    pairs = split_products(weight_T[u], xl)
                    for s in range(NB):
                        for k, (of, to) in enumerate(pairs):
                            last = pe.matmul(ps_o[:, at:at + w], of[:, s, :], to[:, s, at:at + w],
                                             start=(s == 0 and k == 0), stop=(s == NB - 1 and k == len(pairs) - 1))
                    last.then_inc(summed, 1)

            lag = 1 if heads == 1 else 2
            staged(pe, [(lag, turn_weights), (lag + 1, sum_up)])


class ThirdsOfWeights:

    def __init__(self, sem, name, buffers, parts):
        self.buffers, self.parts = buffers, parts
        self.loaded = [sem(f"{name}_loaded{u}") for u in (0, 1)]
        self.high_done, self.split = sem(name + "_high_done"), sem(name + "_split")

    def start(self, sp):
        sp.sem_inc(self.split, 2)

    def load(self, sp, turn, sources):
        for g in range(3):
            sp.wait_ge(self.split, turn * 3 + (2, 1, 3)[g])
            sp.dma_start(self.buffers[g % 2], sources[g]).then_inc(self.loaded[g % 2], 16)

    def high(self, act, turn, g):
        act.wait_ge(self.loaded[g % 2], 16 * (turn + 1 if g == 1 else turn * 2 + 1 + g // 2))
        act.activation(self.parts[0][:, g, :, :], self.buffers[g % 2], ACT.Copy).then_inc(self.high_done, 1)

    def low(self, pool, turn):
        for g in range(3):
            pool.wait_ge(self.high_done, turn * 3 + g + 1)
            pool.tensor_tensor(self.parts[1][:, g, :, :], self.buffers[g % 2], self.parts[0][:, g, :, :],
                               ALU.subtract).then_inc(self.split, 1)

    def wait(self, eng, turn):
        eng.wait_ge(self.split, turn * 3 + 5)


def expert_weights(wqk, wv, e):
    qk = wqk.rearrange("(k p) (g e c) -> g p k e c", p=P, g=2, e=EXPERTS)
    v = wv.rearrange("e (k p) c -> p k e c", p=P)
    return [t.rearrange("p k e c -> p k (e c)") for t in (
        qk[0, :, :, bass.ds(e, 1), :], qk[1, :, :, bass.ds(e, 1), :], v[:, :, bass.ds(e, 1), :])]


def turn_tokens(nc, x, xt, ident, eps_half, xnT, wqk, wv, w_parts, buffers, w1, b1, w2, b2, logits):
    with ExitStack() as ctx:
        sb, ps, sem = scope(nc, ctx)
        stats = sb("stats_n", [P, NB, 24], FP32)
        gate_w1 = sb("gate_w1", [P, KT, P], FP32)
        gate_parts = [sb(f"gate_w1_{part}", [P, KT, P], FP32R) for part in ("high", "low")]
        gate_b1 = sb("gate_b1", [GATE, 1], FP32)
        gate_w2 = sb("gate_w2", [GATE, EXPERTS], FP32)
        gate_b2 = sb("gate_b2", [P, 1, EXPERTS], FP32)
        hidden = sb("gate_hidden", [GATE, NPAD], FP32)
        ps_t = [ps(f"ps_t_n{u}", [P, 2 * BANK]) for u in (0, 1)]
        ps_h = ps("ps_hidden", [P, 3 * BANK])
        ps_g = ps("ps_gate", [P, BANK])
        (stats_ready, mean_scaled, root_ready, pool_order, xn_ready, turned, high_moved, moved, order,
         cleared, gates_in, gate_high, gate_split, hidden_done, hidden_ready, logits_done) = (
            sem(n + "_n") for n in (
                "stats_ready", "mean_scaled", "root_ready", "pool_order", "xn_ready", "turned", "high_moved",
                "moved", "order", "cleared", "gates_in", "gate_high", "gate_split", "hidden_done",
                "hidden_ready", "logits_done"))
        x_in = [sem(f"x_in_n{b}") for b in range(NB)]
        thirds = ThirdsOfWeights(sem, "first", buffers, w_parts)
        block = ctx.enter_context(nc.Block())

        @block.sync
        def _(sp):
            for b in range(NB):
                sp.dma_start(xt[:, b, :], x[b, :, :]).then_inc(x_in[b], 16)
            thirds.start(sp)
            thirds.load(sp, 0, expert_weights(wqk, wv, 0))

        @block.gpsimd
        def _(pool):
            pool.memset(gate_w1[:, :, :], 0.0).then_inc(cleared, 1)
            pool.wait_ge(cleared, 1)
            pool.dma_start(gate_w1[:, :, 0:GATE], w1.rearrange("(k p) n -> p k n", p=P)).then_inc(gates_in, 16)
            pool.dma_start(gate_b1[:, :], b1.unsqueeze(1)).then_inc(gates_in, 16)
            pool.dma_start(gate_w2[:, :], w2).then_inc(gates_in, 16)
            pool.dma_start(gate_b2[:, 0, :], b2.partition_broadcast(P)).then_inc(gates_in, 16)
            for b in range(NB):
                chain = Chain(pool, pool_order, 2, b)
                pool.wait_ge(stats_ready, b + 1)
                chain(root(nc, pool, stats[:, b, :], eps_half, chain))
                chain.end()
                pool.tensor_tensor(stats[:, b, 4:5], stats[:, b, 0:1], stats[:, b, 3:4], ALU.mult).then_inc(mean_scaled, 1)
                pool.wait_ge(mean_scaled, b + 1)
                pool.tensor_tensor(stats[:, b, 5:6], stats[:, b, 4:5], eps_half[:, 2:3], ALU.mult).then_inc(root_ready, 1)
            thirds.low(pool, 0)

        @block.vector
        def _(dve):
            def statistics(b):
                dve.wait_ge(x_in[b], 16)
                for i in (0, 1):
                    last = dve.bn_stats(stats[:, b, 8 + 6 * i:14 + 6 * i], xt[:, b, i * C_IN // 2:(i + 1) * C_IN // 2])
                last.then_inc(order, 1)
                dve.wait_ge(order, b + 1)
                dve.bn_aggr(stats[:, b, 0:2], stats[:, b, 8:20]).then_inc(stats_ready, 1)

            def low_part(b):
                dve.wait_ge(high_moved, b + 1)
                dve.tensor_tensor(xnT[1][:, :, b * P:(b + 1) * P], ps_t[b % 2][:, 0:C_IN].rearrange("p (k c) -> p k c", k=KT),
                                  xnT[0][:, :, b * P:(b + 1) * P], ALU.subtract).then_inc(moved, 1)

            for b in range(3):
                statistics(b)
            for b in range(NB):
                low_part(b)
                if b == 1:
                    dve.wait_ge(gate_high, 1)
                    dve.tensor_tensor(gate_parts[1][:, :, :], gate_w1[:, :, :], gate_parts[0][:, :, :],
                                      ALU.subtract).then_inc(gate_split, 1)
                if b + 3 < NB:
                    statistics(b + 3)
            dve.wait_ge(logits_done, 1)
            dve.tensor_tensor(logits[:, :, :], ps_g[:, 0:NB * EXPERTS].rearrange("p (b e) -> p b e", b=NB),
                              gate_b2[:, :, :].broadcast_to([P, NB, EXPERTS]), ALU.add)

        @block.tensor
        def _(pe):
            pe.sem_inc(turned, 2)

            def transposes(b):
                pe.wait_ge(xn_ready, b + 1)
                pe.wait_ge(moved, b + 1)
                for k in range(KT):
                    last = pe.transpose(ps_t[b % 2][:, k * P:(k + 1) * P], xt[:, b, k * P:(k + 1) * P], ident[:, :])
                last.then_inc(turned, 1)

            def gate_hidden(first, end):
                pe.wait_ge(moved, end + 2)
                pairs = split_products(gate_parts, xnT)
                for k in range(KT):
                    for i, (left, right) in enumerate(pairs):
                        last = pe.matmul(ps_h[:, first * P:end * P], left[:, k, :], right[:, k, first * P:end * P],
                                         start=(k == 0 and i == 0), stop=(k == KT - 1 and i == len(pairs) - 1))
                last.then_inc(hidden_done, 1)

            transposes(0)
            for b in range(1, NB):
                transposes(b)
                if b == 6:
                    pe.wait_ge(gate_split, 1)
                    gate_hidden(0, 4)
            gate_hidden(4, 8)
            gate_hidden(8, NB)
            pe.wait_ge(hidden_ready, 1)
            for b in range(NB):
                last = pe.matmul(ps_g[:, b * EXPERTS:(b + 1) * EXPERTS], hidden[:, b * P:(b + 1) * P],
                                 gate_w2[:, :], start=True, stop=True)
            last.then_inc(logits_done, 1)

        @block.scalar
        def _(act):
            act.sem_inc(moved, 2)

            def shift(b):
                act.wait_ge(root_ready, b + 1)
                act.activation(xt[:, b, :], xt[:, b, :], ACT.Identity, scale=stats[:, b, 3:4],
                               bias=stats[:, b, 5:6]).then_inc(xn_ready, 1)

            def high_part(b):
                act.wait_ge(turned, b + 3)
                act.activation(xnT[0][:, :, b * P:(b + 1) * P], ps_t[b % 2][:, 0:C_IN].rearrange("p (k c) -> p k c", k=KT),
                               ACT.Copy).then_inc(high_moved, 1)

            shift(0)
            for b in range(NB):
                if b + 1 < NB:
                    shift(b + 1)
                high_part(b)
                if b == 1:
                    act.wait_ge(gates_in, 64)
                    act.activation(gate_parts[0][:, :, :], gate_w1[:, :, :], ACT.Copy).then_inc(gate_high, 1)
                if b in (3, 5, 8):
                    thirds.high(act, 0, (3, 5, 8).index(b))
            act.wait_ge(hidden_done, 3)
            act.activation(hidden[:, :], ps_h[0:GATE, 0:NPAD], ACT.Relu, bias=gate_b1[:, :]).then_inc(hidden_ready, 1)


def choose_experts(dve, gate, gate_exp, scratch, shifted, exp_ready, link, share):
    largest, total, keep, above = scratch

    def of(t):
        return t[:, :, :].broadcast_to([P, NB, EXPERTS])

    link(dve.tensor_reduce(largest[:, :, :], gate[:, :, :], axis=AX.X, op=ALU.max))
    dve.tensor_tensor(gate[:, :, :], gate[:, :, :], of(largest), ALU.subtract).then_inc(shifted, 1)
    dve.wait_ge(exp_ready, 1)
    link(dve.tensor_reduce(total[:, :, :], gate_exp[:, :, :], axis=AX.X, op=ALU.add))
    link(dve.reciprocal(total[:, :, :], total[:, :, :]))
    link(dve.tensor_tensor(gate[:, :, :], gate_exp[:, :, :], of(total), ALU.mult))
    g = [gate[:, :, e] for e in range(EXPERTS)]
    for i, (x, y, op) in enumerate(((g[1], g[0], ALU.is_gt), (g[2], g[0], ALU.is_gt),
                                    (g[0], g[1], ALU.is_ge), (g[2], g[1], ALU.is_gt),
                                    (g[0], g[2], ALU.is_ge), (g[1], g[2], ALU.is_ge))):
        link(dve.tensor_tensor(above[:, i, :], x, y, op))
    for e in range(EXPERTS):
        link(dve.tensor_tensor(keep[:, :, e], above[:, 2 * e, :], above[:, 2 * e + 1, :], ALU.mult))
    link(dve.tensor_scalar(keep[:, :, :], keep[:, :, :], -1.0, 1.0, ALU.mult, ALU.add))
    link(dve.tensor_reduce(largest[:, :, :], gate[:, :, :], axis=AX.X, op=ALU.max))
    dve.tensor_tensor(gate[:, :, :], gate[:, :, :], of(largest), ALU.subtract).then_inc(shifted, 1)
    dve.wait_ge(exp_ready, 2)
    link(dve.tensor_tensor(keep[:, :, :], keep[:, :, :], gate_exp[:, :, :], ALU.mult))
    link(dve.tensor_reduce(total[:, :, :], keep[:, :, :], axis=AX.X, op=ALU.add))
    link(dve.reciprocal(total[:, :, :], total[:, :, :]))
    link(dve.tensor_tensor(share[:, :, :].rearrange("p e b -> p b e"), keep[:, :, :], of(total), ALU.mult))


def run_experts(nc, xnT, wqk, bqk, wv, bv, conv_w, conv_b, w_out, w, buffers, gate, share, ident, y):
    CT = HD // P
    SCALE = HD ** -0.5
    NEXT_WEIGHTS = (5, 6, 7)
    MINE = CT + CT
    with ExitStack() as ctx:
        sb, ps, sem = scope(nc, ctx)
        qk_bias = sb("qk_bias", [P, 2, EXPERTS, CT], FP32)
        v_bias = sb("v_bias", [P, EXPERTS, HD], FP32)
        taps = sb("taps", [P, EXPERTS, CT, 3], FP32)
        tap_bias = sb("tap_bias", [P, EXPERTS, CT], FP32)
        raw = sb("raw_q", [P, CT, NODES + 2], FP32)
        qT, kT = sb("qT", [P, CT, NPAD], FP32), sb("kT", [P, CT, NPAD], FP32)
        v = sb("v", [P, NB, HD], FP32)
        future = sb("future", [P, P], FP32)
        prob = [sb(f"prob{u}", [P, NPAD], FP32) for u in (0, 1)]
        prob_T = [sb(f"prob_T{u}", [P, NB, P], FP32) for u in (0, 1)]
        cols = [sb(f"softmax{u}", [P, 4], FP32) for u in (0, 1)]
        gate_exp = sb("gate_exp", [P, NB, EXPERTS], FP32)
        scratch = (sb("gate_max", [P, NB, 1], FP32), sb("gate_sum", [P, NB, 1], FP32),
                   sb("gate_keep", [P, NB, EXPERTS], FP32), sb("gate_above", [P, 6, NB], FP32))
        ps_a, ps_b = ps("ps_scores", [P, 3 * BANK]), ps("ps_turned", [P, 3 * BANK])
        ps_y, ps_v = ps("ps_y", [P, BANK]), ps("ps_v", [P, BANK])
        gate_shifted, gate_exp_ready, gate_order = sem("gate_shifted"), sem("gate_exp_ready"), sem("gate_order")
        thirds = ThirdsOfWeights(sem, "next", buffers, w)
        (loaded, consts, projected, a_free, b_free, y_free, q_raw, q_tap, order, tap_order, q_ready, k_ready, v_ready,
         scored, masked, max_ready, prob_ready, turned, summed, taken, values_done, v_free, v_projected) = (
            sem(n + "_x") for n in (
                "loaded", "consts", "projected", "a_free", "b_free", "y_free", "q_raw", "q_tap",
                "order", "tap_order", "q_ready", "k_ready", "v_ready", "scored", "masked", "max_ready", "prob_ready",
                "turned", "summed", "taken", "values_done", "v_free", "v_projected"))
        block = ctx.enter_context(nc.Block())

        @block.sync
        def _(sp):
            sp.dma_start(qk_bias[:, :, :, :], bqk.rearrange("(g e c p) -> p g e c", g=2, e=EXPERTS, c=CT, p=P),
                         allow_slow_non_contiguous=True).then_inc(loaded, 16)
            sp.dma_start(v_bias[:, :, :].rearrange("p e c -> p (e c)"), bv.rearrange("e c -> (e c)").partition_broadcast(P)).then_inc(loaded, 16)
            sp.dma_start(taps[:, 0, :, :], conv_w.rearrange("(c p) o t -> p c (o t)", p=P)).then_inc(loaded, 16)
            sp.dma_start(tap_bias[:, 0, :], conv_b.rearrange("(c p) -> p c", p=P),
                         allow_slow_non_contiguous=True).then_inc(loaded, 16)
            thirds.start(sp)
            with sp.Fori(0, EXPERTS - 1) as e:
                thirds.load(sp, e, expert_weights(wqk, wv, e + 1))
            thirds.load(sp, EXPERTS - 1, [w_out.rearrange("(k p) (g c) -> g p k c", p=P, g=3)[g] for g in range(3)])

        @block.gpsimd
        def _(pool):
            pool.memset(taps[:, 1:EXPERTS, :, 0:1], 0.0)
            pool.memset(taps[:, 1:EXPERTS, :, 1:2], 1.0)
            pool.memset(taps[:, 1:EXPERTS, :, 2:3], 0.0)
            pool.memset(tap_bias[:, 1:EXPERTS, :], 0.0)
            pool.memset(raw[:, :, 0:1], 0.0)
            pool.memset(raw[:, :, NODES + 1:NODES + 2], 0.0)
            pool.memset(qT[:, :, NODES:NPAD], 0.0)
            pool.memset(future[:, :], 0.0).then_inc(consts, 1)
            pool.wait_ge(consts, 1)
            pool.affine_select(out=future[:, :], in_=future[:, :], compare_op=ALU.is_ge, fill=ABSENT, base=0,
                               pattern=[[-1, P]], channel_multiplier=1).then_inc(consts, 1)
            with pool.Fori(0, EXPERTS) as e:
                thirds.low(pool, e)

        @block.tensor
        def _(pe):
            pe.sem_inc(y_free, 1)
            pe.sem_inc(v_free, 1)
            with pe.Fori(0, EXPERTS) as e:
                pe.wait_ge(thirds.split, e * 3 + 2)
                for i in range(2 * CT):
                    g, c = divmod(i, CT)
                    to = (ps_a, ps_b)[i % 2]
                    if i % 2 == 0:
                        pe.wait_ge(a_free, e * (NB + CT) + i // 2 + 1)
                    else:
                        pe.wait_ge(b_free, e * (NB + CT) + i // 2 + 1)
                    for n in range(0, NPAD, BANK):
                        wide = min(BANK, NPAD - n)
                        for k in range(KT):
                            for j, (left, right) in enumerate(split_products(w, xnT)):
                                last = pe.matmul(to[:, n:n + wide], left[:, g, k, c * P:(c + 1) * P],
                                                 right[:, k, n:n + wide], start=(k == 0 and j == 0),
                                                 stop=(k == KT - 1 and j == 2))
                    last.then_inc(projected, 1)

                def value(b):
                    pe.wait_ge(v_free, e * NB + b + 1)
                    for k in range(KT):
                        for j, (left, right) in enumerate(split_products(xnT, w)):
                            last = pe.matmul(ps_v[:, 0:HD], left[:, k, b * P:(b + 1) * P], right[:, 2, k, :],
                                             start=(k == 0 and j == 0), stop=(k == KT - 1 and j == 2))
                    last.then_inc(v_projected, 1)
                    if b == NB - 1:
                        pe.wait_ge(v_projected, (e + 1) * NB)
                        pe.sem_inc(values_done, 1)

                def score(i):
                    pe.wait_ge(a_free, e * (NB + CT) + CT + i + 1)
                    for n in range(0, (i + 1) * P, BANK):
                        wide = min(BANK, (i + 1) * P - n)
                        for c in range(CT):
                            last = pe.matmul(ps_a[:, n:n + wide], qT[:, c, i * P:(i + 1) * P], kT[:, c, n:n + wide],
                                             start=(c == 0), stop=(c == CT - 1))
                    last.then_inc(scored, 1)

                def turn(i):
                    pe.wait_ge(prob_ready, e * NB + i + 1)
                    pe.wait_ge(b_free, e * (NB + CT) + CT + i + 1)
                    for s in range(i + 1):
                        last = pe.transpose(ps_b[:, s * P:(s + 1) * P], prob[i % 2][:, s * P:(s + 1) * P], ident[:, :])
                    last.then_inc(turned, 1)

                def average(i):
                    pe.wait_ge(b_free, e * (NB + CT) + CT + i + 2)
                    pe.wait_ge(v_ready, e * NB + i + 1)
                    pe.wait_ge(y_free, e * NB + i + 1)
                    for s in range(i + 1):
                        last = pe.matmul(ps_y[:, 0:HD], prob_T[i % 2][:, s, :], v[:, s, :],
                                         start=(s == 0), stop=(s == i))
                    last.then_inc(summed, 1)

                value(0)
                pe.wait_ge(q_ready, (e + 1) * CT)
                pe.wait_ge(b_free, e * (NB + CT) + CT + 1)
                score(0)
                value(1)
                for i in range(1, NB):
                    turn(i - 1)
                    score(i)
                    if 2 * i < NB:
                        value(2 * i)
                    average(i - 1)
                    if 2 * i < NB:
                        value(2 * i + 1)
                turn(NB - 1)
                average(NB - 1)

        @block.scalar
        def _(act):
            act.sem_inc(a_free, 1)
            act.sem_inc(b_free, 1)
            for i in (0, 1):
                act.wait_ge(gate_shifted, i + 1)
                act.activation(gate_exp[:, :, :], gate[:, :, :], ACT.Exp).then_inc(gate_exp_ready, 1)
            act.wait_ge(loaded, 64)
            act.wait_ge(consts, 2)
            with act.Fori(0, EXPERTS) as e:
                for i in range(2 * CT):
                    g, c = divmod(i, CT)
                    of, free = ((ps_a, a_free), (ps_b, b_free))[i % 2]
                    bias = qk_bias[:, g, bass.ds(e, 1), c:c + 1].rearrange("p e c -> p (e c)")
                    act.wait_ge(projected, e * MINE + i + 1)
                    if g == 0:
                        act.activation(raw[:, c, 1:NODES + 1], of[:, 0:NODES], ACT.Identity, bias=bias).then_inc(free, 1)
                        act.wait_ge(free, e * (NB + CT) + 2)
                        act.activation(qT[:, c, 0:NODES], raw[:, c, 0:NODES], ACT.Identity,
                                       scale=taps[:, bass.ds(e, 1), c, 0:1].rearrange("p e t -> p (e t)"),
                                       bias=tap_bias[:, bass.ds(e, 1), c:c + 1].rearrange("p e c -> p (e c)")
                                       ).then_inc(q_tap, 1)
                    else:
                        act.activation(kT[:, c, :], of[:, 0:NPAD], ACT.Identity, bias=bias).then_inc(free, 1)
                for i in range(NB):
                    wide = (i + 1) * P
                    act.wait_ge(max_ready, e * NB + i + 1)
                    act.activation(prob[i % 2][:, 0:wide], ps_a[:, 0:wide], ACT.Exp, scale=SCALE,
                                   bias=cols[i % 2][:, 1:2], accum_out=cols[i % 2][:, 2:3]).then_inc(prob_ready, 1)
                    act.wait_ge(prob_ready, e * NB + i + 1)
                    act.sem_inc(a_free, 1)
                    act.wait_ge(turned, e * NB + i + 1)
                    act.activation(prob_T[i % 2][:, 0:i + 1, :], ps_b[:, 0:wide].rearrange("p (s t) -> p s t", t=P),
                                   ACT.Copy).then_inc(b_free, 1)
                    if i in NEXT_WEIGHTS:
                        if i == NEXT_WEIGHTS[0]:
                            act.wait_ge(values_done, e + 1)
                        thirds.high(act, e, NEXT_WEIGHTS.index(i))

        @block.vector
        def _(dve):
            choose_experts(dve, gate, gate_exp, scratch, gate_shifted, gate_exp_ready, Chain(dve, gate_order), share)
            dve.wait_ge(loaded, 64)
            dve.wait_ge(consts, 2)
            with dve.Fori(0, EXPERTS) as e:
                for c in range(CT):
                    dve.wait_ge(q_tap, e * CT + c + 1)
                    for t in (1, 2):
                        last = dve.scalar_tensor_tensor(
                            out=qT[:, c, 0:NODES], in0=raw[:, c, t:t + NODES],
                            scalar=taps[:, bass.ds(e, 1), c, t:t + 1].rearrange("p e t -> p (e t)"),
                            in1=qT[:, c, 0:NODES], op0=ALU.mult, op1=ALU.add)
                        last.then_inc(tap_order, 1)
                        dve.wait_ge(tap_order, e * 2 * CT + 2 * c + t)
                    dve.sem_inc(q_ready, 1)

                def take_value(b):
                    dve.wait_ge(v_projected, e * NB + b + 1)
                    dve.tensor_tensor(v[:, b, :], ps_v[:, 0:HD],
                                      v_bias[:, bass.ds(e, 1), :].rearrange("p e c -> p (e c)"), ALU.add).then_inc(v_ready, 1)
                    dve.wait_ge(v_ready, e * NB + b + 1)
                    dve.sem_inc(v_free, 1)

                def softmax_max(i):
                    c = cols[i % 2]
                    dve.wait_ge(scored, e * NB + i + 1)
                    dve.tensor_tensor(ps_a[:, i * P:(i + 1) * P], ps_a[:, i * P:(i + 1) * P], future[:, :],
                                      ALU.add).then_inc(masked, 1)
                    dve.wait_ge(masked, e * NB + i + 1)
                    dve.tensor_reduce(c[:, 0:1], ps_a[:, 0:(i + 1) * P], axis=AX.X, op=ALU.max).then_inc(order, 1)
                    dve.wait_ge(order, e * 3 * NB + LINKS[i][0])
                    dve.tensor_scalar(c[:, 1:2], c[:, 0:1], -SCALE, None, ALU.mult).then_inc(max_ready, 1)

                def take(i):
                    c = cols[i % 2]
                    dve.wait_ge(summed, e * NB + i + 1)
                    dve.reciprocal(c[:, 3:4], c[:, 2:3]).then_inc(order, 1)
                    dve.wait_ge(order, e * 3 * NB + LINKS[i][1])
                    dve.tensor_tensor(c[:, 3:4], c[:, 3:4], share[:, bass.ds(e, 1), i:i + 1].rearrange("p e b -> p (e b)"),
                                      ALU.mult).then_inc(order, 1)
                    dve.wait_ge(order, e * 3 * NB + LINKS[i][1] + 1)
                    dve.tensor_scalar(y[:, i, bass.ds(e * HD, HD)], ps_y[:, 0:HD], c[:, 3:4], None,
                                      ALU.mult).then_inc(taken, 1)
                    dve.wait_ge(taken, e * NB + i + 1)
                    dve.sem_inc(y_free, 1)

                LINKS = [(1 if i == 0 else 3 * i - 1, 3 * i + 3 if i < NB - 1 else 3 * NB - 1) for i in range(NB)]
                take_value(0)
                softmax_max(0)
                take_value(1)
                for i in range(1, NB):
                    softmax_max(i)
                    if 2 * i < NB:
                        take_value(2 * i)
                    take(i - 1)
                    if 2 * i < NB:
                        take_value(2 * i + 1)
                take(NB - 1)


def project_out(nc, y, w, bias, x, ident, out):
    with ExitStack() as ctx:
        sb, ps, sem = scope(nc, ctx)
        bias_row = sb("out_bias", [P, C_IN], FP32)
        yt = [sb(f"yt{u}", [P, C_IN], FP32) for u in (0, 1)]
        yT = [[sb(f"yT{part}{u}", [P, KT, P], FP32R) for part in (0, 1)] for u in (0, 1)]
        xt = [sb(f"xt_o{u}", [P, C_IN], FP32) for u in (0, 1)]
        out_t = [sb(f"out_t{u}", [P, C_IN], FP32) for u in (0, 1)]
        ps_t, ps_o = ps("ps_t_o", [P, 2 * BANK]), [ps(f"ps_o_o{u}", [P, 2 * BANK]) for u in (0, 1)]
        loaded, y_ready, turned, high_moved, moved, product, taken, out_ready = (
            sem(n + "_o") for n in ("loaded", "y_ready", "turned", "high_moved", "moved", "product", "taken",
                                    "out_ready"))
        x_in, stored = ([sem(f"{n}_o{u}") for u in (0, 1)] for n in ("x_in", "stored"))
        block = ctx.enter_context(nc.Block())

        def rows_of(dram, b):
            return dram[bass.ds(b, 1), :, :].rearrange("b p c -> (b p) c")

        @block.sync
        def _(sp):
            sp.dma_start(bias_row[:, :], bias.partition_broadcast(P)).then_inc(loaded, 16)
            for u in (0, 1):
                sp.sem_inc(stored[u], 16)
            for b, u, _ in blocks_by_two(sp):
                sp.wait_ge(out_ready, b + 1)
                sp.dma_start(xt[u][:, :], rows_of(x, b)).then_inc(x_in[u], 16)

        @block.gpsimd
        def _(pool):
            for b, u, _ in blocks_by_two(pool):
                pool.wait_ge(turned, b + 1)
                pool.tensor_copy(yt[u][:, :], y[:, bass.ds(b, 1), :].rearrange("p b c -> p (b c)")).then_inc(y_ready, 1)

        @block.tensor
        def _(pe):
            pe.sem_inc(turned, 2)

            def transposes(b, u):
                pe.wait_ge(y_ready, b + 1)
                pe.wait_ge(moved, b + 1)
                for k in range(KT):
                    last = pe.transpose(ps_t[:, k * P:(k + 1) * P], yt[u][:, k * P:(k + 1) * P], ident[:, :])
                last.then_inc(turned, 1)

            def products(b, u):
                pe.wait_ge(moved, b + 2)
                pe.wait_ge(taken, b + 1)
                for g in range(3):
                    for k in range(KT):
                        for i, (left, right) in enumerate(split_products(yT[u], w)):
                            last = pe.matmul(ps_o[u][:, g * HD:(g + 1) * HD], left[:, k, :], right[:, g, k, :],
                                             start=(k == 0 and i == 0), stop=(k == KT - 1 and i == 2))
                last.then_inc(product, 1)

            one_ahead(pe, transposes, products)

        @block.scalar
        def _(act):
            act.sem_inc(moved, 1)
            act.sem_inc(product, 2)

            def move_yT(b, u):
                act.wait_ge(turned, b + 3)
                act.wait_ge(product, b + 1)
                act.activation(yT[u][0][:, :, :], ps_t[:, 0:C_IN].rearrange("p (k c) -> p k c", k=KT), ACT.Copy).then_inc(high_moved, 1)

            def store(b, u):
                act.wait_ge(out_ready, b + 3)
                act.dma_start(rows_of(out, b), out_t[u][:, :]).then_inc(stored[u], 16)

            one_ahead(act, move_yT, store)
            for u in (0, 1):
                act.wait_ge(stored[u], 16 * (NB // 2 + 1))

        @block.vector
        def _(dve):
            dve.sem_inc(taken, 2)
            dve.sem_inc(out_ready, 2)
            dve.wait_ge(loaded, 16)

            def low_part(b, u):
                dve.wait_ge(high_moved, b + 1)
                dve.tensor_tensor(yT[u][1][:, :, :], ps_t[:, 0:C_IN].rearrange("p (k c) -> p k c", k=KT),
                                  yT[u][0][:, :, :], ALU.subtract).then_inc(moved, 1)

            def close(b, u):
                dve.wait_ge(stored[u], x_loads(b, u))
                dve.wait_ge(product, b + 3)
                dve.tensor_tensor(out_t[u][:, :], ps_o[u][:, 0:C_IN], bias_row[:, :], ALU.add).then_inc(taken, 1)
                dve.wait_ge(taken, b + 3)
                dve.wait_ge(x_in[u], x_loads(b, u))
                dve.tensor_tensor(out_t[u][:, :], out_t[u][:, :], xt[u][:, :], ALU.add).then_inc(out_ready, 1)

            one_ahead(dve, low_part, close)


def gnn_then_experts(nc, x, src, dst, W1, a_src1, a_dst1, b1, g1, be1, Wr1, br1, W2, a_src2, a_dst2, b2, g2, be2,
                     Wr2, br2, Wqk, bqk, Wv, bv, conv_w, conv_b, Wg1, bg1, Wg2, bg2, Wp, bp, out):
    def blocks(dram):
        return dram.rearrange("(b p) c -> b p c", p=P)

    x, out = blocks(x), blocks(out)
    skip1, h1, skip2, x2 = (blocks(nc.dram_tensor(name, [NPAD, c], FP32).ap()) for name, c in (
        ("skip1", HC), ("h1", HC), ("skip2", C_IN), ("x2", C_IN)))
    with ExitStack() as ctx:
        sb, _, sem = scope(nc, ctx)
        ident, ones, eps_half = sb("ident", [P, P], FP32), sb("ones", [P, P], FP32), sb("eps_half", [P, 3], FP32)
        cleared = sem("cleared")
        with nc.Block() as block:
            @block.gpsimd
            def _(pool):
                pool.memset(ident[:, :], 0.0).then_inc(cleared, 1)
                pool.memset(ones[:, :], 1.0)
                pool.memset(eps_half[:, 0:1], LN_EPS)
                pool.memset(eps_half[:, 1:2], -0.5)
                pool.memset(eps_half[:, 2:3], -1.0)
                pool.wait_ge(cleared, 1)
                pool.affine_select(out=ident[:, :], in_=ident[:, :], compare_op=ALU.not_equal, fill=1.0, base=0,
                                   pattern=[[-1, P]], channel_multiplier=1)

        counts = nc.dram_tensor("counts", [NB, P, NPAD], U16).ap()
        with ExitStack() as graph:
            g_sb, _, _ = scope(nc, graph)
            shared = [g_sb(f"weight_{part}", [P, KT * HC], FP32R) for part in ("high", "low")]
            for (layer, kt, heads, width, feats, residual, w, a_src, a_dst, bias, gain, shift, w_skip, b_skip, skip,
                 result) in (
                    (1, KT, HEADS, HID, x, None, W1, a_src1, a_dst1, b1, g1, be1, Wr1, br1, skip1, h1),
                    (2, HKT, 1, C_IN, h1, x, W2, a_src2, a_dst2, b2, g2, be2, Wr2, br2, skip2, x2)):
                F = heads * width
                weights = [t[:, :].rearrange("p (k n) -> p k n", k=kt) for t in shared]
                with ExitStack() as one:
                    l_sb, _, _ = scope(nc, one)
                    xl = ([l_sb("xl1", [P, NB, F], FP32)] if layer == 1 else
                          [l_sb(f"xl2_{part}", [P, NB, F], FP32R) for part in ("high", "low")])
                    src_row = l_sb(f"src_row{layer}", [P, heads, NPAD], FP32)
                    dst_col = l_sb(f"dst_col{layer}", [P, NB, heads], FP32)
                    if layer == 1:
                        count_edges(nc, src, dst, counts, w, weights)
                    with ExitStack() as skip_weights:
                        s_sb, _, _ = scope(nc, skip_weights)
                        skips = [s_sb(f"skips{layer}_{part}", [P, kt, F], FP32R) for part in ("high", "low")]
                        project(nc, kt, heads, width, layer == 1, feats, residual, weights, skips, w_skip, b_skip,
                                a_src, a_dst, ident, ones, eps_half, xl, src_row, dst_col, skip)
                    following = (W2, [t[:, :].rearrange("p (k n) -> p k n", k=HKT) for t in shared]) if layer == 1 else ()
                    attend(nc, heads, width, layer == 1, counts, xl, src_row, dst_col, bias, gain, shift,
                           eps_half, ident, skip, result, *following)

        xnT = [sb(f"xnT_{part}", [P, KT, NPAD], FP32R) for part in ("high", "low")]
        w_parts = [sb(f"w_expert_{part}", [P, 3, KT, HD], FP32R) for part in ("high", "low")]
        gate = sb("gate", [P, NB, EXPERTS], FP32)
        share = sb("share", [P, EXPERTS, NB], FP32)
        y = sb("y", [P, NB, C_IN], FP32)
        with ExitStack() as experts:
            e_sb, _, _ = scope(nc, experts)
            buffers = [e_sb(f"w_raw{u}", [P, KT, HD], FP32)[:, :, :] for u in (0, 1)]
            turn_tokens(nc, x2, y, ident, eps_half, xnT, Wqk, Wv, w_parts, buffers, Wg1, bg1, Wg2, bg2, gate)
            run_experts(nc, xnT, Wqk, bqk, Wv, bv, conv_w, conv_b, Wp, w_parts, buffers, gate, share, ident, y)
        project_out(nc, y, w_parts, bp, x2, ident, out)


_INS = (["x", "src", "dst"] + ["L0_gnn_" + n for n in (
    "W1", "a_src1", "a_dst1", "b1", "g1", "be1", "Wr1", "br1", "W2", "a_src2", "a_dst2", "b2", "g2", "be2", "Wr2",
    "br2")] + ["L0_ffn_" + n for n in ("Wqk", "bqk", "Wv", "bv", "conv_w", "conv_b", "Wg1", "bg1", "Wg2", "bg2",
                                       "Wp", "bp")])


def kernel(**inputs):
    import numpy as np
    import concourse.bacc as bacc
    from concourse.bass_utils import run_bass_kernel_spmd

    nc = bacc.Bacc("TRN2", target_bir_lowering=False, num_devices=1)
    arrays, args = {}, []
    for name in _INS:
        a = np.ascontiguousarray(inputs[name])
        if name == "x":
            a = np.pad(a, ((0, NPAD - NODES), (0, 0)))
        elif name in ("src", "dst"):
            a = np.pad(a, (0, CHUNKS * P - EDGES), constant_values=NPAD)
            a = np.ascontiguousarray(a.reshape(CHUNKS, P).T)
        arrays[f"in_{name}"] = a
        args.append(nc.dram_tensor(f"in_{name}", a.shape, mybir.dt.from_np(a.dtype), kind="ExternalInput").ap())
    args.append(nc.dram_tensor("out_0", (NPAD, C_IN), FP32, kind="ExternalOutput").ap())
    gnn_then_experts(nc, *args)
    r = run_bass_kernel_spmd(nc, [arrays], core_ids=[0])
    return r.results[0]["out_0"][:NODES]
```
